# Optimizing a Trainium2 kernel written in Bass

```python
import numpy as np
import jax
import jax.numpy as jnp

def _softmax(x, axis=-1):
    return jax.nn.softmax(x, axis=axis)

def _gelu(x):
    return jax.nn.gelu(x, approximate=True)

def _silu(x):
    return jax.nn.silu(x)

def _sigmoid(x):
    return jax.nn.sigmoid(x)

def _layernorm(x, axis=-1, eps=1e-05):
    m = jnp.mean(x, axis=axis, keepdims=True)
    v = jnp.var(x, axis=axis, keepdims=True)
    return (x - m) / jnp.sqrt(v + eps)

def _scatter_add(tgt, idx, src, axis=0):
    return tgt.at[idx].add(src)

def _segment_sum(src, seg, n):
    return jax.ops.segment_sum(src, seg, n)
kernel_name = 'mk_hybrid_d1_jaxref_r8_1a0f43'

def setup_inputs(seed: int=0):
    np.random.seed(seed)
    _w = jnp.asarray

    def _L0_attn_a_setup():
        import jax, jax.numpy as jnp
        import numpy as np
        N_HEADS = 32
        WINDOW = 128

        def _sliding_window_attention(x, Wq, Wk, Wv, Wo, n_heads=N_HEADS, window=WINDOW):
            B, T, D = x.shape
            H, dk = (n_heads, D // n_heads)
            bs = window
            assert T % bs == 0
            nb = T // bs

            def heads(y):
                return y.reshape(B, T, H, dk).transpose(0, 2, 1, 3)
            q = heads(x @ Wq.T)
            k = heads(x @ Wk.T)
            v = heads(x @ Wv.T)
            qb = q.reshape(B, H, nb, bs, dk)
            zpad = jnp.zeros((B, H, bs, dk), dtype=x.dtype)
            kp = jnp.concatenate([zpad, k], axis=2).reshape(B, H, nb + 1, bs, dk)
            vp = jnp.concatenate([zpad, v], axis=2).reshape(B, H, nb + 1, bs, dk)
            kw = jnp.concatenate([kp[:, :, :-1], kp[:, :, 1:]], axis=3)
            vw = jnp.concatenate([vp[:, :, :-1], vp[:, :, 1:]], axis=3)
            scale = 1.0 / np.sqrt(dk).astype(np.float32)
            scores = jnp.einsum('bhnrd,bhncd->bhnrc', qb, kw) * scale
            i = jnp.arange(nb)[:, None, None]
            r = jnp.arange(bs)[None, :, None]
            c = jnp.arange(2 * bs)[None, None, :]
            dist = bs + r - c
            key_global = i * bs - bs + c
            valid = (dist >= 0) & (dist <= window) & (key_global >= 0)
            scores = jnp.where(valid[None, None], scores, jnp.finfo(scores.dtype).min)
            probs = jax.nn.softmax(scores, axis=-1)
            out = jnp.einsum('bhnrc,bhncd->bhnrd', probs, vw)
            out = out.reshape(B, H, T, dk).transpose(0, 2, 1, 3).reshape(B, T, D)
            return out @ Wo.T
        key = jax.random.key(seed)
        ks = jax.random.split(key, 5)
        B, T, D = (2, 512, 256)
        w_std = 0.02
        return {'x': jax.random.normal(ks[0], (B, T, D), dtype=jnp.float32), 'Wq': jax.random.normal(ks[1], (D, D), dtype=jnp.float32) * w_std, 'Wk': jax.random.normal(ks[2], (D, D), dtype=jnp.float32) * w_std, 'Wv': jax.random.normal(ks[3], (D, D), dtype=jnp.float32) * w_std, 'Wo': jax.random.normal(ks[4], (D, D), dtype=jnp.float32) * w_std}
    _L0_attn_a_in = _L0_attn_a_setup()

    def _L0_attn_b_setup():
        import jax, jax.numpy as jnp
        import numpy as np
        HIDDEN = 256
        N_HEADS = 32
        HEAD_DIM = HIDDEN // N_HEADS
        CONV_K = 4
        INTER = 704
        EPS = 1e-06

        def _rms(x, w):
            return x * jax.lax.rsqrt(jnp.mean(x * x, axis=-1, keepdims=True) + EPS) * w

        def _l2norm(x):
            n = jnp.sqrt(jnp.sum(x * x, axis=-1, keepdims=True))
            return x / jnp.maximum(n, 1e-12)

        def _causal_dwconv(x, w):
            C, K = w.shape
            xt = jnp.transpose(x, (0, 2, 1))
            out = jax.lax.conv_general_dilated(xt, w[:, None, :], window_strides=(1,), padding=[(K - 1, 0)], feature_group_count=C, dimension_numbers=('NCH', 'OIH', 'NCH'))
            return jnp.transpose(out, (0, 2, 1))

        def _delta_scan(k, q, v, beta):
            B, T, nh, hd = k.shape
            km, qm, vm = (jnp.moveaxis(a, 1, 0) for a in (k, q, v))
            bm = jnp.moveaxis(beta, 1, 0)

            def step(S, inp):
                kt, qt, vt, bt = inp
                err = jnp.einsum('bhvk,bhk->bhv', S, kt) - vt
                S = S - bt[..., None, None] * err[..., None] * kt[..., None, :]
                o = jnp.einsum('bhvk,bhk->bhv', S, qt)
                return (S, o)
            S0 = jnp.zeros((B, nh, hd, hd), k.dtype)
            S, o = jax.lax.scan(step, S0, (km, qm, vm, bm))
            return (jnp.moveaxis(o, 0, 1), S)

        def _reference_tuple_inner(hidden_states, attn_norm_w, Wq, Wk, Wv, conv_q, conv_k, conv_v, Wbeta, out_norm_w, Wout, mlp_norm_w, Wgate, Wup, Wdown):
            x = hidden_states
            B, T, H = x.shape
            nh, hd = (N_HEADS, HEAD_DIM)
            silu = jax.nn.silu
            h = _rms(x, attn_norm_w)
            q = silu(silu(_causal_dwconv(h @ Wq.T, conv_q)))
            k = silu(silu(_causal_dwconv(h @ Wk.T, conv_k)))
            v = silu(silu(_causal_dwconv(h @ Wv.T, conv_v)))
            q = _l2norm(q.reshape(B, T, nh, hd))
            k = _l2norm(k.reshape(B, T, nh, hd))
            v = v.reshape(B, T, nh, hd)
            beta = jax.nn.sigmoid(h @ Wbeta.T)
            o, memory_state = _delta_scan(k, q, v, beta)
            o = o.reshape(B, T, H)
            o = _rms(o, out_norm_w) @ Wout.T
            x = x + o
            h2 = _rms(x, mlp_norm_w)
            gate = h2 @ Wgate.T
            up = h2 @ Wup.T
            x = x + silu(gate) * up @ Wdown.T
            return (x, memory_state)
        key = jax.random.key(seed)
        ks = jax.random.split(key, 12)
        s = 0.02
        d = {'hidden_states': jax.random.normal(ks[0], (1, 128, HIDDEN), jnp.float32), 'attn_norm_w': jnp.ones((HIDDEN,), jnp.float32), 'Wq': jax.random.normal(ks[1], (HIDDEN, HIDDEN), jnp.float32) * s, 'Wk': jax.random.normal(ks[2], (HIDDEN, HIDDEN), jnp.float32) * s, 'Wv': jax.random.normal(ks[3], (HIDDEN, HIDDEN), jnp.float32) * s, 'conv_q': jax.random.normal(ks[4], (HIDDEN, CONV_K), jnp.float32) * 0.1, 'conv_k': jax.random.normal(ks[5], (HIDDEN, CONV_K), jnp.float32) * 0.1, 'conv_v': jax.random.normal(ks[6], (HIDDEN, CONV_K), jnp.float32) * 0.1, 'Wbeta': jax.random.normal(ks[7], (N_HEADS, HIDDEN), jnp.float32) * s, 'out_norm_w': jnp.ones((HIDDEN,), jnp.float32), 'Wout': jax.random.normal(ks[8], (HIDDEN, HIDDEN), jnp.float32) * s, 'mlp_norm_w': jnp.ones((HIDDEN,), jnp.float32), 'Wgate': jax.random.normal(ks[9], (INTER, HIDDEN), jnp.float32) * s, 'Wup': jax.random.normal(ks[10], (INTER, HIDDEN), jnp.float32) * s, 'Wdown': jax.random.normal(ks[11], (HIDDEN, INTER), jnp.float32) * s}
        return d
    _L0_attn_b_in = _L0_attn_b_setup()

    def _L0_ffn_setup():
        import jax, jax.numpy as jnp
        import numpy as np
        BLOCK = 64

        def dequant4bit(q, scale):
            return (q.astype(jnp.float32) - 7.5) * jnp.repeat(scale, BLOCK, axis=1)
        key = jax.random.key(seed)
        ks = jax.random.split(key, 11)
        B, S, D, H, R = (4, 256, 256, 1024, 16)
        return {'x1': jax.random.normal(ks[0], (B, S, D), jnp.float32), 'w_up_q': jax.random.randint(ks[1], (H, D), 0, 16, dtype=jnp.int32), 'w_up_scale': jax.random.uniform(ks[2], (H, D // BLOCK), jnp.float32) * 0.02, 'b_up': jax.random.normal(ks[3], (H,), jnp.float32) * 0.01, 'w_up_lora_a': jax.random.normal(ks[4], (D, R), jnp.float32) * 0.02, 'w_up_lora_b': jax.random.normal(ks[5], (R, H), jnp.float32) * 0.02, 'w_down_q': jax.random.randint(ks[6], (D, H), 0, 16, dtype=jnp.int32), 'w_down_scale': jax.random.uniform(ks[7], (D, H // BLOCK), jnp.float32) * 0.02, 'b_down': jax.random.normal(ks[8], (D,), jnp.float32) * 0.01, 'w_down_lora_a': jax.random.normal(ks[9], (H, R), jnp.float32) * 0.02, 'w_down_lora_b': jax.random.normal(ks[10], (R, D), jnp.float32) * 0.02}
    _L0_ffn_in = _L0_ffn_setup()
    _d = {'L0_attn_a_x': _L0_attn_a_in['x'], 'L0_attn_a_Wq': _L0_attn_a_in['Wq'], 'L0_attn_a_Wk': _L0_attn_a_in['Wk'], 'L0_attn_a_Wv': _L0_attn_a_in['Wv'], 'L0_attn_a_Wo': _L0_attn_a_in['Wo'], 'L0_attn_b_attn_norm_w': _L0_attn_b_in['attn_norm_w'], 'L0_attn_b_Wq': _L0_attn_b_in['Wq'], 'L0_attn_b_Wk': _L0_attn_b_in['Wk'], 'L0_attn_b_Wv': _L0_attn_b_in['Wv'], 'L0_attn_b_conv_q': _L0_attn_b_in['conv_q'], 'L0_attn_b_conv_k': _L0_attn_b_in['conv_k'], 'L0_attn_b_conv_v': _L0_attn_b_in['conv_v'], 'L0_attn_b_Wbeta': _L0_attn_b_in['Wbeta'], 'L0_attn_b_out_norm_w': _L0_attn_b_in['out_norm_w'], 'L0_attn_b_Wout': _L0_attn_b_in['Wout'], 'L0_attn_b_mlp_norm_w': _L0_attn_b_in['mlp_norm_w'], 'L0_attn_b_Wgate': _L0_attn_b_in['Wgate'], 'L0_attn_b_Wup': _L0_attn_b_in['Wup'], 'L0_attn_b_Wdown': _L0_attn_b_in['Wdown'], 'L0_ffn_w_up_q': _L0_ffn_in['w_up_q'], 'L0_ffn_w_up_scale': _L0_ffn_in['w_up_scale'], 'L0_ffn_b_up': _L0_ffn_in['b_up'], 'L0_ffn_w_up_lora_a': _L0_ffn_in['w_up_lora_a'], 'L0_ffn_w_up_lora_b': _L0_ffn_in['w_up_lora_b'], 'L0_ffn_w_down_q': _L0_ffn_in['w_down_q'], 'L0_ffn_w_down_scale': _L0_ffn_in['w_down_scale'], 'L0_ffn_b_down': _L0_ffn_in['b_down'], 'L0_ffn_w_down_lora_a': _L0_ffn_in['w_down_lora_a'], 'L0_ffn_w_down_lora_b': _L0_ffn_in['w_down_lora_b']}
    _x0 = _d['L0_attn_a_x']
    _d['L0_attn_a_x'] = jax.random.normal(jax.random.fold_in(jax.random.key(seed), 1), (2, 1024, 256), dtype=_x0.dtype)
    del _x0
    return _d

def reference(L0_attn_a_x, L0_attn_a_Wq, L0_attn_a_Wk, L0_attn_a_Wv, L0_attn_a_Wo, L0_attn_b_attn_norm_w, L0_attn_b_Wq, L0_attn_b_Wk, L0_attn_b_Wv, L0_attn_b_conv_q, L0_attn_b_conv_k, L0_attn_b_conv_v, L0_attn_b_Wbeta, L0_attn_b_out_norm_w, L0_attn_b_Wout, L0_attn_b_mlp_norm_w, L0_attn_b_Wgate, L0_attn_b_Wup, L0_attn_b_Wdown, L0_ffn_w_up_q, L0_ffn_w_up_scale, L0_ffn_b_up, L0_ffn_w_up_lora_a, L0_ffn_w_up_lora_b, L0_ffn_w_down_q, L0_ffn_w_down_scale, L0_ffn_b_down, L0_ffn_w_down_lora_a, L0_ffn_w_down_lora_b):

    def _L0_attn_a_ref(x, Wq, Wk, Wv, Wo):
        import jax, jax.numpy as jnp
        import numpy as np
        N_HEADS = 32
        WINDOW = 128

        def _sliding_window_attention(x, Wq, Wk, Wv, Wo, n_heads=N_HEADS, window=WINDOW):
            B, T, D = x.shape
            H, dk = (n_heads, D // n_heads)
            bs = window
            assert T % bs == 0
            nb = T // bs

            def heads(y):
                return y.reshape(B, T, H, dk).transpose(0, 2, 1, 3)
            q = heads(x @ Wq.T)
            k = heads(x @ Wk.T)
            v = heads(x @ Wv.T)
            qb = q.reshape(B, H, nb, bs, dk)
            zpad = jnp.zeros((B, H, bs, dk), dtype=x.dtype)
            kp = jnp.concatenate([zpad, k], axis=2).reshape(B, H, nb + 1, bs, dk)
            vp = jnp.concatenate([zpad, v], axis=2).reshape(B, H, nb + 1, bs, dk)
            kw = jnp.concatenate([kp[:, :, :-1], kp[:, :, 1:]], axis=3)
            vw = jnp.concatenate([vp[:, :, :-1], vp[:, :, 1:]], axis=3)
            scale = 1.0 / np.sqrt(dk).astype(np.float32)
            scores = jnp.einsum('bhnrd,bhncd->bhnrc', qb, kw) * scale
            i = jnp.arange(nb)[:, None, None]
            r = jnp.arange(bs)[None, :, None]
            c = jnp.arange(2 * bs)[None, None, :]
            dist = bs + r - c
            key_global = i * bs - bs + c
            valid = (dist >= 0) & (dist <= window) & (key_global >= 0)
            scores = jnp.where(valid[None, None], scores, jnp.finfo(scores.dtype).min)
            probs = jax.nn.softmax(scores, axis=-1)
            out = jnp.einsum('bhnrc,bhncd->bhnrd', probs, vw)
            out = out.reshape(B, H, T, dk).transpose(0, 2, 1, 3).reshape(B, T, D)
            return out @ Wo.T
        return _sliding_window_attention(x, Wq, Wk, Wv, Wo)

    def _L0_attn_b_ref(hidden_states, attn_norm_w, Wq, Wk, Wv, conv_q, conv_k, conv_v, Wbeta, out_norm_w, Wout, mlp_norm_w, Wgate, Wup, Wdown):
        import jax, jax.numpy as jnp
        import numpy as np
        HIDDEN = 256
        N_HEADS = 32
        HEAD_DIM = HIDDEN // N_HEADS
        CONV_K = 4
        INTER = 704
        EPS = 1e-06

        def _rms(x, w):
            return x * jax.lax.rsqrt(jnp.mean(x * x, axis=-1, keepdims=True) + EPS) * w

        def _l2norm(x):
            n = jnp.sqrt(jnp.sum(x * x, axis=-1, keepdims=True))
            return x / jnp.maximum(n, 1e-12)

        def _causal_dwconv(x, w):
            C, K = w.shape
            xt = jnp.transpose(x, (0, 2, 1))
            out = jax.lax.conv_general_dilated(xt, w[:, None, :], window_strides=(1,), padding=[(K - 1, 0)], feature_group_count=C, dimension_numbers=('NCH', 'OIH', 'NCH'))
            return jnp.transpose(out, (0, 2, 1))

        def _delta_scan(k, q, v, beta):
            B, T, nh, hd = k.shape
            km, qm, vm = (jnp.moveaxis(a, 1, 0) for a in (k, q, v))
            bm = jnp.moveaxis(beta, 1, 0)

            def step(S, inp):
                kt, qt, vt, bt = inp
                err = jnp.einsum('bhvk,bhk->bhv', S, kt) - vt
                S = S - bt[..., None, None] * err[..., None] * kt[..., None, :]
                o = jnp.einsum('bhvk,bhk->bhv', S, qt)
                return (S, o)
            S0 = jnp.zeros((B, nh, hd, hd), k.dtype)
            S, o = jax.lax.scan(step, S0, (km, qm, vm, bm))
            return (jnp.moveaxis(o, 0, 1), S)

        def _reference_tuple_inner(hidden_states, attn_norm_w, Wq, Wk, Wv, conv_q, conv_k, conv_v, Wbeta, out_norm_w, Wout, mlp_norm_w, Wgate, Wup, Wdown):
            x = hidden_states
            B, T, H = x.shape
            nh, hd = (N_HEADS, HEAD_DIM)
            silu = jax.nn.silu
            h = _rms(x, attn_norm_w)
            q = silu(silu(_causal_dwconv(h @ Wq.T, conv_q)))
            k = silu(silu(_causal_dwconv(h @ Wk.T, conv_k)))
            v = silu(silu(_causal_dwconv(h @ Wv.T, conv_v)))
            q = _l2norm(q.reshape(B, T, nh, hd))
            k = _l2norm(k.reshape(B, T, nh, hd))
            v = v.reshape(B, T, nh, hd)
            beta = jax.nn.sigmoid(h @ Wbeta.T)
            o, memory_state = _delta_scan(k, q, v, beta)
            o = o.reshape(B, T, H)
            o = _rms(o, out_norm_w) @ Wout.T
            x = x + o
            h2 = _rms(x, mlp_norm_w)
            gate = h2 @ Wgate.T
            up = h2 @ Wup.T
            x = x + silu(gate) * up @ Wdown.T
            return (x, memory_state)
        return _reference_tuple_inner(hidden_states, attn_norm_w, Wq, Wk, Wv, conv_q, conv_k, conv_v, Wbeta, out_norm_w, Wout, mlp_norm_w, Wgate, Wup, Wdown)[0]

    def _L0_ffn_ref(x1, w_up_q, w_up_scale, b_up, w_up_lora_a, w_up_lora_b, w_down_q, w_down_scale, b_down, w_down_lora_a, w_down_lora_b):
        import jax, jax.numpy as jnp
        import numpy as np
        BLOCK = 64

        def dequant4bit(q, scale):
            return (q.astype(jnp.float32) - 7.5) * jnp.repeat(scale, BLOCK, axis=1)
        w_up = dequant4bit(w_up_q, w_up_scale).T
        y1 = x1 @ w_up + b_up + x1 @ w_up_lora_a @ w_up_lora_b
        x2 = jax.nn.relu(y1)
        w_down = dequant4bit(w_down_q, w_down_scale).T
        y2 = x2 @ w_down + b_down + x2 @ w_down_lora_a @ w_down_lora_b
        return y2
    x = L0_attn_a_x
    x = x + _L0_attn_a_ref(_layernorm(x, axis=-1), L0_attn_a_Wq, L0_attn_a_Wk, L0_attn_a_Wv, L0_attn_a_Wo)
    x = x + _L0_ffn_ref(_layernorm(x, axis=-1), L0_ffn_w_up_q, L0_ffn_w_up_scale, L0_ffn_b_up, L0_ffn_w_up_lora_a, L0_ffn_w_up_lora_b, L0_ffn_w_down_q, L0_ffn_w_down_scale, L0_ffn_b_down, L0_ffn_w_down_lora_a, L0_ffn_w_down_lora_b)
    x = x + _L0_attn_b_ref(_layernorm(x, axis=-1), L0_attn_b_attn_norm_w, L0_attn_b_Wq, L0_attn_b_Wk, L0_attn_b_Wv, L0_attn_b_conv_q, L0_attn_b_conv_k, L0_attn_b_conv_v, L0_attn_b_Wbeta, L0_attn_b_out_norm_w, L0_attn_b_Wout, L0_attn_b_mlp_norm_w, L0_attn_b_Wgate, L0_attn_b_Wup, L0_attn_b_Wdown)
    x = x + _L0_ffn_ref(_layernorm(x, axis=-1), L0_ffn_w_up_q, L0_ffn_w_up_scale, L0_ffn_b_up, L0_ffn_w_up_lora_a, L0_ffn_w_up_lora_b, L0_ffn_w_down_q, L0_ffn_w_down_scale, L0_ffn_b_down, L0_ffn_w_down_lora_a, L0_ffn_w_down_lora_b)
    return x

_drawn_inputs = setup_inputs


def setup_inputs(seed=0):
    import zlib

    import numpy as np

    out = dict(_drawn_inputs(seed))
    spreads = {'L0_attn_b_attn_norm_w': (1.0, 0.2),
     'L0_attn_b_out_norm_w': (1.0, 0.6),
     'L0_attn_b_mlp_norm_w': (1.0, 0.6)}
    factors = {'L0_attn_a_Wq': 8.0,
     'L0_attn_a_Wk': 8.0,
     'L0_attn_a_Wv': 5.11,
     'L0_attn_a_Wo': 5.233,
     'L0_attn_b_Wbeta': 3.029,
     'L0_attn_b_Wgate': 5.518,
     'L0_attn_b_Wup': 5.488,
     'L0_attn_b_Wdown': 5.462,
     'L0_ffn_b_up': 6.171,
     'L0_ffn_b_down': 6.515,
     'L0_ffn_w_up_lora_a': 2.768,
     'L0_ffn_w_up_lora_b': 2.763,
     'L0_ffn_w_down_lora_b': 2.669}
    for name, (base, spread) in spreads.items():
        noise = np.random.default_rng([zlib.crc32(name.encode()), seed]).standard_normal(out[name].shape)
        drawn = base * np.exp(spread * noise) if base else spread * noise
        out[name] = jnp.asarray(drawn.astype(out[name].dtype))
    for name, factor in factors.items():
        out[name] = (out[name] * factor).astype(out[name].dtype)
    return out
```

```python
import concourse.bass as bass
from concourse import mybir
from contextlib import ExitStack

F32 = mybir.dt.float32
BF16 = mybir.dt.bfloat16
I32 = mybir.dt.int32
ACT = mybir.ActivationFunctionType
ALU = mybir.AluOpType
AX = mybir.AxisListType

B, T, D = 2, 1024, 256
H, DK = 32, 8
W = 128
NB = T // W
BT = B * W
KT = D // 128
HH = D // 128
HPH = H // HH
FF = 1024
FT = FF // 128
RANK = 16
QBLK = 64
INTER = 704
IT = (INTER + 127) // 128
TAPS = 4
C = 4
NC_ = W // C
VH = 2
VR = DK // VH
PAIRS_K = [(i, j) for i in range(1, C) for j in range(i)]
PAIRS_Q = [(i, j) for i in range(C) for j in range(i + 1)]
NPK, NPQ = len(PAIRS_K), len(PAIRS_Q)
PIECE_PAIRS = [(0, 0), (0, 1), (1, 0), (1, 1), (0, 2), (2, 0)]
SROWS = DK * len(PIECE_PAIRS)
MROW = SROWS
PADROW = SROWS + 3
BIG = 1e30
LN_EPS, RMS_EPS, L2_MIN2 = 1e-5, 1e-6, 1e-24
SUB = 32
SPAN = W + SUB
VE = 16
UPG = HPH // 2
NG = B * HH


def layer_program(nc, a):
    with ExitStack() as ctx:
        def sb(name, shape, dt=F32):
            return ctx.enter_context(nc.sbuf_tensor(name, shape, dt))

        def sem(name):
            return ctx.enter_context(nc.semaphore(name))

        q_pieces = nc.dram_tensor("q_pieces", (3, HH, 128, B, W), BF16, kind="Internal").ap()
        k_pieces = nc.dram_tensor("k_pieces", (3, HH, 128, B, W + T), BF16, kind="Internal").ap()
        lane_q = nc.dram_tensor("lane_q", (B, HH, 128, W), F32, kind="Internal").ap()
        lane_k = nc.dram_tensor("lane_k", (B, HH, 128, W), F32, kind="Internal").ap()
        lane_v = nc.dram_tensor("lane_v", (B, HH, 128, W), F32, kind="Internal").ap()
        lane_o = nc.dram_tensor("lane_o", (B, HH, 128, W), F32, kind="Internal").ap()

        ident = sb("ident", [128, 128])
        ones = sb("ones", [128, 128])
        head_sum = sb("head_sum", [128, 128])
        to_lanes = sb("to_lanes", [128, B * HH, 128])
        edge_mask_f = sb("edge_mask_f", [128, 2 * SUB])
        tri_mask_f = sb("tri_mask_f", [128, 2 * W])
        identb = sb("identb", [128, 128], BF16)
        edge_mask = sb("edge_mask", [128, 2 * SUB], BF16)
        tri_mask = sb("tri_mask", [128, 2 * W], BF16)
        stack_cols = sb("stack_cols", [128, 2])
        eps = sb("eps", [128, 4])
        wqkv_a = sb("wqkv_a", [128, KT, 3 * D])
        wo_a = sb("wo_a", [128, KT, D])
        wqkv_b = sb("wqkv_b", [128, KT, 3 * D])
        wbeta = sb("wbeta", [128, KT, B, 128])
        wout_b = sb("wout_b", [128, KT, D])
        wgu = sb("wgu", [128, KT, 2 * INTER])
        wdown_b = sb("wdown_b", [128, IT, D])
        norm_w = sb("norm_w", [128, 3, KT])
        conv_w = sb("conv_w", [128, 3, HH, TAPS])
        w_up = sb("w_up", [128, KT, FF])
        w_dn = sb("w_dn", [128, FT, D])
        b_up = sb("b_up", [128, FT])
        b_dn = sb("b_dn", [128, D])

        x_in = sb("x_in", [128, B, D])
        tok = sb("tok", [128, B, D])
        feat = sb("feat", [128, KT, B, W])
        tok_c = sb("tok_c", [128, B, D])
        feat_c = sb("feat_c", [128, KT, B, W])
        stats = sb("stats", [128, B, 6])
        mv = sb("mv", [128, B, 2])
        lnv = sb("lnv", [128, B])
        rstd = sb("rstd", [128, B])
        sq = sb("sq", [128, D])
        lnt = sb("lnt", [128, B])
        lnt_c = sb("lnt_c", [128, B])
        stats_c = sb("stats_c", [128, B, 6])
        mv_c = sb("mv_c", [128, B, 2])
        lnv_c = sb("lnv_c", [128, B])
        rstd_c = sb("rstd_c", [128, B])
        sq_c = sq
        x1 = sb("x1", [128, B, D])
        x2 = sb("x2", [128, B, D])
        z = sb("z", [128, B, D])
        y = sb("y", [128, B, D])
        xy = sb("xy", [128, B, D])
        x3 = z
        x1b = xy
        x3b = x1
        x_out = x2
        hid = sb("hid", [128, FT, BT])
        hid_c = hid
        sqk = sb("sqk", [128, 2, HH * BT])
        conv = sb("conv", [128, 3, HH * BT])
        pieces = conv[:].bitcast(BF16).rearrange("p s (a t) -> p (s a) t", a=2).rearrange("p (s j) t -> p s j t", s=2)
        rest = sqk
        q_stack = sb("q_stack", [128, 2, HPH, W], BF16)
        k_stack = sb("k_stack", [128, 2, HPH, 2 * W], BF16)
        v_ext = sb("v_ext", [128, B, 2, H, VE])
        mx = sb("mx", [128, NG, HPH])
        nmx = sb("nmx", [128, NG, HPH])
        mpieces = sb("mpieces", [128, NG, 3, HPH], BF16)
        m_rows = sb("m_rows", [2 * 3 * HPH, NG // 2, W], BF16)
        probs = sb("probs", [128, 2, 2 * 2 * W])
        o_rows = sb("o_rows", [128, 512])
        rden = sb("rden", [128, HPH])
        raw = sb("raw", [128, 3, HH, B, TAPS - 1 + W])
        prodk = hid[:].rearrange("p a b -> p (a b)").rearrange("p (h b q c) -> p h b q c", h=HH, b=B, q=NPK + NPQ)
        beta_l = sb("beta_l", [128, W])
        k_l = sb("k_l", [128, DK, W])
        q_l = sb("q_l", [128, DK, W])
        v_l = sb("v_l", [128, VR, W])
        pair_l = sb("pair_l", [128, NPK + NPQ, NC_])
        tm = sb("tm", [128, NC_, C, C])
        mm_ = sb("mm_", [128, C, C, NC_])
        tmp_t = sb("tmp_t", [128, NC_, C])
        k_til = sb("k_til", [128, NC_, C, DK])
        tmp_k = prodk.rearrange("p h b q c -> p (h b q c)")[:, 0:NC_ * C * DK].rearrange("p (c i k) -> p c i k", i=C, k=DK)
        lane_buf = sb("lane_buf", [128, NC_ * VR * C * (DK + 1)])
        first = lane_buf[:].rearrange("p (c v i k) -> p c v i k", v=VR, i=C, k=DK + 1)
        tmp_v = sb("tmp_v", [128, NC_, VR, C])
        u_l = sb("u_l", [128, NC_, VR, C])
        state = sb("state", [128, NC_ + 1, VR, DK, C + 1])
        out_terms = lane_buf[:, 0:2 * W * (DK + C)].rearrange("p (v c i e) -> p v c i e", v=2, i=C, e=DK + C)
        o_l = k_l[:].rearrange("p k t -> p (k t)")[:, 0:VR * W].rearrange("p (v c i) -> p v c i", v=VR, i=C)
        o_t = tok_c[:].rearrange("p h (b t) -> p h b t", b=B)
        o_n = feat_c
        rs_o = sq
        gate = sqk[:, 0].rearrange("p (i t) -> p i t", i=2)
        act_c = hid[:, 0:IT]

        bank = [ctx.enter_context(nc.psum_tensor(f"bank{i}", [128, 512], F32)) for i in range(8)]
        bank_b = bank[0][:, :].bitcast(BF16)

        consts_in = sem("consts_in")
        weights_in = sem("weights_in")
        quant_in = sem("quant_in")
        lora_in = sem("lora_in")
        lora_prod = sem("lora_prod")
        lora_added = sem("lora_added")
        consts_cast = sem("consts_cast")
        weights_scaled = sem("weights_scaled")
        zeroed = sem("zeroed")
        pad_out = sem("pad_out")
        x_loaded = sem("x_loaded")
        x_used = sem("x_used")
        vstep = sem("vstep")
        astep = sem("astep")
        gstep = sem("gstep")
        vars_ready = sem("vars_ready")
        rstd_ready = sem("rstd_ready")
        tok_ready = sem("tok_ready")
        turned = sem("turned")
        feat_ready = sem("feat_ready")
        qkv_done = sem("qkv_done")
        piece1 = sem("piece1")
        rest1 = sem("rest1")
        piece2 = sem("piece2")
        piece3 = sem("piece3")
        v_done = sem("v_done")
        pieces_out = sem("pieces_out")
        stacks_in = [sem("stacks_in0"), sem("stacks_in1")]
        stack_init = sem("stack_init")
        sq_rstd = sem("sq_rstd")
        scores1 = sem("scores1")
        max_done = sem("max_done")
        mpieces_ready = sem("mpieces_ready")
        m_turned = sem("m_turned")
        m_copied = sem("m_copied")
        m_in = [sem("m_in0"), sem("m_in1")]
        scores2 = sem("scores2")
        exp_done = sem("exp_done")
        pv_done = sem("pv_done")
        o_copied = sem("o_copied")
        o_turned = sem("o_turned")
        o_scaled = sem("o_scaled")
        wo_done = sem("wo_done")
        x1_ready = sem("x1_ready")
        x1b_ready = sem("x1b_ready")
        hid_done = sem("hid_done")
        hid_ready = sem("hid_ready")
        ffn_done = sem("ffn_done")
        x2_ready = sem("x2_ready")
        z_ready = sem("z_ready")
        projb_done = sem("projb_done")
        raw_ready = sem("raw_ready")
        beta_ready = sem("beta_ready")
        conv_ready = sem("conv_ready")
        silu_ready = sem("silu_ready")
        sq_ready = sem("sq_ready")
        ss_done = sem("ss_done")
        rn_ready = sem("rn_ready")
        unit_ready = sem("unit_ready")
        prod_ready = sem("prod_ready")
        pairs_done = sem("pairs_done")
        pairs_copied = sem("pairs_copied")
        lanes_out = sem("lanes_out")
        lanes_in = sem("lanes_in")
        tm_ready = sem("tm_ready")
        til_ready = sem("til_ready")
        scan_done = sem("scan_done")
        terms_ready = sem("terms_ready")
        o_ready = sem("o_ready")
        o_out = sem("o_out")
        o_in = sem("o_in")
        osq_ready = sem("osq_ready")
        oss_done = sem("oss_done")
        ors_ready = sem("ors_ready")
        on_ready = sem("on_ready")
        wout_done = sem("wout_done")
        y_ready = sem("y_ready")
        xy_ready = sem("xy_ready")
        var_c_ready = sem("var_c_ready")
        rstd_c_ready = sem("rstd_c_ready")
        tok_c_ready = sem("tok_c_ready")
        turned_c = sem("turned_c")
        feat_c_ready = sem("feat_c_ready")
        gu_done = sem("gu_done")
        gate_ready = sem("gate_ready")
        act_ready = sem("act_ready")
        mlp_done = sem("mlp_done")
        x3_ready = sem("x3_ready")
        x3b_ready = sem("x3b_ready")
        hid_c_done = sem("hid_c_done")
        hid_c_ready = sem("hid_c_ready")
        ffn_c_done = sem("ffn_c_done")
        out_ready = sem("out_ready")
        out_stored = sem("out_stored")

        inner = [(i, min(128, INTER - 128 * i)) for i in range(IT)]
        N_UNITS = B * H // 2
        STACK_DMAS = 2 * len(PIECE_PAIRS) + 2
        x_v = a["x"].rearrange("b (n p) d -> n p b d", p=W)
        out_v = a["out"].rearrange("b (n p) d -> n p b d", p=W)

        plain = [
            (wqkv_a[:], a["wqkv_a"].rearrange("(k p) n -> p k n", p=128)),
            (wo_a[:], a["wo_a"].rearrange("(k p) n -> p k n", p=128)),
            (b_up[:], a["b_up"]),
            (b_dn[:], a["b_dn"].broadcast_to([128, D])),
            (conv_w[:], a["conv_w"]),
            (wqkv_b[:], a["wqkv_b"].rearrange("(k p) n -> p k n", p=128)),
            (wbeta[:], a["wbeta"].rearrange("(k p) b n -> p k b n", p=128)),
            (norm_w[:], a["norm_w"]),
            (wout_b[:], a["wout_b"].rearrange("(k p) n -> p k n", p=128)),
            (wgu[:], a["wgu"].rearrange("(k p) n -> p k n", p=128)),
        ]
        consts = [(ident[:], a["ident"]), (ones[:], a["ones"]), (head_sum[:], a["head_sum"]),
                  (to_lanes[:], a["to_lanes"]), (edge_mask_f[:], a["edge_mask"]),
                  (tri_mask_f[:], a["tri_mask"]), (stack_cols[:], a["stack_cols"]), (eps[:], a["eps"])]
        q_up = k_stack[:, 0].rearrange("p a b -> p (a b)").bitcast(I32)
        q_dn = k_stack[:, 1].rearrange("p a b -> p (a b)").bitcast(I32)
        s_up = lane_buf[:, 0:KT * FF]
        s_dn = lane_buf[:, KT * FF:KT * FF + FT * D]
        lora_a_up = sqk[0:RANK, 0, 0:D]
        lora_b_dn = sqk[0:RANK, 0, D:2 * D]
        lora_b_up = hid[0:RANK, 0:4, :].rearrange("p a b -> p (a b)")
        lora_a_dn = hid[0:RANK, 4:8, :].rearrange("p a b -> p (a b)")

        block = ctx.enter_context(nc.Block())

        @block.sync
        def _(sp):
            for dst, src in consts:
                sp.dma_start(dst, src).then_inc(consts_in, 16)
            sp.dma_start(q_up.rearrange("p (k n) -> p k n", k=KT),
                         a["q_up"].rearrange("(k p) n -> p k n", p=128)).then_inc(quant_in, 16)
            sp.dma_start(q_dn.rearrange("p (k n) -> p k n", k=FT),
                         a["q_dn"].rearrange("(k p) n -> p k n", p=128)).then_inc(quant_in, 16)
            for half in range(128 // QBLK):
                rows = slice(half * QBLK, (half + 1) * QBLK)
                for k in range(KT):
                    sp.dma_start(s_up[rows, k * FF:(k + 1) * FF],
                                 a["s_up"][2 * k + half:2 * k + half + 1, :].broadcast_to([QBLK, FF])
                                 ).then_inc(quant_in, 16)
                for k in range(FT):
                    sp.dma_start(s_dn[rows, k * D:(k + 1) * D],
                                 a["s_dn"][2 * k + half:2 * k + half + 1, :].broadcast_to([QBLK, D])
                                 ).then_inc(quant_in, 16)
            for dst, src in [(lora_a_up, a["lora_a_up"]), (lora_b_dn, a["lora_b_dn"]),
                             (lora_b_up, a["lora_b_up"]), (lora_a_dn, a["lora_a_dn"])]:
                sp.dma_start(dst, src).then_inc(lora_in, 16)
            sp.wait_ge(zeroed, 1)
            for p in range(3):
                for hh in range(HH):
                    sp.dma_start(k_pieces[p, hh, :, :, 0:W],
                                 q_stack[:, 0, 0:B, :]).then_inc(pad_out, 16)
            sp.wait_ge(pad_out, 16 * 3 * HH)
            sp.wait_ge(stack_init, 2)

            with sp.Fori(0, NB) as n:
                sp.wait_ge(x_used, n + 1)
                sp.dma_start(x_in[:], x_v[bass.ds(n, 1)].rearrange("n p b d -> (n p) b d")).then_inc(x_loaded, 16)
                sp.wait_ge(piece3, n * 2 + 2)
                for p in range(3):
                    sp.dma_start(q_pieces[p].rearrange("h p b t -> p h b t"),
                                 pieces[:, 0, p, :].rearrange("p (h b t) -> p h b t", h=HH, b=B)
                                 ).then_inc(pieces_out, 16)
                    for hh in range(HH):
                        sp.dma_start(k_pieces[p, hh, :, :, bass.ds(n * W + W, W)],
                                     pieces[:, 1, p, hh * BT:(hh + 1) * BT].rearrange("p (b t) -> p b t", b=B)
                                     ).then_inc(pieces_out, 16)
                sp.wait_ge(pieces_out, n * 144 + 144)

                def load_stacks(g):
                    b, hh = divmod(g, HH)
                    for r, (i, j) in enumerate(PIECE_PAIRS):
                        rows = slice(r * DK, (r + 1) * DK)
                        sp.dma_start(q_stack[rows, g % 2], q_pieces[i, hh, :, b, :].rearrange(
                            "(h d) t -> d h t", d=DK)).then_inc(stacks_in[g % 2], 16)
                        sp.dma_start(k_stack[rows, g % 2], k_pieces[j, hh, :, b, bass.ds(n * W, 2 * W)].rearrange(
                            "(h d) t -> d h t", d=DK)).then_inc(stacks_in[g % 2], 16)
                    sp.dma_start(q_stack[MROW:MROW + 3, g % 2], a["zero_rows"]).then_inc(stacks_in[g % 2], 16)
                    sp.dma_start(k_stack[PADROW:PADROW + 1, g % 2],
                                 a["pad_row"][:, bass.ds(n * W, 2 * W)].rearrange("a (o t) -> a o t", o=1)
                                 .broadcast_to([1, HPH, 2 * W])).then_inc(stacks_in[g % 2], 16)

                def load_max(g):
                    sp.wait_ge(m_copied, n * (NG // 2) + g // 2 + 1)
                    for j in range(3):
                        sp.dma_start(q_stack[MROW + j:MROW + j + 1, g % 2],
                                     m_rows[((g % 2) * 3 + j) * HPH:((g % 2) * 3 + j + 1) * HPH, g // 2, :]).then_inc(m_in[g % 2], 16)

                for g in range(2):
                    load_stacks(g)
                for g in range(2):
                    load_max(g)
                for g in range(2, NG):
                    sp.wait_ge(scores2, n * N_UNITS + (g - 1) * UPG)
                    load_stacks(g)
                for g in range(2, NG):
                    load_max(g)
                sp.wait_ge(unit_ready, n * 2 + 2)
                sp.wait_ge(silu_ready, n * 3 + 3)
                for s, dst in enumerate((lane_q, lane_k, lane_v)):
                    for hh in range(HH):
                        sp.dma_start(dst[:, hh].rearrange("b p t -> p b t"),
                                     conv[:, s, hh * BT:(hh + 1) * BT].rearrange("p (b t) -> p b t", b=B)
                                     ).then_inc(lanes_out, 16)
                sp.wait_ge(lanes_out, n * 96 + 96)
                for src, dst in ((lane_q, q_l), (lane_k, k_l)):
                    sp.dma_start(dst[:].rearrange("p k t -> p (k t)"),
                                 src.rearrange("b hh (h o d) t -> (b hh h) o (d t)", o=1, d=DK)
                                 .broadcast_to([B * H, VH, DK * W])).then_inc(lanes_in, 16)
                sp.dma_start(v_l[:].rearrange("p k t -> p (k t)"),
                             lane_v.rearrange("b hh (h v) t -> (b hh h) (v t)", v=VR)).then_inc(lanes_in, 16)
                sp.wait_ge(o_ready, n * 2 + 2)
                sp.dma_start(lane_o.rearrange("b hh (h v) t -> (b hh h) (v t)", v=VR),
                             o_l.rearrange("p v c i -> p (v c i)")).then_inc(o_out, 16)
                sp.wait_ge(o_out, n * 16 + 16)
                for hh in range(HH):
                    sp.dma_start(o_t[:, hh], lane_o[:, hh].rearrange("b p t -> p b t")).then_inc(o_in, 16)
                sp.wait_ge(out_ready, n + 1)
                sp.dma_start(out_v[bass.ds(n, 1)].rearrange("n p b d -> (n p) b d"), x_out[:]).then_inc(out_stored, 16)
            sp.wait_ge(out_stored, 16 * NB + 16)

        @block.gpsimd
        def _(pool):
            pool.memset(q_stack[:], 0.0).then_inc(zeroed, 1)
            pool.memset(v_ext[:], 0.0).then_inc(gstep, 1)
            pool.wait_ge(gstep, 1)
            pool.memset(v_ext[:, :, :, :, DK:DK + 1], 1.0).then_inc(zeroed, 1)
            pool.memset(raw[:], 0.0).then_inc(zeroed, 1)
            pool.memset(tm[:], 0.0).then_inc(zeroed, 1)
            pool.memset(mm_[:], 0.0).then_inc(zeroed, 1)
            pool.memset(state[:], 0.0).then_inc(zeroed, 1)
            pool.sem_clear(gstep)

            def body(n):
                steps = 0

                def done(ins):
                    nonlocal steps
                    steps += 1
                    ins.then_inc(gstep, 1)
                    pool.wait_ge(gstep, steps)

                pool.wait_ge(x1_ready, n + 1)
                for b in range(B):
                    last = pool.tensor_tensor(x1b[:, b], x1[:, b], b_dn[:], ALU.add)
                last.then_inc(x1b_ready, 1)
                pool.wait_ge(tm_ready, n + 1)
                pool.wait_ge(lanes_in, n * 48 + 48)
                kc = k_l[:].rearrange("p k (c i) -> p c i k", i=C)
                vc = v_l[:].rearrange("p v (c i) -> p c v i", i=C)
                for j in range(C):
                    rows = C - j
                    out = (k_til if j == 0 else tmp_k)[:, :, j:C, :]
                    for i in range(j, C):
                        last = pool.tensor_tensor(
                            (k_til if j == 0 else tmp_k)[:, :, i, :],
                            tm[:, :, i, j:j + 1].broadcast_to([128, NC_, DK]), kc[:, :, j, :], ALU.mult)
                    done(last)
                    if j:
                        done(pool.tensor_tensor(k_til[:, :, j:C, :], k_til[:, :, j:C, :],
                                                tmp_k[:, :, j:C, :], ALU.add))
                for j in range(C):
                    for i in range(j, C):
                        dst = first[:, :, :, i, DK] if j == 0 else tmp_v[:, :, :, i]
                        last = pool.tensor_tensor(dst, tm[:, :, i, j:j + 1].broadcast_to([128, NC_, VR]),
                                                  vc[:, :, :, j], ALU.mult)
                    if j:
                        done(last)
                        last = pool.tensor_tensor(first[:, :, :, j:C, DK], first[:, :, :, j:C, DK],
                                                  tmp_v[:, :, :, j:C], ALU.add)
                    if j == C - 1:
                        last.then_inc(til_ready, 1)
                    else:
                        done(last)
                pool.wait_ge(scan_done, n + 1)
                qc = q_l[:].rearrange("p k (c i) -> p c i k", i=C)
                for half in range(2):
                    if half:
                        pool.wait_ge(o_ready, n * 2 + 1)
                    for vv in range(2):
                        v = 2 * half + vv
                        for i in range(C):
                            pool.tensor_tensor(out_terms[:, vv, :, i, 0:DK], state[:, 0:NC_, v, :, C],
                                               qc[:, :, i, :], ALU.mult)
                            last = pool.tensor_tensor(out_terms[:, vv, :, i, DK:DK + C],
                                                      mm_[:, i].rearrange("p j c -> p c j"),
                                                      u_l[:, :, v, :], ALU.mult)
                    last.then_inc(terms_ready, 1)
                pool.wait_ge(y_ready, n + 1)
                pool.tensor_tensor(xy[:], x2[:], y[:], ALU.add).then_inc(xy_ready, 1)
                pool.wait_ge(x3_ready, n + 1)
                for b in range(B):
                    last = pool.tensor_tensor(x3b[:, b], x3[:, b], b_dn[:], ALU.add)
                last.then_inc(x3b_ready, 1)
                pool.sem_clear(gstep)

            with pool.Fori(0, NB) as n:
                body(n)

        @block.scalar
        def _(act):
            for dst, src in plain:
                act.dma_start(dst, src).then_inc(weights_in, 16)
            for i, m in inner:
                act.dma_start(wdown_b[0:m, i, :], a["wdown_b"][128 * i:128 * i + m, :]).then_inc(weights_in, 16)

            def body(n):
                steps = 0

                def done(ins):
                    nonlocal steps
                    steps += 1
                    ins.then_inc(astep, 1)
                    act.wait_ge(astep, steps)

                def rsqrt(dst, src, tmp, e, scale):
                    done(act.activation(tmp, src, ACT.Ln, bias=eps[:, e:e + 1], scale=scale))
                    return act.activation(dst, tmp, ACT.Exp, scale=-0.5)

                def norm_a(k):
                    act.wait_ge(vars_ready, n * 3 + k)
                    rsqrt(rstd[:], mv[:, :, 1], lnv[:], 0, 1.0).then_inc(rstd_ready, 1)

                def turn_a(k):
                    act.wait_ge(turned, n * 4 + k)
                    act.copy(feat[:].rearrange("p k b t -> p (k b t)"), bank[0][:]).then_inc(feat_ready, 1)

                def ffn(hidden, hid_bank, done_sem, ready_sem):
                    for i in range(FT):
                        act.wait_ge(done_sem, n * FT + i + 1)
                        act.activation(hidden[:, i, :], hid_bank[i % 2][:, 0:BT], ACT.Relu,
                                       bias=b_up[:, i:i + 1]).then_inc(ready_sem, 1)

                norm_a(1)
                turn_a(1)
                for s in range(2):
                    act.wait_ge(qkv_done, n * 3 + s + 1)
                    act.copy(pieces[:, s, 0], bank[1 + s][:]).then_inc(piece1, 1)
                for s in range(2):
                    act.wait_ge(rest1, n * 2 + s + 1)
                    act.copy(pieces[:, s, 1], rest[:, s]).then_inc(piece2, 1)
                act.wait_ge(qkv_done, n * 3 + 3)
                for b in range(B):
                    last = act.copy(v_ext[:, b, 1, :, 0:DK],
                                    bank[3][:, b * D:(b + 1) * D].rearrange("p (h d) -> p h d", d=DK))
                last.then_inc(v_done, 1)
                for pair in range(NG // 2):
                    act.wait_ge(m_turned, n * (NG // 2) + pair + 1)
                    act.copy(m_rows[:, pair], bank_b[0:6 * HPH, 0:W]).then_inc(m_copied, 1)
                    for g in (2 * pair, 2 * pair + 1):
                        for u in range(g * UPG, (g + 1) * UPG):
                            act.wait_ge(scores2, n * N_UNITS + u + 1)
                            act.activation(probs[:, u % 2], bank[3 + u % 2][:], ACT.Exp,
                                           scale=float(DK) ** -0.5).then_inc(exp_done, 1)
                        act.wait_ge(pv_done, n * NG + g + 1)
                        if g:
                            act.wait_ge(o_turned, n * NG + g)
                        act.copy(o_rows[:], bank[5][:]).then_inc(o_copied, 1)
                done(act.copy(v_ext[:, :, 0, :, 0:DK], v_ext[:, :, 1, :, 0:DK]))
                turn_a(2)
                norm_a(2)
                turn_a(3)
                ffn(hid, (bank[1], bank[2]), hid_done, hid_ready)
                norm_a(3)
                act.wait_ge(z_ready, n + 1)
                for b in range(B):
                    done(act.activation(sq[:], z[:, b], ACT.Square, accum_out=lnv[:, b:b + 1]))
                rsqrt(rstd[:], lnv[:], lnt[:], 1, 1.0 / D).then_inc(sq_rstd, 1)
                turn_a(4)
                for s in range(3):
                    act.wait_ge(projb_done, n * 4 + s + 1)
                    for hh in range(HH):
                        last = act.copy(raw[:, s, hh, :, TAPS - 1:],
                                        bank[1 + s][:, hh * BT:(hh + 1) * BT].rearrange("p (b t) -> p b t", b=B))
                    last.then_inc(raw_ready, 1)
                act.wait_ge(projb_done, n * 4 + 4)
                act.activation(beta_l[:], bank[4][:, 0:W], ACT.Sigmoid).then_inc(beta_ready, 1)
                for s in range(3):
                    act.wait_ge(conv_ready, n * 3 + s + 1)
                    done(act.activation(conv[:, s], conv[:, s], ACT.Silu))
                    last = act.activation(conv[:, s], conv[:, s], ACT.Silu)
                    last.then_inc(silu_ready, 1)
                    if s < 2:
                        act.wait_ge(silu_ready, n * 3 + s + 1)
                        act.activation(sqk[:, s], conv[:, s], ACT.Square).then_inc(sq_ready, 1)
                for s in range(2):
                    act.wait_ge(ss_done, n * 2 + s + 1)
                    done(act.activation(sqk[:, s], bank[1 + s][:], ACT.Relu, bias=eps[:, 2:3]))
                    done(act.activation(sqk[:, s], sqk[:, s], ACT.Ln, bias=eps[:, 3:4]))
                    act.activation(sqk[:, s], sqk[:, s], ACT.Exp, scale=-0.5).then_inc(rn_ready, 1)
                act.wait_ge(pairs_done, n + 1)
                act.copy(pair_l[:].rearrange("p a c -> p (a c)"), bank[3][:]).then_inc(pairs_copied, 1)
                act.wait_ge(o_in, n * 32 + 32)
                act.activation(o_n[:], o_t, ACT.Square).then_inc(osq_ready, 1)
                act.wait_ge(oss_done, n + 1)
                rsqrt(rs_o[:], bank[6][:, 0:BT], rs_o[:], 1, 1.0 / D).then_inc(ors_ready, 1)
                act.wait_ge(y_ready, n + 1)
                for b in range(B):
                    done(act.activation(sq_c[:], y[:, b], ACT.Square, accum_out=lnv_c[:, b:b + 1]))
                rsqrt(rstd_c[:], lnv_c[:], lnt_c[:], 1, 1.0 / D).then_inc(rstd_c_ready, 1)
                act.wait_ge(turned_c, n * 2 + 1)
                act.copy(feat_c[:].rearrange("p k b t -> p (k b t)"), bank[7][:]).then_inc(feat_c_ready, 1)
                for i, m in inner:
                    act.wait_ge(gu_done, n * IT + i + 1)
                    if i >= 2:
                        act.wait_ge(act_ready, n * IT + i - 1)
                    act.activation(gate[0:m, i % 2], bank[6 + i % 2][0:m, 0:BT], ACT.Silu).then_inc(gate_ready, 1)
                act.wait_ge(var_c_ready, n + 1)
                rsqrt(rstd_c[:], mv_c[:, :, 1], lnv_c[:], 0, 1.0).then_inc(rstd_c_ready, 1)
                act.wait_ge(turned_c, n * 2 + 2)
                act.copy(feat_c[:].rearrange("p k b t -> p (k b t)"), bank[7][:]).then_inc(feat_c_ready, 1)
                ffn(hid_c, (bank[6], bank[7]), hid_c_done, hid_c_ready)
                act.sem_clear(astep)

            act.wait_ge(consts_in, 16 * len(consts))
            act.wait_ge(weights_in, 16 * (len(plain) + IT))
            with act.Fori(0, NB) as n:
                body(n)

        @block.vector
        def _(dve):
            dve.wait_ge(consts_in, 16 * len(consts))
            dve.tensor_copy(identb[:], ident[:])
            dve.tensor_copy(edge_mask[:], edge_mask_f[:])
            dve.tensor_copy(tri_mask[:], tri_mask_f[:]).then_inc(consts_cast, 1)
            dve.wait_ge(quant_in, 16 * (2 + 2 * (KT + FT)))
            dve.scalar_tensor_tensor(out=w_up[:].rearrange("p k n -> p (k n)"), in0=q_up, scalar=-7.5,
                                     in1=s_up, op0=ALU.add, op1=ALU.mult)
            dve.scalar_tensor_tensor(out=w_dn[:].rearrange("p k n -> p (k n)"), in0=q_dn, scalar=-7.5,
                                     in1=s_dn, op0=ALU.add, op1=ALU.mult).then_inc(vstep, 1)
            dve.wait_ge(vstep, 1)
            dve.wait_ge(lora_prod, 1)
            for k in range(KT):
                for c in range(2):
                    w = w_up[:, k, c * 512:(c + 1) * 512]
                    dve.tensor_tensor(w, w, bank[2 * k + c][:], ALU.add)
            for k in range(FT // 2):
                w = w_dn[:, 2 * k:2 * k + 2, :].rearrange("p a n -> p (a n)")
                dve.tensor_tensor(w, w, bank[4 + k][:], ALU.add).then_inc(lora_added, 1)
            dve.wait_ge(weights_in, 16 * (len(plain) + IT))
            for k in range(KT):
                for w, i in ((wqkv_b[:, k], 0), (wbeta[:, k], 0), (wout_b[:, k], 1), (wgu[:, k], 2)):
                    last = dve.tensor_scalar(w, w, norm_w[:, i, k:k + 1], None, ALU.mult)
            last.then_inc(weights_scaled, 1)
            dve.wait_ge(zeroed, 6)
            dve.wait_ge(pad_out, 16 * 3 * HH)
            dve.tensor_scalar(q_stack[:], q_stack[:], stack_cols[:, 0:1], None, ALU.add).then_inc(stack_init, 1)
            dve.memset(k_stack[:], 0.0).then_inc(vstep, 1)
            dve.wait_ge(vstep, 2)
            dve.tensor_scalar(k_stack[:], k_stack[:], stack_cols[:, 1:2], None, ALU.add).then_inc(stack_init, 1)
            dve.sem_clear(vstep)
            dve.nop().then_inc(x_used, 1)
            dve.nop().then_inc(out_stored, 16)

            def body(n):
                steps = 0

                def done(ins):
                    nonlocal steps
                    steps += 1
                    ins.then_inc(vstep, 1)
                    dve.wait_ge(vstep, steps)

                def normalise(src, dst, st, m_v, rs, ready, rs_sem, rs_count):
                    for b in range(B):
                        last = dve.bn_stats(st[:, b], src[:, b])
                    done(last)
                    for b in range(B):
                        last = dve.bn_aggr(m_v[:, b], st[:, b])
                    last.then_inc(ready, 1)
                    dve.wait_ge(rs_sem, rs_count)
                    for b in range(B):
                        last = dve.tensor_scalar(dst[:, b], src[:, b], m_v[:, b, 0:1], rs[:, b:b + 1],
                                                 ALU.subtract, ALU.mult)
                    return last

                dve.wait_ge(x_loaded, n * 16 + 16)
                normalise(x_in, tok, stats, mv, rstd, vars_ready, rstd_ready, n * 3 + 1).then_inc(tok_ready, 1)
                for s in range(2):
                    dve.wait_ge(piece1, n * 2 + s + 1)
                    dve.tensor_tensor(rest[:, s], bank[1 + s][:], pieces[:, s, 0], ALU.subtract).then_inc(rest1, 1)
                for s in range(2):
                    dve.wait_ge(piece2, n * 2 + s + 1)
                    dve.tensor_tensor(pieces[:, s, 2], rest[:, s], pieces[:, s, 1], ALU.subtract).then_inc(piece3, 1)
                for pair in range(NG // 2):
                    for g in (2 * pair, 2 * pair + 1):
                        for u in range(UPG):
                            v = g * UPG + u
                            dve.wait_ge(scores1, n * N_UNITS + v + 1)
                            last = dve.tensor_reduce(
                                mx[:, g, 2 * u:2 * u + 2],
                                bank[1 + v % 2][:, 0:2 * SPAN].rearrange("p (h k) -> p h k", h=2), AX.X, ALU.max)
                            last.then_inc(max_done, 1)
                        dve.wait_ge(max_done, n * N_UNITS + (g + 1) * UPG)
                        nm = nmx[:, g]
                        done(dve.tensor_scalar(nm, mx[:, g], -1.0, None, ALU.mult))
                        done(dve.tensor_copy(mpieces[:, g, 0], nm))
                        done(dve.tensor_tensor(nm, nm, mpieces[:, g, 0], ALU.subtract))
                        done(dve.tensor_copy(mpieces[:, g, 1], nm))
                        dve.tensor_tensor(mpieces[:, g, 2], nm, mpieces[:, g, 1], ALU.subtract).then_inc(mpieces_ready, 1)
                    for g in (2 * pair, 2 * pair + 1):
                        b, hh = divmod(g, HH)
                        dve.wait_ge(o_turned, n * NG + g + 1)
                        ov = bank[0][:].rearrange("p (h e) -> p h e", e=32)
                        done(dve.reciprocal(rden[:], ov[:, :, DK]))
                        dve.tensor_tensor(
                            tok[:, b, hh * 128:(hh + 1) * 128].rearrange("p (h d) -> p h d", d=DK), ov[:, :, 0:DK],
                            rden[:].rearrange("p (h o) -> p h o", o=1).broadcast_to([128, HPH, DK]),
                            ALU.mult).then_inc(o_scaled, 1)
                dve.wait_ge(o_scaled, n * 4 + 4)
                dve.nop().then_inc(tok_ready, 1)
                dve.wait_ge(wo_done, n + 1)
                done(dve.tensor_tensor(x1[:].rearrange("p b d -> p (b d)"), bank[1][:],
                                       x_in[:].rearrange("p b d -> p (b d)"), ALU.add))
                dve.nop().then_inc(x_used, 1)
                dve.nop().then_inc(x1_ready, 1)
                normalise(x1, tok, stats, mv, rstd, vars_ready, rstd_ready, n * 3 + 2).then_inc(tok_ready, 1)
                dve.wait_ge(ffn_done, n + 1)
                dve.wait_ge(x1b_ready, n + 1)
                done(dve.tensor_tensor(x2[:].rearrange("p b d -> p (b d)"), bank[3][:],
                                       x1b[:].rearrange("p b d -> p (b d)"), ALU.add))
                normalise(x2, z, stats, mv, rstd, vars_ready, rstd_ready, n * 3 + 3).then_inc(z_ready, 1)
                dve.wait_ge(sq_rstd, n + 1)
                for b in range(B):
                    last = dve.tensor_scalar(tok[:, b], z[:, b], rstd[:, b:b + 1], None, ALU.mult)
                last.then_inc(tok_ready, 1)
                for s in range(3):
                    dve.wait_ge(raw_ready, n * 3 + s + 1)
                    for tap in range(TAPS):
                        for hh in range(HH):
                            src = raw[:, s, hh, :, tap:tap + W]
                            dst = conv[:, s, hh * BT:(hh + 1) * BT].rearrange("p (b t) -> p b t", b=B)
                            w = conv_w[:, s, hh, tap:tap + 1]
                            if tap == 0:
                                last = dve.tensor_scalar(dst, src, w, None, ALU.mult)
                            else:
                                last = dve.scalar_tensor_tensor(out=dst, in0=src, scalar=w, in1=dst,
                                                                op0=ALU.mult, op1=ALU.add)
                        if tap < TAPS - 1:
                            done(last)
                    last.then_inc(conv_ready, 1)
                dve.tensor_copy(raw[:, :, :, :, 0:TAPS - 1].rearrange("p s h b t -> p (s h b) t"),
                                raw[:, :, :, :, W:W + TAPS - 1].rearrange("p s h b t -> p (s h b) t"))
                for s in range(2):
                    dve.wait_ge(rn_ready, n * 2 + s + 1)
                    dve.tensor_tensor(conv[:, s], conv[:, s], sqk[:, s], ALU.mult).then_inc(unit_ready, 1)
                dve.wait_ge(unit_ready, n * 2 + 2)
                for hh in range(HH):
                    kk = conv[:, 1, hh * BT:(hh + 1) * BT].rearrange("p (b c i) -> p b i c", b=B, i=C)
                    qq = conv[:, 0, hh * BT:(hh + 1) * BT].rearrange("p (b c i) -> p b i c", b=B, i=C)
                    at = 0
                    for left, lo in ((kk, 1), (qq, 0)):
                        for i in range(lo, C):
                            m = i if lo else i + 1
                            for b in range(B):
                                last = dve.tensor_tensor(prodk[:, hh, b, at:at + m, :], kk[:, b, 0:m],
                                                         left[:, b, i:i + 1].broadcast_to([128, m, NC_]), ALU.mult)
                            at += m
                last.then_inc(prod_ready, 1)
                dve.wait_ge(pairs_copied, n + 1)
                dve.wait_ge(beta_ready, n + 1)
                bc = beta_l[:].rearrange("p (c i) -> p c i", i=C)
                for i in range(C):
                    dve.tensor_scalar(tm[:, :, i, i], bc[:, :, i], -1.0, None, ALU.mult)
                for at, (i, j) in enumerate(PAIRS_K):
                    dve.scalar_tensor_tensor(out=pair_l[:, at, :], in0=pair_l[:, at, :], scalar=-1.0,
                                             in1=bc[:, :, i], op0=ALU.mult, op1=ALU.mult)
                for at, (i, j) in enumerate(PAIRS_Q):
                    dve.tensor_copy(mm_[:, i, j, :], pair_l[:, NPK + at, :])
                done(dve.tensor_copy(state[:, 0, :, :, C], state[:, NC_, :, :, C]))
                for i in range(1, C):
                    for j in reversed(range(i)):
                        at = PAIRS_K.index((i, j))
                        g = pair_l[:, at, :].rearrange("p (c o) -> p c o", o=1).broadcast_to([128, NC_, j + 1])
                        row = tm[:, :, i, 0:j + 1]
                        if j == i - 1:
                            done(dve.tensor_tensor(row, g, tm[:, :, j, 0:j + 1], ALU.mult))
                        else:
                            done(dve.tensor_tensor(tmp_t[:, :, 0:j + 1], g, tm[:, :, j, 0:j + 1], ALU.mult))
                            done(dve.tensor_tensor(row, row, tmp_t[:, :, 0:j + 1], ALU.add))
                dve.nop().then_inc(tm_ready, 1)
                kc = k_l[:].rearrange("p k (c i) -> p c k i", i=C)
                dve.wait_ge(lanes_in, n * 48 + 48)
                dve.wait_ge(til_ready, n + 1)
                for c in range(NC_):
                    done(dve.tensor_tensor(
                        first[:, c, :, :, 0:DK],
                        state[:, c, :, :, C].rearrange("p v (o k) -> p v o k", o=1).broadcast_to([128, VR, C, DK]),
                        k_til[:, c:c + 1].broadcast_to([128, VR, C, DK]), ALU.mult))
                    done(dve.tensor_reduce(u_l[:, c], first[:, c], AX.X, ALU.add))
                    done(dve.tensor_tensor(
                        state[:, c, :, :, 0:C],
                        u_l[:, c].rearrange("p v (o i) -> p v o i", o=1).broadcast_to([128, VR, DK, C]),
                        kc[:, c:c + 1].broadcast_to([128, VR, DK, C]), ALU.mult))
                    done(dve.tensor_reduce(state[:, c + 1, :, :, C], state[:, c], AX.X, ALU.add))
                dve.nop().then_inc(scan_done, 1)
                for half in range(2):
                    dve.wait_ge(terms_ready, n * 2 + half + 1)
                    dve.tensor_reduce(o_l[:, 2 * half:2 * half + 2].rearrange("p v c i -> p (v c i)"),
                                      out_terms.rearrange("p v c i e -> p (v c i) e"), AX.X,
                                      ALU.add).then_inc(o_ready, 1)
                dve.wait_ge(ors_ready, n + 1)
                dve.wait_ge(oss_done, n + 1)
                for hh in range(HH):
                    last = dve.scalar_tensor_tensor(out=o_n[:, hh].rearrange("p b t -> p (b t)"),
                                                    in0=o_t[:, hh].rearrange("p b t -> p (b t)"), scalar=-1.0,
                                                    in1=rs_o[:], op0=ALU.mult, op1=ALU.mult)
                last.then_inc(on_ready, 1)
                dve.wait_ge(wout_done, n + 1)
                dve.tensor_tensor(y[:].rearrange("p b d -> p (b d)"), bank[6][:],
                                  z[:].rearrange("p b d -> p (b d)"), ALU.add).then_inc(y_ready, 1)
                dve.wait_ge(rstd_c_ready, n * 2 + 1)
                for b in range(B):
                    last = dve.tensor_scalar(tok_c[:, b], y[:, b], rstd_c[:, b:b + 1], None, ALU.mult)
                last.then_inc(tok_c_ready, 1)
                for i, m in inner:
                    dve.wait_ge(gate_ready, n * IT + i + 1)
                    dve.tensor_tensor(act_c[0:m, i], bank[6 + i % 2][0:m, BT:2 * BT], gate[0:m, i % 2],
                                      ALU.mult).then_inc(act_ready, 1)
                dve.wait_ge(mlp_done, n + 1)
                dve.wait_ge(xy_ready, n + 1)
                done(dve.tensor_tensor(x3[:].rearrange("p b d -> p (b d)"), bank[6][:],
                                       xy[:].rearrange("p b d -> p (b d)"), ALU.add))
                dve.nop().then_inc(x3_ready, 1)
                normalise(x3, tok_c, stats_c, mv_c, rstd_c, var_c_ready, rstd_c_ready, n * 2 + 2).then_inc(tok_c_ready, 1)
                dve.wait_ge(ffn_c_done, n + 1)
                dve.wait_ge(x3b_ready, n + 1)
                dve.wait_ge(out_stored, n * 16 + 16)
                dve.tensor_tensor(x_out[:].rearrange("p b d -> p (b d)"), bank[6][:],
                                  x3b[:].rearrange("p b d -> p (b d)"), ALU.add).then_inc(out_ready, 1)
                dve.sem_clear(vstep)

            with dve.Fori(0, NB) as n:
                body(n)

        @block.tensor
        def _(pe):
            pe.wait_ge(lora_in, 64)
            for k in range(KT):
                for c in range(2):
                    pe.matmul(bank[2 * k + c][:], lora_a_up[:, k * 128:(k + 1) * 128],
                              lora_b_up[:, c * 512:(c + 1) * 512], start=True, stop=True)
            for k in range(FT):
                last = pe.matmul(bank[4 + k // 2][:, (k % 2) * D:(k % 2 + 1) * D],
                                 lora_a_dn[:, k * 128:(k + 1) * 128], lora_b_dn, start=True, stop=True)
            last.then_inc(lora_prod, 1)
            pe.wait_ge(lora_added, FT // 2)
            pe.wait_ge(weights_scaled, 1)
            pe.wait_ge(consts_cast, 1)
            pe.wait_ge(stack_init, 2)

            def body(n):
                def turn(src, dst_bank):
                    for k in range(KT):
                        for b in range(B):
                            at = (k * B + b) * W
                            last = pe.transpose(dst_bank[:, at:at + W], src[:, b, k * 128:(k + 1) * 128], ident[:])
                    return last

                def turn_a(k):
                    pe.wait_ge(tok_ready, n * 4 + k)
                    turn(tok, bank[0]).then_inc(turned, 1)
                    pe.wait_ge(feat_ready, n * 4 + k)

                def to_tokens(dst, src, w, tiles):
                    for b in range(B):
                        for k, m in tiles:
                            last = pe.matmul(dst[:, b * D:(b + 1) * D], src[0:m, k, b * W:(b + 1) * W],
                                             w[0:m, k, :], start=(k == 0), stop=(k == tiles[-1][0]))
                    return last

                def ffn(ft, hidden, hid_bank, out_bank, done_sem, ready_sem, ffn_sem):
                    f = ft[:].rearrange("p k b t -> p k (b t)")
                    for i in range(FT):
                        if i >= 2:
                            pe.wait_ge(ready_sem, n * FT + i - 1)
                        for k in range(KT):
                            last = pe.matmul(hid_bank[i % 2][:, 0:BT], w_up[:, k, i * 128:(i + 1) * 128],
                                             f[:, k], start=(k == 0), stop=(k == KT - 1))
                        last.then_inc(done_sem, 1)
                    pe.wait_ge(ready_sem, n * FT + FT)
                    to_tokens(out_bank, hidden, w_dn, [(k, 128) for k in range(FT)]).then_inc(ffn_sem, 1)

                turn_a(1)
                f = feat[:].rearrange("p k b t -> p k (b t)")
                for s in range(2):
                    for hh in range(HH):
                        for k in range(KT):
                            last = pe.matmul(bank[1 + s][:, hh * BT:(hh + 1) * BT],
                                             wqkv_a[:, k, s * D + hh * 128:s * D + (hh + 1) * 128],
                                             f[:, k], start=(k == 0), stop=(k == KT - 1))
                    last.then_inc(qkv_done, 1)
                for b in range(B):
                    for k in range(KT):
                        last = pe.matmul(bank[3][:, b * D:(b + 1) * D], feat[:, k, b, :],
                                         wqkv_a[:, k, 2 * D:3 * D], start=(k == 0), stop=(k == KT - 1))
                last.then_inc(qkv_done, 1)
                pe.wait_ge(rest1, n * 2 + 2)

                def scores_max(g):
                    pe.wait_ge(stacks_in[g % 2], (n * (NG // 2) + g // 2 + 1) * 16 * STACK_DMAS)
                    for v in range(UPG):
                        u = g * UPG + v
                        if u >= 2:
                            pe.wait_ge(max_done, n * N_UNITS + u - 1)
                        pb = bank[1 + u % 2][:, 0:2 * SPAN]
                        edges = pb.rearrange("p (h k) -> p h k", h=2)
                        for e in range(2):
                            pe.matmul(edges[:, :, e * W:e * W + SUB], identb[:],
                                      edge_mask[:, e * SUB:(e + 1) * SUB].rearrange("p (o s) -> p o s", o=1)
                                      .broadcast_to([128, 2, SUB]), start=(e == 0), stop=False, skip_group_check=True)
                        for hp in range(2):
                            for s in range(W // SUB):
                                last = pe.matmul(pb[s * SUB:(s + 1) * SUB, hp * SPAN:(hp + 1) * SPAN],
                                                 q_stack[:, g % 2, 2 * v + hp, s * SUB:(s + 1) * SUB],
                                                 k_stack[:, g % 2, 2 * v + hp, s * SUB:s * SUB + SPAN],
                                                 start=False, stop=True, skip_group_check=True)
                        last.then_inc(scores1, 1)

                def turn_max(pair):
                    pe.wait_ge(mpieces_ready, n * NG + 2 * pair + 2)
                    if pair:
                        pe.wait_ge(o_scaled, n * NG + 2 * pair)
                    pe.transpose(bank_b[0:6 * HPH, 0:W],
                                 mpieces[:, 2 * pair:2 * pair + 2].rearrange("p g j h -> p (g j h)"),
                                 identb[:]).then_inc(m_turned, 1)

                def scores(u):
                    g, v = divmod(u, UPG)
                    if v == 0:
                        pe.wait_ge(m_in[g % 2], (n * (NG // 2) + g // 2 + 1) * 48)
                    if u >= 2:
                        pe.wait_ge(exp_done, n * N_UNITS + u - 1)
                    pb = bank[3 + u % 2]
                    pe.matmul(pb[:], identb[:], tri_mask[:].rearrange("p (o t) -> p o t", o=1)
                              .broadcast_to([128, 2, 2 * W]), start=True, stop=False, skip_group_check=True)
                    for hp in range(2):
                        for kb in range(2):
                            at = (hp * 2 + kb) * W
                            last = pe.matmul(pb[:, at:at + W], k_stack[:, g % 2, 2 * v + hp, kb * W:(kb + 1) * W],
                                             q_stack[:, g % 2, 2 * v + hp, :], start=False, stop=True,
                                             skip_group_check=True)
                    last.then_inc(scores2, 1)

                def values(u):
                    g, v = divmod(u, UPG)
                    pe.wait_ge(exp_done, n * N_UNITS + u + 1)
                    if v == 0 and g:
                        pe.wait_ge(o_copied, n * NG + g)
                    for hp in range(2):
                        b, h = divmod(2 * u + hp, H)
                        row, col = 32 * (h % 4), (h % HPH) // 4 * W
                        for kb in range(2):
                            last = pe.matmul(bank[5][row:row + VE, col:col + W], v_ext[:, b, kb, h, :],
                                             probs[:, u % 2, (hp * 2 + kb) * W:(hp * 2 + kb + 1) * W],
                                             start=(kb == 0), stop=(kb == 1))
                    if v == UPG - 1:
                        last.then_inc(pv_done, 1)

                def turn_out(g):
                    pe.wait_ge(o_copied, n * NG + g + 1)
                    if g % 2 == 0:
                        pe.wait_ge(m_copied, n * (NG // 2) + g // 2 + 1)
                    else:
                        pe.wait_ge(o_scaled, n * NG + g)
                    for j in range(4):
                        last = pe.transpose(bank[0][:, j * W:(j + 1) * W], o_rows[:, j * W:(j + 1) * W], ident[:])
                    last.then_inc(o_turned, 1)

                for pair in range(NG // 2):
                    for g in (2 * pair, 2 * pair + 1):
                        scores_max(g)
                    turn_max(pair)
                    if pair == 0:
                        pe.wait_ge(v_done, n + 1)
                    u0, u1 = 2 * pair * UPG, (2 * pair + 2) * UPG
                    for u in range(u0, u1 + 1):
                        if u < u1:
                            scores(u)
                        if u > u0:
                            values(u - 1)
                        if u == u0 + UPG + 2:
                            turn_out(2 * pair)
                    turn_out(2 * pair + 1)
                turn_a(2)
                to_tokens(bank[1], f, wo_a, [(k, 128) for k in range(KT)]).then_inc(wo_done, 1)
                turn_a(3)
                pe.wait_ge(x1_ready, n + 1)
                ffn(feat, hid, (bank[1], bank[2]), bank[3], hid_done, hid_ready, ffn_done)
                turn_a(4)
                for s in range(3):
                    for hh in range(HH):
                        for k in range(KT):
                            last = pe.matmul(bank[1 + s][:, hh * BT:(hh + 1) * BT],
                                             wqkv_b[:, k, s * D + hh * 128:s * D + (hh + 1) * 128],
                                             f[:, k], start=(k == 0), stop=(k == KT - 1))
                    last.then_inc(projb_done, 1)
                for b in range(B):
                    for k in range(KT):
                        last = pe.matmul(bank[4][:, 0:W], wbeta[:, k, b, :], feat[:, k, b, :],
                                         start=(b == 0 and k == 0), stop=(b == B - 1 and k == KT - 1))
                last.then_inc(projb_done, 1)
                for s in range(2):
                    pe.wait_ge(raw_ready, n * 3 + s + 1)
                    pe.wait_ge(sq_ready, n * 2 + s + 1)
                    pe.matmul(bank[1 + s][:], head_sum[:], sqk[:, s], start=True, stop=True).then_inc(ss_done, 1)
                pe.wait_ge(prod_ready, n + 1)
                pe.wait_ge(raw_ready, n * 3 + 3)
                for hh in range(HH):
                    for b in range(B):
                        g = b * HH + hh
                        last = pe.matmul(bank[3][:], to_lanes[:, g], prodk[:, hh, b].rearrange("p a c -> p (a c)"),
                                         start=(hh == 0 and b == 0), stop=(hh == HH - 1 and b == B - 1))
                last.then_inc(pairs_done, 1)
                pe.wait_ge(osq_ready, n + 1)
                for hh in range(HH):
                    last = pe.matmul(bank[6][:, 0:BT], ones[:], o_n[:, hh].rearrange("p b t -> p (b t)"),
                                     start=(hh == 0), stop=(hh == HH - 1))
                last.then_inc(oss_done, 1)
                pe.wait_ge(on_ready, n + 1)
                pe.wait_ge(ors_ready, n + 1)
                to_tokens(bank[6], o_n[:].rearrange("p k b t -> p k (b t)"), wout_b,
                          [(k, 128) for k in range(KT)]).then_inc(wout_done, 1)
                pe.wait_ge(tok_c_ready, n * 2 + 1)
                turn(tok_c, bank[7]).then_inc(turned_c, 1)
                pe.wait_ge(feat_c_ready, n * 2 + 1)
                fc = feat_c[:].rearrange("p k b t -> p k (b t)")
                for i, m in inner:
                    if i == 0:
                        pe.wait_ge(y_ready, n + 1)
                    if i >= 2:
                        pe.wait_ge(act_ready, n * IT + i - 1)
                    for g in range(2):
                        for k in range(KT):
                            last = pe.matmul(bank[6 + i % 2][0:m, g * BT:(g + 1) * BT],
                                             wgu[:, k, g * INTER + 128 * i:g * INTER + 128 * i + m],
                                             fc[:, k], start=(k == 0), stop=(k == KT - 1))
                    last.then_inc(gu_done, 1)
                pe.wait_ge(act_ready, n * IT + IT)
                to_tokens(bank[6], act_c, wdown_b, inner).then_inc(mlp_done, 1)
                pe.wait_ge(tok_c_ready, n * 2 + 2)
                turn(tok_c, bank[7]).then_inc(turned_c, 1)
                pe.wait_ge(feat_c_ready, n * 2 + 2)
                pe.wait_ge(x3_ready, n + 1)
                ffn(feat_c, hid_c, (bank[6], bank[7]), bank[6], hid_c_done, hid_c_ready, ffn_c_done)

            with pe.Fori(0, NB) as n:
                body(n)


def kernel(**inputs):
    import numpy as np
    import ml_dtypes
    import concourse.bacc as bacc
    from concourse.bass_utils import run_bass_kernel_spmd

    g = {k: np.asarray(v) for k, v in inputs.items()}
    t = lambda x: np.ascontiguousarray(x)
    A, Bp, Fp = "L0_attn_a_", "L0_attn_b_", "L0_ffn_"
    rows = lambda v: v.reshape(-1, 128).T
    ar = {
        "x": g[A + "x"],
        "wqkv_a": np.concatenate([g[A + "Wq"].T, g[A + "Wk"].T, g[A + "Wv"].T], axis=1),
        "wo_a": g[A + "Wo"].T,
        "wqkv_b": np.concatenate([g[Bp + "Wq"].T, g[Bp + "Wk"].T, g[Bp + "Wv"].T], axis=1),
        "wout_b": g[Bp + "Wout"].T,
        "wgu": np.concatenate([g[Bp + "Wgate"].T, g[Bp + "Wup"].T], axis=1),
        "wdown_b": g[Bp + "Wdown"].T,
        "norm_w": np.stack([rows(g[Bp + n]) for n in ("attn_norm_w", "out_norm_w", "mlp_norm_w")], axis=1),
        "conv_w": np.stack([g[Bp + n].reshape(HH, 128, TAPS).transpose(1, 0, 2)
                            for n in ("conv_q", "conv_k", "conv_v")], axis=1),
        "q_up": g[Fp + "w_up_q"].T, "s_up": g[Fp + "w_up_scale"].T, "b_up": rows(g[Fp + "b_up"]),
        "lora_a_up": g[Fp + "w_up_lora_a"].T, "lora_b_up": g[Fp + "w_up_lora_b"],
        "q_dn": g[Fp + "w_down_q"].T, "s_dn": g[Fp + "w_down_scale"].T, "b_dn": g[Fp + "b_down"][None],
        "lora_a_dn": g[Fp + "w_down_lora_a"].T, "lora_b_dn": g[Fp + "w_down_lora_b"],
    }
    wb = np.zeros((D, B, B, H, VH), np.float32)
    for b in range(B):
        wb[:, b, b] = g[Bp + "Wbeta"].T[:, :, None]
    ar["wbeta"] = wb.reshape(D, B, B * H * VH)
    p = np.arange(128)
    ar["ident"] = np.eye(128, dtype=np.float32)
    ar["ones"] = np.ones((128, 128), np.float32)
    ar["head_sum"] = (p[:, None] // DK == p[None] // DK).astype(np.float32)
    lanes = np.zeros((128, B * HH, B * HH, HPH, VH), np.float32)
    for s in range(B * HH):
        lanes[:, s, s] = (p[:, None] // DK == np.arange(HPH)[None])[:, :, None]
    ar["to_lanes"] = lanes.reshape(128, B * HH, 128)
    q32, c32 = (p % SUB)[:, None], np.arange(SUB)[None]
    ar["edge_mask"] = np.concatenate([np.where(c32 < q32, -BIG, 0), np.where(c32 > q32, -BIG, 0)], 1).astype(np.float32)
    ar["tri_mask"] = np.concatenate([np.where(p[:, None] < p[None], -BIG, 0),
                                     np.where(p[:, None] > p[None], -BIG, 0)], 1).astype(np.float32)
    cols = np.zeros((128, 2), np.float32)
    cols[PADROW, 0] = 1
    cols[MROW:MROW + 3, 1] = 1
    ar["stack_cols"] = cols
    ar["eps"] = np.tile(np.array([[LN_EPS, RMS_EPS, -L2_MIN2, L2_MIN2]], np.float32), (128, 1))
    pad = np.zeros((1, W + T), ml_dtypes.bfloat16)
    pad[:, :W] = -BIG
    ar["pad_row"] = pad
    ar["zero_rows"] = np.zeros((3, HPH, W), ml_dtypes.bfloat16)

    nc = bacc.Bacc("TRN2", target_bir_lowering=False, num_devices=1)
    arrays, aps = {}, {}
    for name, v in ar.items():
        v = np.ascontiguousarray(v)
        arrays[f"in_{name}"] = v
        aps[name] = nc.dram_tensor(f"in_{name}", v.shape, mybir.dt.from_np(v.dtype), kind="ExternalInput").ap()
    aps["out"] = nc.dram_tensor("out_x", (B, T, D), F32, kind="ExternalOutput").ap()
    layer_program(nc, aps)
    r = run_bass_kernel_spmd(nc, [arrays], core_ids=[0])
    return r.results[0]["out_x"]
```

```python
import concourse.bass as bass
from concourse import mybir
from contextlib import ExitStack

F32 = mybir.dt.float32
BF16 = mybir.dt.bfloat16
I32 = mybir.dt.int32
ACT = mybir.ActivationFunctionType
ALU = mybir.AluOpType
AX = mybir.AxisListType

B, T, D = 2, 1024, 256
H, DK = 32, 8
W = 128
NB = T // W
BT = B * W
KT = D // 128
HH = D // 128
HPH = H // HH
FF = 1024
FT = FF // 128
RANK = 16
QBLK = 64
INTER = 704
IT = (INTER + 127) // 128
TAPS = 4
C = 4
NC_ = W // C
VH = 2
VR = DK // VH
PAIRS_K = [(i, j) for i in range(1, C) for j in range(i)]
PAIRS_Q = [(i, j) for i in range(C) for j in range(i + 1)]
NPK, NPQ = len(PAIRS_K), len(PAIRS_Q)
PIECE_PAIRS = [(0, 0), (0, 1), (1, 0), (1, 1), (0, 2), (2, 0)]
SROWS = DK * len(PIECE_PAIRS)
MROW = SROWS
PADROW = SROWS + 3
BIG = 1e30
LOG_EXP_SET = "natural_log_exp_and_others"
LN_EPS, RMS_EPS, L2_MIN2 = 1e-5, 1e-6, 1e-24
HALF = FT // 2
SUB = 32
SPAN = W + SUB
VE = 16
UPG = HPH // 2
NG = B * HH


def layer_program(nc, a):
    with ExitStack() as ctx:
        def sb(name, shape, dt=F32):
            return ctx.enter_context(nc.sbuf_tensor(name, shape, dt))

        def sem(name):
            return ctx.enter_context(nc.semaphore(name))

        q_pieces = nc.dram_tensor("q_pieces", (3, HH, 128, B, W), BF16, kind="Internal").ap()
        k_pieces = nc.dram_tensor("k_pieces", (3, HH, 128, B, W + T), BF16, kind="Internal").ap()
        lane_q = nc.dram_tensor("lane_q", (B, HH, 128, W), F32, kind="Internal").ap()
        lane_k = nc.dram_tensor("lane_k", (B, HH, 128, W), F32, kind="Internal").ap()
        lane_v = nc.dram_tensor("lane_v", (B, HH, 128, W), F32, kind="Internal").ap()
        lane_o = nc.dram_tensor("lane_o", (B, HH, 128, W), F32, kind="Internal").ap()

        ident = sb("ident", [128, 128])
        ones = sb("ones", [128, 128])
        head_sum = sb("head_sum", [128, 128])
        to_lanes = sb("to_lanes", [128, B * HH, 128])
        edge_mask_f = sb("edge_mask_f", [128, 2 * SUB])
        tri_mask_f = sb("tri_mask_f", [128, 2 * W])
        identb = sb("identb", [128, 128], BF16)
        edge_mask = sb("edge_mask", [128, 2 * SUB], BF16)
        tri_mask = sb("tri_mask", [128, 2 * W], BF16)
        stack_cols = sb("stack_cols", [128, 2])
        eps = sb("eps", [128, 6])
        wqkv_a = sb("wqkv_a", [128, KT, 3 * D])
        wo_a = sb("wo_a", [128, KT, D])
        wqkv_b = sb("wqkv_b", [128, KT, 3 * D])
        wbeta = sb("wbeta", [128, KT, B, 128])
        wout_b = sb("wout_b", [128, KT, D])
        wgu = sb("wgu", [128, KT, 2 * INTER])
        wdown_b = sb("wdown_b", [128, IT, D])
        norm_w = sb("norm_w", [128, 3, KT])
        conv_w = sb("conv_w", [128, 3, HH, TAPS])
        w_up = sb("w_up", [128, KT, FF])
        w_dn = sb("w_dn", [128, FT, D])
        b_up = sb("b_up", [128, FT])
        b_dn = sb("b_dn", [128, D])

        x_in = sb("x_in", [128, B, D])
        tok = sb("tok", [128, B, D])
        feat = sb("feat", [128, KT, B, W])
        tok_c = sb("tok_c", [128, B, D])
        feat_c = sb("feat_c", [128, KT, B, W])
        stats = sb("stats", [128, B, 6])
        mv = sb("mv", [128, B, 2])
        lnv = sb("lnv", [128, B])
        rstd = sb("rstd", [128, B])
        sq = sb("sq", [128, D])
        lnt = sb("lnt", [128, B])
        lnt_c = sb("lnt_c", [128, B])
        stats_c = sb("stats_c", [128, B, 6])
        mv_c = sb("mv_c", [128, B, 2])
        lnv_c = sb("lnv_c", [128, B])
        rstd_c = sb("rstd_c", [128, B])
        rs_o = sb("rs_o", [128, BT])
        x1 = x_in
        x2 = sb("x2", [128, B, D])
        z = sb("z", [128, B, D])
        x2_c = sb("x2_c", [128, B, D])
        z_c = sb("z_c", [128, B, D])
        hid = sb("hid", [128, FT, BT])
        hid_c = sb("hid_c", [128, HALF, BT])
        sqk = sb("sqk", [128, 2, HH * BT])
        conv = sb("conv", [128, 3, HH * BT])
        pieces = conv[:].bitcast(BF16).rearrange("p s (a t) -> p (s a) t", a=2).rearrange("p (s j) t -> p s j t", s=2)
        rest = sqk
        q_stack = sb("q_stack", [128, 2, HPH, W], BF16)
        k_stack = sb("k_stack", [128, 2, HPH, 2 * W], BF16)
        v_ext = sb("v_ext", [128, B, 2, H, VE])
        mx = sb("mx", [128, NG, HPH])
        nmx = sb("nmx", [128, NG, HPH])
        mpieces = sb("mpieces", [128, NG, 3, HPH], BF16)
        m_rows = sb("m_rows", [2 * 3 * HPH, NG // 2, W], BF16)
        probs = sb("probs", [128, 2, 2 * 2 * W])
        o_rows = tok_c[:].rearrange("p b d -> p (b d)")
        rden = sb("rden", [128, HPH])
        raw = sb("raw", [128, 3, HH, B, TAPS - 1 + W])
        prodk = hid[:].rearrange("p a b -> p (a b)").rearrange("p (h b q c) -> p h b q c", h=HH, b=B, q=NPK + NPQ)
        beta_l = sb("beta_l", [128, W])
        k_l = sb("k_l", [128, DK, W])
        q_l = sb("q_l", [128, DK, W])
        v_l = sb("v_l", [128, VR, W])
        tm = sb("tm", [128, NC_, C, C])
        mm_ = sb("mm_", [128, C, C, NC_])
        tmp_t = sb("tmp_t", [128, NC_, C])
        k_til = sb("k_til", [128, NC_, C, DK])
        tmp_k = prodk.rearrange("p h b q c -> p (h b q c)")[:, 0:NC_ * C * DK].rearrange("p (c i k) -> p c i k", i=C, k=DK)
        lane_buf = sb("lane_buf", [128, NC_ * VR * C * (DK + 1)])
        first = lane_buf[:].rearrange("p (c v i k) -> p c v i k", v=VR, i=C, k=DK + 1)
        tmp_v = sb("tmp_v", [128, NC_, VR, C])
        u_l = sb("u_l", [128, NC_, VR, C])
        pair_l = u_l[:].rearrange("p c v i -> p (c v i)").rearrange("p (a c) -> p a c", c=NC_)
        state = sb("state", [128, NC_ + 1, VR, DK, C + 1])
        out_terms = lane_buf[:, 0:VR * W // 2 * (DK + C)].rearrange("p (v c i e) -> p v c i e", v=VR, i=C, e=DK + C)
        o_l = k_l[:].rearrange("p k t -> p (k t)")[:, 0:VR * W].rearrange("p (v c i) -> p v c i", v=VR, i=C)
        o_t = q_l[:, 0:DK // 2].rearrange("p k t -> p (k t)").rearrange("p (h b t) -> p h b t", h=HH, b=B)
        o_n = q_l[:, DK // 2:DK].rearrange("p k t -> p (k t)").rearrange("p (h b t) -> p h b t", h=HH, b=B)
        gate = probs[:, 0].rearrange("p (i t) -> p i t", i=2)

        bank = [ctx.enter_context(nc.psum_tensor(f"bank{i}", [128, 512], F32)) for i in range(8)]
        bank_b = bank[0][:, :].bitcast(BF16)

        consts_in = sem("consts_in")
        weights_in = sem("weights_in")
        quant_in = sem("quant_in")
        lora_in = sem("lora_in")
        lora_prod = sem("lora_prod")
        lora_added = sem("lora_added")
        consts_cast = sem("consts_cast")
        weights_scaled = sem("weights_scaled")
        zeroed = sem("zeroed")
        pad_out = sem("pad_out")
        x_loaded = sem("x_loaded")
        x_used = sem("x_used")
        vstep = sem("vstep")
        astep = sem("astep")
        gstep = sem("gstep")
        vars_ready = sem("vars_ready")
        rstd_ready = sem("rstd_ready")
        tok_ready = sem("tok_ready")
        turned = sem("turned")
        feat_ready = sem("feat_ready")
        qkv_done = sem("qkv_done")
        piece1 = sem("piece1")
        rest1 = sem("rest1")
        piece2 = sem("piece2")
        piece3 = sem("piece3")
        v_done = sem("v_done")
        pieces_out = sem("pieces_out")
        stacks_in = [sem("stacks_in0"), sem("stacks_in1")]
        stack_init = sem("stack_init")
        sq_rstd = sem("sq_rstd")
        scores1 = sem("scores1")
        max_done = sem("max_done")
        mpieces_ready = sem("mpieces_ready")
        m_turned = sem("m_turned")
        m_copied = sem("m_copied")
        m_in = [sem("m_in0"), sem("m_in1")]
        scores2 = sem("scores2")
        exp_done = sem("exp_done")
        pv_done = sem("pv_done")
        o_copied = sem("o_copied")
        o_turned = sem("o_turned")
        o_scaled = sem("o_scaled")
        wo_done = sem("wo_done")
        x1_ready = sem("x1_ready")
        x1b_ready = sem("x1b_ready")
        hid_done = sem("hid_done")
        hid_ready = sem("hid_ready")
        ffn_done = sem("ffn_done")
        x2_ready = sem("x2_ready")
        z_ready = sem("z_ready")
        projb_done = sem("projb_done")
        raw_ready = sem("raw_ready")
        beta_ready = sem("beta_ready")
        beta_exp = sem("beta_exp")
        conv_ready = sem("conv_ready")
        silu_ready = sem("silu_ready")
        sq_ready = sem("sq_ready")
        ss_done = sem("ss_done")
        rn_ready = sem("rn_ready")
        unit_ready = sem("unit_ready")
        prod_ready = sem("prod_ready")
        pairs_done = sem("pairs_done")
        pairs_copied = sem("pairs_copied")
        lanes_out = sem("lanes_out")
        lanes_in = sem("lanes_in")
        tm_ready = sem("tm_ready")
        til_ready = sem("til_ready")
        held = sem("held")
        scanned = sem("scanned")
        terms_ready = sem("terms_ready")
        o_ready = sem("o_ready")
        o_out = sem("o_out")
        o_in = sem("o_in")
        osq_ready = sem("osq_ready")
        oss_done = sem("oss_done")
        ors_ready = sem("ors_ready")
        on_ready = sem("on_ready")
        wout_done = sem("wout_done")
        y_ready = sem("y_ready")
        xy_ready = sem("xy_ready")
        var_c_ready = sem("var_c_ready")
        rstd_c_ready = sem("rstd_c_ready")
        tok_c_ready = sem("tok_c_ready")
        turned_c = sem("turned_c")
        feat_c_ready = sem("feat_c_ready")
        gu_done = sem("gu_done")
        gate_ready = sem("gate_ready")
        act_ready = sem("act_ready")
        mlp_half = sem("mlp_half")
        mlp_done = sem("mlp_done")
        x3_ready = sem("x3_ready")
        x3b_ready = sem("x3b_ready")
        hid_c_done = sem("hid_c_done")
        hid_c_ready = sem("hid_c_ready")
        ffn_c_half = sem("ffn_c_half")
        ffn_c_done = sem("ffn_c_done")
        out_ready = sem("out_ready")
        out_stored = sem("out_stored")

        inner = [(i, min(128, INTER - 128 * i)) for i in range(IT)]
        N_UNITS = B * H // 2
        STACK_DMAS = 2 * len(PIECE_PAIRS) + 2
        x_v = a["x"].rearrange("b (n p) d -> n p b d", p=W)
        out_v = a["out"].rearrange("b (n p) d -> n p b d", p=W)

        plain = [
            (wqkv_a[:], a["wqkv_a"].rearrange("(k p) n -> p k n", p=128)),
            (wo_a[:], a["wo_a"].rearrange("(k p) n -> p k n", p=128)),
            (b_up[:], a["b_up"]),
            (b_dn[:], a["b_dn"].broadcast_to([128, D])),
            (conv_w[:], a["conv_w"]),
            (wqkv_b[:], a["wqkv_b"].rearrange("(k p) n -> p k n", p=128)),
            (wbeta[:], a["wbeta"].rearrange("(k p) b n -> p k b n", p=128)),
            (norm_w[:], a["norm_w"]),
            (wout_b[:], a["wout_b"].rearrange("(k p) n -> p k n", p=128)),
            (wgu[:], a["wgu"].rearrange("(k p) n -> p k n", p=128)),
        ]
        consts = [(ident[:], a["ident"]), (ones[:], a["ones"]), (head_sum[:], a["head_sum"]),
                  (to_lanes[:], a["to_lanes"]), (edge_mask_f[:], a["edge_mask"]),
                  (tri_mask_f[:], a["tri_mask"]), (stack_cols[:], a["stack_cols"]), (eps[:], a["eps"])]
        q_up = k_stack[:, 0].rearrange("p a b -> p (a b)").bitcast(I32)
        q_dn = k_stack[:, 1].rearrange("p a b -> p (a b)").bitcast(I32)
        s_up = lane_buf[:, 0:KT * FF]
        s_dn = lane_buf[:, KT * FF:KT * FF + FT * D]
        lora_a_up = sqk[0:RANK, 0, 0:D]
        lora_b_dn = sqk[0:RANK, 0, D:2 * D]
        lora_b_up = hid[0:RANK, 0:4, :].rearrange("p a b -> p (a b)")
        lora_a_dn = hid[0:RANK, 4:8, :].rearrange("p a b -> p (a b)")

        block = ctx.enter_context(nc.Block())

        def terms_of(engine, cs):
            qc = q_l[:].rearrange("p k (c i) -> p i c k", i=C)
            n_c = cs.stop - cs.start
            for i in range(C):
                for v in range(VR):
                    engine.tensor_tensor(out_terms[:, v, :, i, 0:DK], state[:, cs, v, :, C], qc[:, i, cs, :], ALU.mult)
                last = engine.tensor_tensor(
                    out_terms[:, :, :, i, DK:DK + C],
                    mm_[:, i, :, cs].rearrange("p j (o c) -> p o c j", o=1).broadcast_to([128, VR, n_c, C]),
                    u_l[:, cs].rearrange("p c v j -> p v c j"), ALU.mult)
            return last

        @block.sync
        def _(sp):
            for dst, src in consts:
                sp.dma_start(dst, src).then_inc(consts_in, 16)
            sp.dma_start(q_up.rearrange("p (k n) -> p k n", k=KT),
                         a["q_up"].rearrange("(k p) n -> p k n", p=128)).then_inc(quant_in, 16)
            sp.dma_start(q_dn.rearrange("p (k n) -> p k n", k=FT),
                         a["q_dn"].rearrange("(k p) n -> p k n", p=128)).then_inc(quant_in, 16)
            for half in range(128 // QBLK):
                rows = slice(half * QBLK, (half + 1) * QBLK)
                for k in range(KT):
                    sp.dma_start(s_up[rows, k * FF:(k + 1) * FF],
                                 a["s_up"][2 * k + half:2 * k + half + 1, :].broadcast_to([QBLK, FF])
                                 ).then_inc(quant_in, 16)
                for k in range(FT):
                    sp.dma_start(s_dn[rows, k * D:(k + 1) * D],
                                 a["s_dn"][2 * k + half:2 * k + half + 1, :].broadcast_to([QBLK, D])
                                 ).then_inc(quant_in, 16)
            for dst, src in [(lora_a_up, a["lora_a_up"]), (lora_b_dn, a["lora_b_dn"]),
                             (lora_b_up, a["lora_b_up"]), (lora_a_dn, a["lora_a_dn"])]:
                sp.dma_start(dst, src).then_inc(lora_in, 16)
            sp.wait_ge(zeroed, 1)
            for p in range(3):
                for hh in range(HH):
                    sp.dma_start(k_pieces[p, hh, :, :, 0:W],
                                 q_stack[:, 0, 0:B, :]).then_inc(pad_out, 16)
            sp.wait_ge(pad_out, 16 * 3 * HH)
            sp.wait_ge(stack_init, 2)

            def load_x(n):
                sp.wait_ge(x_used, n + 1)
                sp.dma_start(x_in[:], x_v[bass.ds(n, 1)].rearrange("n p b d -> (n p) b d")).then_inc(x_loaded, 16)

            def load_stacks(n, g):
                b, hh = divmod(g, HH)
                for r, (i, j) in enumerate(PIECE_PAIRS):
                    rows = slice(r * DK, (r + 1) * DK)
                    sp.dma_start(q_stack[rows, g % 2], q_pieces[i, hh, :, b, :].rearrange(
                        "(h d) t -> d h t", d=DK)).then_inc(stacks_in[g % 2], 16)
                    sp.dma_start(k_stack[rows, g % 2], k_pieces[j, hh, :, b, bass.ds(n * W, 2 * W)].rearrange(
                        "(h d) t -> d h t", d=DK)).then_inc(stacks_in[g % 2], 16)
                sp.dma_start(q_stack[MROW:MROW + 3, g % 2], a["zero_rows"]).then_inc(stacks_in[g % 2], 16)
                sp.dma_start(k_stack[PADROW:PADROW + 1, g % 2],
                             a["pad_row"][:, bass.ds(n * W, 2 * W)].rearrange("a (o t) -> a o t", o=1)
                             .broadcast_to([1, HPH, 2 * W])).then_inc(stacks_in[g % 2], 16)

            def stack_front(n):
                sp.wait_ge(piece3, n * 2 + 2)
                for p in range(3):
                    sp.dma_start(q_pieces[p].rearrange("h p b t -> p h b t"),
                                 pieces[:, 0, p, :].rearrange("p (h b t) -> p h b t", h=HH, b=B)
                                 ).then_inc(pieces_out, 16)
                    for hh in range(HH):
                        sp.dma_start(k_pieces[p, hh, :, :, bass.ds(n * W + W, W)],
                                     pieces[:, 1, p, hh * BT:(hh + 1) * BT].rearrange("p (b t) -> p b t", b=B)
                                     ).then_inc(pieces_out, 16)
                sp.wait_ge(pieces_out, n * 144 + 144)
                for g in range(2):
                    load_stacks(n, g)

            def load_max(n, g):
                sp.wait_ge(m_copied, n * (NG // 2) + g // 2 + 1)
                for j in range(3):
                    sp.dma_start(q_stack[MROW + j:MROW + j + 1, g % 2],
                                 m_rows[((g % 2) * 3 + j) * HPH:((g % 2) * 3 + j + 1) * HPH, g // 2, :]
                                 ).then_inc(m_in[g % 2], 16)

            def attention(n):
                for g in range(2):
                    load_max(n, g)
                for g in range(2, NG):
                    sp.wait_ge(scores2, n * N_UNITS + (g - 1) * UPG)
                    load_stacks(n, g)
                for g in range(2, NG):
                    load_max(n, g)

            def outputs_turn(n):
                sp.wait_ge(o_ready, n + 1)
                sp.dma_start(lane_o.rearrange("b hh (h v) t -> (b hh h) (v t)", v=VR),
                             o_l.rearrange("p v c i -> p (v c i)")).then_inc(o_out, 16)
                sp.wait_ge(o_out, n * 16 + 16)
                for hh in range(HH):
                    sp.dma_start(o_t[:, hh], lane_o[:, hh].rearrange("b p t -> p b t")).then_inc(o_in, 16)

            def to_lanes_dma(n, after_c):
                sp.wait_ge(unit_ready, n * 2 + 2)
                sp.wait_ge(silu_ready, n * 3 + 3)
                for s, dst in enumerate((lane_q, lane_k, lane_v)):
                    for hh in range(HH):
                        sp.dma_start(dst[:, hh].rearrange("b p t -> p b t"),
                                     conv[:, s, hh * BT:(hh + 1) * BT].rearrange("p (b t) -> p b t", b=B)
                                     ).then_inc(lanes_out, 16)
                sp.wait_ge(lanes_out, n * 96 + 96)
                if after_c:
                    sp.wait_ge(wout_done, n)
                for src, dst in ((lane_q, q_l), (lane_k, k_l)):
                    sp.dma_start(dst[:].rearrange("p k t -> p (k t)"),
                                 src.rearrange("b hh (h o d) t -> (b hh h) o (d t)", o=1, d=DK)
                                 .broadcast_to([B * H, VH, DK * W])).then_inc(lanes_in, 16)
                sp.dma_start(v_l[:].rearrange("p k t -> p (k t)"),
                             lane_v.rearrange("b hh (h v) t -> (b hh h) (v t)", v=VR)).then_inc(lanes_in, 16)

            def body(t, scan=True, following=True, front=True):
                if following:
                    attention(t + 1)
                if scan:
                    outputs_turn(t)
                if front:
                    load_x(t + 2)
                if following:
                    to_lanes_dma(t + 1, scan)
                if front:
                    stack_front(t + 2)
                if scan:
                    sp.wait_ge(out_ready, t + 1)
                    sp.dma_start(out_v[bass.ds(t, 1)].rearrange("n p b d -> (n p) b d"), z_c[:]
                                 ).then_inc(out_stored, 16)

            load_x(0)
            stack_front(0)
            body(-1, scan=False)
            with sp.Fori(0, NB - 2) as t:
                body(t)
            body(NB - 2, front=False)
            body(NB - 1, following=False, front=False)
            sp.wait_ge(out_stored, 16 * NB + 16)

        @block.gpsimd
        def _(pool):
            pool.memset(q_stack[:], 0.0).then_inc(zeroed, 1)
            pool.memset(v_ext[:], 0.0).then_inc(gstep, 1)
            pool.wait_ge(gstep, 1)
            pool.memset(v_ext[:, :, :, :, DK:DK + 1], 1.0).then_inc(zeroed, 1)
            pool.memset(raw[:], 0.0).then_inc(zeroed, 1)
            pool.memset(tm[:], 0.0).then_inc(zeroed, 1)
            pool.memset(mm_[:], 0.0).then_inc(zeroed, 1)
            pool.memset(state[:], 0.0).then_inc(zeroed, 1)
            pool.sem_clear(gstep)

            steps = 0

            def done(ins):
                nonlocal steps
                steps += 1
                ins.then_inc(gstep, 1)
                pool.wait_ge(gstep, steps)

            def first_terms(n):
                pool.wait_ge(scanned, n + 1)
                terms_of(pool, slice(0, NC_ // 2)).then_inc(terms_ready, 1)

            def ffn_bias(n):
                pool.wait_ge(x1_ready, n + 1)
                pool.wait_ge(tok_ready, n * 4 + 3)
                for b in range(B):
                    last = pool.tensor_tensor(x1[:, b], x1[:, b], b_dn[:], ALU.add)
                last.then_inc(x1b_ready, 1)

            def residual(n):
                pool.wait_ge(y_ready, n + 1)
                pool.tensor_tensor(x2_c[:], x2_c[:], z_c[:], ALU.add).then_inc(xy_ready, 1)

            def ffn_bias_c(n):
                pool.wait_ge(tok_c_ready, n * 2 + 2)
                for b in range(B):
                    last = pool.tensor_tensor(z_c[:, b], z_c[:, b], b_dn[:], ALU.add)
                last.then_inc(x3b_ready, 1)

            def til(n):
                pool.wait_ge(tm_ready, n + 1)
                pool.wait_ge(lanes_in, n * 48 + 48)
                kc = k_l[:].rearrange("p k (c i) -> p c i k", i=C)
                vc = v_l[:].rearrange("p v (c i) -> p c v i", i=C)
                for j in range(C):
                    rows = C - j
                    for i in range(j, C):
                        last = pool.tensor_tensor(
                            (k_til if j == 0 else tmp_k)[:, :, i, :],
                            tm[:, :, i, j:j + 1].broadcast_to([128, NC_, DK]), kc[:, :, j, :], ALU.mult)
                    done(last)
                    if j:
                        done(pool.tensor_tensor(k_til[:, :, j:C, :], k_til[:, :, j:C, :],
                                                tmp_k[:, :, j:C, :], ALU.add))
                for j in range(C):
                    for i in range(j, C):
                        dst = first[:, :, :, i, DK] if j == 0 else tmp_v[:, :, :, i]
                        last = pool.tensor_tensor(dst, tm[:, :, i, j:j + 1].broadcast_to([128, NC_, VR]),
                                                  vc[:, :, :, j], ALU.mult)
                    if j:
                        done(last)
                        last = pool.tensor_tensor(first[:, :, :, j:C, DK], first[:, :, :, j:C, DK],
                                                  tmp_v[:, :, :, j:C], ALU.add)
                    done(last)
                pool.nop().then_inc(til_ready, 1)

            def body(t, scan=True, following=True):
                nonlocal steps
                steps = 0
                if scan:
                    first_terms(t)
                if following:
                    ffn_bias(t + 1)
                if scan:
                    residual(t)
                    ffn_bias_c(t)
                if following:
                    til(t + 1)
                pool.sem_clear(gstep)

            body(-1, scan=False)
            with pool.Fori(0, NB - 2) as t:
                body(t)
            body(NB - 2)
            body(NB - 1, following=False)

        @block.scalar
        def _(act):
            for dst, src in plain:
                act.dma_start(dst, src).then_inc(weights_in, 16)
            for i, m in inner:
                act.dma_start(wdown_b[0:m, i, :], a["wdown_b"][128 * i:128 * i + m, :]).then_inc(weights_in, 16)

            steps = 0

            def done(ins):
                nonlocal steps
                steps += 1
                ins.then_inc(astep, 1)
                act.wait_ge(astep, steps)

            def rsqrt(dst, src, tmp, e, scale):
                done(act.activation(tmp, src, ACT.Ln, bias=eps[:, e:e + 1], scale=scale))
                return act.activation(dst, tmp, ACT.Exp, scale=-0.5)

            def norm_a(n, k):
                act.wait_ge(vars_ready, n * 3 + k)
                rsqrt(rstd[:], mv[:, :, 1], lnv[:], 0, 1.0).then_inc(rstd_ready, 1)

            def turn_a(n, k):
                act.wait_ge(turned, n * 4 + k)
                act.copy(feat[:].rearrange("p k b t -> p (k b t)"), bank[0][:]).then_inc(feat_ready, 1)

            def turn_c(n, k):
                act.wait_ge(turned_c, n * 2 + k)
                act.copy(feat_c[:].rearrange("p k b t -> p (k b t)"), bank[7][:]).then_inc(feat_c_ready, 1)

            def hold(n):
                act.wait_ge(z_ready, n + 1)
                act.wait_ge(out_stored, n * 16 + 16)
                act.copy(z_c[:], z[:])
                act.copy(x2_c[:], x2[:]).then_inc(held, 1)

            def piece_first(n, after_p):
                for s in range(2):
                    act.wait_ge(qkv_done, n * 3 + s + 1)
                    if after_p and s == 0:
                        act.wait_ge(lanes_out, n * 96)
                        act.wait_ge(prod_ready, n)
                    act.copy(pieces[:, s, 0], bank[1 + s][:]).then_inc(piece1, 1)

            def piece_second(n):
                for s in range(2):
                    act.wait_ge(rest1, n * 2 + s + 1)
                    act.copy(pieces[:, s, 1], rest[:, s]).then_inc(piece2, 1)

            def values_out(n):
                act.wait_ge(qkv_done, n * 3 + 3)
                for b in range(B):
                    last = act.copy(v_ext[:, b, 1, :, 0:DK],
                                    bank[3][:, b * D:(b + 1) * D].rearrange("p (h d) -> p h d", d=DK))
                last.then_inc(v_done, 1)

            def attention(n):
                for pair in range(NG // 2):
                    act.wait_ge(m_turned, n * (NG // 2) + pair + 1)
                    act.copy(m_rows[:, pair], bank_b[0:6 * HPH, 0:W]).then_inc(m_copied, 1)
                    for g in (2 * pair, 2 * pair + 1):
                        for u in range(g * UPG, (g + 1) * UPG):
                            act.wait_ge(scores2, n * N_UNITS + u + 1)
                            act.activation(probs[:, u % 2], bank[3 + u % 2][:], ACT.Exp,
                                           scale=float(DK) ** -0.5).then_inc(exp_done, 1)
                        act.wait_ge(pv_done, n * NG + g + 1)
                        if g:
                            act.wait_ge(o_turned, n * NG + g)
                        act.copy(o_rows, bank[5][:]).then_inc(o_copied, 1)
                done(act.copy(v_ext[:, :, 0, :, 0:DK], v_ext[:, :, 1, :, 0:DK]))
                turn_a(n, 2)

            def ffn(n, after_p):
                norm_a(n, 2)
                turn_a(n, 3)
                if after_p:
                    act.wait_ge(til_ready, n)
                for i in range(FT):
                    act.wait_ge(hid_done, n * FT + i + 1)
                    act.activation(hid[:, i, :], bank[1 + i % 2][:, 0:BT], ACT.Relu,
                                   bias=b_up[:, i:i + 1]).then_inc(hid_ready, 1)

            def norms_z(n):
                norm_a(n, 3)
                act.wait_ge(z_ready, n + 1)
                for b in range(B):
                    done(act.activation(sq[:], z[:, b], ACT.Square, accum_out=lnv[:, b:b + 1]))
                rsqrt(rstd[:], lnv[:], lnt[:], 1, 1.0 / D).then_inc(sq_rstd, 1)

            def beta_exp_of(n):
                act.wait_ge(projb_done, n * 4 + 1)
                act.activation(beta_l[:], bank[4][:, 0:W], ACT.Exp, scale=-1.0).then_inc(beta_exp, 1)

            def raw_of(n):
                for s in range(3):
                    act.wait_ge(projb_done, n * 4 + s + 2)
                    for hh in range(HH):
                        last = act.copy(raw[:, s, hh, :, TAPS - 1:],
                                        bank[1 + s][:, hh * BT:(hh + 1) * BT].rearrange("p (b t) -> p b t", b=B))
                    last.then_inc(raw_ready, 1)

            def silu_twice(n, s):
                act.wait_ge(conv_ready, n * 3 + s + 1)
                done(act.activation(conv[:, s], conv[:, s], ACT.Silu))
                act.activation(conv[:, s], conv[:, s], ACT.Silu).then_inc(silu_ready, 1)
                if s < 2:
                    act.wait_ge(silu_ready, n * 3 + s + 1)
                    act.activation(sqk[:, s], conv[:, s], ACT.Square).then_inc(sq_ready, 1)

            def l2_norms(n):
                for s in range(2):
                    act.wait_ge(ss_done, n * 2 + s + 1)
                    done(act.activation(sqk[:, s], bank[1 + s][:], ACT.Relu, bias=eps[:, 2:3]))
                    done(act.activation(sqk[:, s], sqk[:, s], ACT.Ln, bias=eps[:, 3:4]))
                    act.activation(sqk[:, s], sqk[:, s], ACT.Exp, scale=-0.5).then_inc(rn_ready, 1)

            def pairs_out(n):
                act.wait_ge(pairs_done, n + 1)
                act.copy(pair_l.rearrange("p a c -> p (a c)"), bank[3][:]).then_inc(pairs_copied, 1)

            def output_norm(n):
                act.wait_ge(o_in, n * 32 + 32)
                act.activation(o_n, o_t, ACT.Square).then_inc(osq_ready, 1)
                act.wait_ge(oss_done, n + 1)
                rsqrt(rs_o[:], bank[6][:, 0:BT], rs_o[:], 1, 1.0 / D).then_inc(ors_ready, 1)

            def y_norm(n):
                act.wait_ge(y_ready, n + 1)
                for b in range(B):
                    done(act.activation(sq[:], z_c[:, b], ACT.Square, accum_out=lnv_c[:, b:b + 1]))
                rsqrt(rstd_c[:], lnv_c[:], lnt_c[:], 1, 1.0 / D).then_inc(rstd_c_ready, 1)

            def gate_of(n, i):
                m = inner[i][1]
                act.wait_ge(gu_done, n * IT + i + 1)
                if i >= 2:
                    act.wait_ge(act_ready, n * IT + i - 1)
                act.activation(gate[0:m, i % 2], bank[6 + i % 2][0:m, 0:BT], ACT.Silu).then_inc(gate_ready, 1)

            def norm_c(n):
                act.wait_ge(var_c_ready, n + 1)
                rsqrt(rstd_c[:], mv_c[:, :, 1], lnv_c[:], 0, 1.0).then_inc(rstd_c_ready, 1)

            def ffn_c(n, lo, hi):
                for i in range(lo, hi):
                    act.wait_ge(hid_c_done, n * FT + i + 1)
                    if i == HALF:
                        act.wait_ge(ffn_c_half, n + 1)
                    act.activation(hid_c[:, i % HALF, :], bank[6 + i % 2][:, 0:BT], ACT.Relu,
                                   bias=b_up[:, i:i + 1]).then_inc(hid_c_ready, 1)

            def body(t, scan=True, following=True, front=True):
                nonlocal steps
                steps = 0
                n = t + 1
                if scan:
                    hold(t)
                if following:
                    attention(n)
                    ffn(n, scan)
                if scan:
                    output_norm(t)
                    y_norm(t)
                    turn_c(t, 1)
                if following:
                    norms_z(n)
                    turn_a(n, 4)
                    beta_exp_of(n)
                if scan:
                    gate_of(t, 0)
                    gate_of(t, 1)
                if following:
                    raw_of(n)
                    silu_twice(n, 0)
                if scan:
                    gate_of(t, 2)
                    gate_of(t, 3)
                if following:
                    silu_twice(n, 1)
                if scan:
                    gate_of(t, 4)
                    gate_of(t, 5)
                if following:
                    silu_twice(n, 2)
                nc.scalar.preload_act_table_set(LOG_EXP_SET)
                if following:
                    l2_norms(n)
                if front:
                    norm_a(t + 2, 1)
                    turn_a(t + 2, 1)
                if scan:
                    norm_c(t)
                if following:
                    pairs_out(n)
                if front:
                    piece_first(t + 2, True)
                if scan:
                    turn_c(t, 2)
                if front:
                    values_out(t + 2)
                if scan:
                    ffn_c(t, 0, 4)
                if front:
                    piece_second(t + 2)
                if scan:
                    ffn_c(t, 4, FT)
                act.sem_clear(astep)

            act.wait_ge(consts_in, 16 * len(consts))
            act.wait_ge(weights_in, 16 * (len(plain) + IT))
            nc.scalar.preload_act_table_set(LOG_EXP_SET)
            norm_a(0, 1)
            turn_a(0, 1)
            piece_first(0, False)
            values_out(0)
            piece_second(0)
            act.sem_clear(astep)
            body(-1, scan=False)
            with act.Fori(0, NB - 2) as t:
                body(t)
            body(NB - 2, front=False)
            body(NB - 1, following=False, front=False)

        @block.vector
        def _(dve):
            dve.wait_ge(consts_in, 16 * len(consts))
            dve.tensor_copy(identb[:], ident[:])
            dve.tensor_copy(edge_mask[:], edge_mask_f[:])
            dve.tensor_copy(tri_mask[:], tri_mask_f[:]).then_inc(consts_cast, 1)
            dve.wait_ge(quant_in, 16 * (2 + 2 * (KT + FT)))
            dve.scalar_tensor_tensor(out=w_up[:].rearrange("p k n -> p (k n)"), in0=q_up, scalar=-7.5,
                                     in1=s_up, op0=ALU.add, op1=ALU.mult)
            dve.scalar_tensor_tensor(out=w_dn[:].rearrange("p k n -> p (k n)"), in0=q_dn, scalar=-7.5,
                                     in1=s_dn, op0=ALU.add, op1=ALU.mult).then_inc(vstep, 1)
            dve.wait_ge(vstep, 1)
            dve.wait_ge(lora_prod, 1)
            for k in range(KT):
                for c in range(2):
                    w = w_up[:, k, c * 512:(c + 1) * 512]
                    dve.tensor_tensor(w, w, bank[2 * k + c][:], ALU.add)
            for k in range(FT // 2):
                w = w_dn[:, 2 * k:2 * k + 2, :].rearrange("p a n -> p (a n)")
                dve.tensor_tensor(w, w, bank[4 + k][:], ALU.add).then_inc(lora_added, 1)
            dve.wait_ge(weights_in, 16 * (len(plain) + IT))
            for k in range(KT):
                for w, i in ((wqkv_b[:, k], 0), (wbeta[:, k], 0), (wout_b[:, k], 1), (wgu[:, k], 2)):
                    last = dve.tensor_scalar(w, w, norm_w[:, i, k:k + 1], None, ALU.mult)
            last.then_inc(weights_scaled, 1)
            dve.wait_ge(zeroed, 6)
            dve.wait_ge(pad_out, 16 * 3 * HH)
            dve.tensor_scalar(q_stack[:], q_stack[:], stack_cols[:, 0:1], None, ALU.add).then_inc(stack_init, 1)
            dve.memset(k_stack[:], 0.0).then_inc(vstep, 1)
            dve.wait_ge(vstep, 2)
            dve.tensor_scalar(k_stack[:], k_stack[:], stack_cols[:, 1:2], None, ALU.add).then_inc(stack_init, 1)
            dve.sem_clear(vstep)
            dve.nop().then_inc(x_used, 1)
            dve.nop().then_inc(out_stored, 16)

            steps = 0

            def mark(ins):
                nonlocal steps
                steps += 1
                ins.then_inc(vstep, 1)
                return steps

            def done(ins):
                dve.wait_ge(vstep, mark(ins))

            def flat(x):
                return x[:].rearrange("p b d -> p (b d)")

            def normalise(src, dst, st, m_v, rs, ready, rs_sem, rs_count):
                for b in range(B):
                    last = dve.bn_stats(st[:, b], src[:, b])
                done(last)
                for b in range(B):
                    last = dve.bn_aggr(m_v[:, b], st[:, b])
                last.then_inc(ready, 1)
                dve.wait_ge(rs_sem, rs_count)
                for b in range(B):
                    last = dve.tensor_scalar(dst[:, b], src[:, b], m_v[:, b, 0:1], rs[:, b:b + 1],
                                             ALU.subtract, ALU.mult)
                return last

            def norm_in(n):
                dve.wait_ge(x_loaded, n * 16 + 16)
                normalise(x_in, tok, stats, mv, rstd, vars_ready, rstd_ready, n * 3 + 1).then_inc(tok_ready, 1)

            def rests_first(n):
                for s in range(2):
                    dve.wait_ge(piece1, n * 2 + s + 1)
                    dve.tensor_tensor(rest[:, s], bank[1 + s][:], pieces[:, s, 0], ALU.subtract).then_inc(rest1, 1)

            def rests_second(n):
                for s in range(2):
                    dve.wait_ge(piece2, n * 2 + s + 1)
                    dve.tensor_tensor(pieces[:, s, 2], rest[:, s], pieces[:, s, 1], ALU.subtract).then_inc(piece3, 1)

            def max_unit(n, u):
                g, v = divmod(u, UPG)
                dve.wait_ge(scores1, n * N_UNITS + u + 1)
                dve.tensor_reduce(mx[:, g, 2 * v:2 * v + 2],
                                  bank[1 + u % 2][:, 0:2 * SPAN].rearrange("p (h k) -> p h k", h=2),
                                  AX.X, ALU.max).then_inc(max_done, 1)

            def max_piece(n, pair, step, before):
                gs = slice(2 * pair, 2 * pair + 2)
                nm = nmx[:, gs]
                if step == 0:
                    dve.wait_ge(max_done, n * N_UNITS + (2 * pair + 2) * UPG)
                    return mark(dve.tensor_scalar(nm, mx[:, gs], -1.0, None, ALU.mult))
                dve.wait_ge(vstep, before)
                if step == 1:
                    return mark(dve.tensor_copy(mpieces[:, gs, 0], nm))
                if step == 2:
                    return mark(dve.tensor_tensor(nm, nm, mpieces[:, gs, 0], ALU.subtract))
                if step == 3:
                    return mark(dve.tensor_copy(mpieces[:, gs, 1], nm))
                dve.tensor_tensor(mpieces[:, gs, 2], nm, mpieces[:, gs, 1], ALU.subtract).then_inc(mpieces_ready, 1)
                return None

            def out_scale(n, g):
                b, hh = divmod(g, HH)
                dve.wait_ge(o_turned, n * NG + g + 1)
                ov = bank[0][:].rearrange("p (h e) -> p h e", e=32)
                done(dve.reciprocal(rden[:], ov[:, :, DK]))
                dve.tensor_tensor(
                    tok[:, b, hh * 128:(hh + 1) * 128].rearrange("p (h d) -> p h d", d=DK), ov[:, :, 0:DK],
                    rden[:].rearrange("p (h o) -> p h o", o=1).broadcast_to([128, HPH, DK]),
                    ALU.mult).then_inc(o_scaled, 1)

            def first_residual(n):
                dve.wait_ge(wo_done, n + 1)
                done(dve.tensor_tensor(flat(x1), bank[1][:], flat(x_in), ALU.add))
                dve.nop().then_inc(x1_ready, 1)
                normalise(x1, tok, stats, mv, rstd, vars_ready, rstd_ready, n * 3 + 2).then_inc(tok_ready, 1)

            def second_residual(n, after_p):
                dve.wait_ge(ffn_done, n + 1)
                dve.wait_ge(x1b_ready, n + 1)
                if after_p:
                    dve.wait_ge(held, n)
                done(dve.tensor_tensor(flat(x2), bank[3][:], flat(x1), ALU.add))
                dve.nop().then_inc(x_used, 1)
                normalise(x2, z, stats, mv, rstd, vars_ready, rstd_ready, n * 3 + 3).then_inc(z_ready, 1)
                dve.wait_ge(sq_rstd, n + 1)
                for b in range(B):
                    last = dve.tensor_scalar(tok[:, b], z[:, b], rstd[:, b:b + 1], None, ALU.mult)
                last.then_inc(tok_ready, 1)

            def convolve(n, s):
                dve.wait_ge(raw_ready, n * 3 + s + 1)
                for tap in range(TAPS):
                    for hh in range(HH):
                        src = raw[:, s, hh, :, tap:tap + W]
                        dst = conv[:, s, hh * BT:(hh + 1) * BT].rearrange("p (b t) -> p b t", b=B)
                        w = conv_w[:, s, hh, tap:tap + 1]
                        if tap == 0:
                            last = dve.tensor_scalar(dst, src, w, None, ALU.mult)
                        else:
                            last = dve.scalar_tensor_tensor(out=dst, in0=src, scalar=w, in1=dst,
                                                            op0=ALU.mult, op1=ALU.add)
                    if tap < TAPS - 1:
                        done(last)
                last.then_inc(conv_ready, 1)

            def keep_taps():
                dve.tensor_copy(raw[:, :, :, :, 0:TAPS - 1].rearrange("p s h b t -> p (s h b) t"),
                                raw[:, :, :, :, W:W + TAPS - 1].rearrange("p s h b t -> p (s h b) t"))

            def beta_of(n):
                dve.wait_ge(beta_exp, n + 1)
                done(dve.tensor_scalar(beta_l[:], beta_l[:], 1.0, None, ALU.add))
                dve.reciprocal(beta_l[:], beta_l[:]).then_inc(beta_ready, 1)

            def units(n):
                for s in range(2):
                    dve.wait_ge(rn_ready, n * 2 + s + 1)
                    dve.tensor_tensor(conv[:, s], conv[:, s], sqk[:, s], ALU.mult).then_inc(unit_ready, 1)

            def products(n):
                dve.wait_ge(unit_ready, n * 2 + 2)
                for hh in range(HH):
                    kk = conv[:, 1, hh * BT:(hh + 1) * BT].rearrange("p (b c i) -> p b i c", b=B, i=C)
                    qq = conv[:, 0, hh * BT:(hh + 1) * BT].rearrange("p (b c i) -> p b i c", b=B, i=C)
                    at = 0
                    for left, lo in ((kk, 1), (qq, 0)):
                        for i in range(lo, C):
                            m = i if lo else i + 1
                            for b in range(B):
                                last = dve.tensor_tensor(prodk[:, hh, b, at:at + m, :], kk[:, b, 0:m],
                                                         left[:, b, i:i + 1].broadcast_to([128, m, NC_]), ALU.mult)
                            at += m
                last.then_inc(prod_ready, 1)

            def inverse_head(n):
                dve.wait_ge(pairs_copied, n + 1)
                dve.wait_ge(beta_ready, n + 1)
                bc = beta_l[:].rearrange("p (c i) -> p c i", i=C)
                for i in range(C):
                    dve.tensor_scalar(tm[:, :, i, i], bc[:, :, i], -1.0, None, ALU.mult)
                for at, (i, j) in enumerate(PAIRS_K):
                    dve.scalar_tensor_tensor(out=pair_l[:, at, :], in0=pair_l[:, at, :], scalar=-1.0,
                                             in1=bc[:, :, i], op0=ALU.mult, op1=ALU.mult)
                for at, (i, j) in enumerate(PAIRS_Q):
                    dve.tensor_copy(mm_[:, i, j, :], pair_l[:, NPK + at, :])
                done(dve.tensor_copy(state[:, 0, :, :, C], state[:, NC_, :, :, C]))

            def inverse_rows(n):
                for i in range(1, C):
                    for j in reversed(range(i)):
                        at = PAIRS_K.index((i, j))
                        g = pair_l[:, at, :].rearrange("p (c o) -> p c o", o=1).broadcast_to([128, NC_, j + 1])
                        row = tm[:, :, i, 0:j + 1]
                        if j == i - 1:
                            done(dve.tensor_tensor(row, g, tm[:, :, j, 0:j + 1], ALU.mult))
                        else:
                            done(dve.tensor_tensor(tmp_t[:, :, 0:j + 1], g, tm[:, :, j, 0:j + 1], ALU.mult))
                            done(dve.tensor_tensor(row, row, tmp_t[:, :, 0:j + 1], ALU.add))
                dve.nop().then_inc(tm_ready, 1)

            def between(n, c, slot, before):
                if c < UPG and slot % 2 == 0:
                    max_unit(n, 2 * c + slot // 2)
                if c == 8 or (c == 9 and slot == 0):
                    return max_piece(n, 0, 4 * (c - 8) + slot, before)
                if c == 17 and slot == 0:
                    out_scale(n, 0)
                if c == 19 and slot == 0:
                    out_scale(n, 1)
                if 20 <= c < 20 + UPG and slot % 2 == 0:
                    max_unit(n, 2 * UPG + 2 * (c - 20) + slot // 2)
                if c == 28 or (c == 29 and slot == 0):
                    return max_piece(n, 1, 4 * (c - 28) + slot, before)
                return None

            def scan(n, following):
                kc = k_l[:].rearrange("p k (c i) -> p c k i", i=C)
                dve.wait_ge(lanes_in, n * 48 + 48)
                dve.wait_ge(til_ready, n + 1)
                other = None
                for c in range(NC_):
                    at = mark(dve.tensor_tensor(
                        first[:, c, :, :, 0:DK],
                        state[:, c, :, :, C].rearrange("p v (o k) -> p v o k", o=1).broadcast_to([128, VR, C, DK]),
                        k_til[:, c:c + 1].broadcast_to([128, VR, C, DK]), ALU.mult))
                    if following:
                        other = between(n + 1, c, 0, other)
                    dve.wait_ge(vstep, at)
                    at = mark(dve.tensor_reduce(u_l[:, c], first[:, c], AX.X, ALU.add))
                    if following:
                        other = between(n + 1, c, 1, other)
                    dve.wait_ge(vstep, at)
                    at = mark(dve.tensor_tensor(
                        state[:, c, :, :, 0:C],
                        u_l[:, c].rearrange("p v (o i) -> p v o i", o=1).broadcast_to([128, VR, DK, C]),
                        kc[:, c:c + 1].broadcast_to([128, VR, DK, C]), ALU.mult))
                    if following:
                        other = between(n + 1, c, 2, other)
                    dve.wait_ge(vstep, at)
                    at = mark(dve.tensor_reduce(state[:, c + 1, :, :, C], state[:, c], AX.X, ALU.add))
                    if following:
                        other = between(n + 1, c, 3, other)
                    dve.wait_ge(vstep, at)
                    if (c + 1) * (DK + 1) >= NC_ // 2 * (DK + C) > c * (DK + 1):
                        dve.nop().then_inc(scanned, 1)

            def attention_alone(n):
                other = None
                for c in range(NC_):
                    for slot in range(4):
                        other = between(n, c, slot, other)

            def reduce_terms(half):
                cs = slice(half * NC_ // 2, (half + 1) * NC_ // 2)
                return dve.tensor_reduce(o_l[:, :, cs], out_terms, AX.X, ALU.add)

            def half_outputs(n):
                dve.wait_ge(terms_ready, n + 1)
                done(reduce_terms(0))
                done(terms_of(dve, slice(NC_ // 2, NC_)))

            def output_norm(n):
                dve.wait_ge(ors_ready, n + 1)
                dve.wait_ge(oss_done, n + 1)
                for hh in range(HH):
                    last = dve.scalar_tensor_tensor(out=o_n[:, hh].rearrange("p b t -> p (b t)"),
                                                    in0=o_t[:, hh].rearrange("p b t -> p (b t)"), scalar=-1.0,
                                                    in1=rs_o[:], op0=ALU.mult, op1=ALU.mult)
                last.then_inc(on_ready, 1)

            def y_of(n):
                dve.wait_ge(wout_done, n + 1)
                dve.wait_ge(held, n + 1)
                dve.tensor_tensor(flat(z_c), bank[6][:], flat(z_c), ALU.add).then_inc(y_ready, 1)

            def y_tok(n):
                dve.wait_ge(rstd_c_ready, n * 2 + 1)
                dve.wait_ge(y_ready, n + 1)
                for b in range(B):
                    last = dve.tensor_scalar(tok_c[:, b], z_c[:, b], rstd_c[:, b:b + 1], None, ALU.mult)
                last.then_inc(tok_c_ready, 1)

            def act_of(n, i):
                m = inner[i][1]
                dve.wait_ge(gate_ready, n * IT + i + 1)
                if i == HALF:
                    dve.wait_ge(mlp_half, n + 1)
                dve.tensor_tensor(hid_c[0:m, i % HALF], bank[6 + i % 2][0:m, BT:2 * BT], gate[0:m, i % 2],
                                  ALU.mult).then_inc(act_ready, 1)

            def third_residual(n):
                dve.wait_ge(mlp_done, n + 1)
                dve.wait_ge(xy_ready, n + 1)
                for b in range(B):
                    last = dve.tensor_tensor(z_c[:, b], bank[4 + b][:, 0:D], x2_c[:, b], ALU.add)
                done(last)
                normalise(z_c, tok_c, stats_c, mv_c, rstd_c, var_c_ready, rstd_c_ready, n * 2 + 2
                          ).then_inc(tok_c_ready, 1)

            def result(n):
                dve.wait_ge(ffn_c_done, n + 1)
                dve.wait_ge(x3b_ready, n + 1)
                for b in range(B):
                    last = dve.tensor_tensor(z_c[:, b], bank[4 + b][:, 0:D], z_c[:, b], ALU.add)
                last.then_inc(out_ready, 1)

            def body(t, has_scan=True, following=True, front=True):
                nonlocal steps
                steps = 0
                n = t + 1
                if has_scan:
                    scan(t, following)
                    half_outputs(t)
                else:
                    attention_alone(n)
                if following:
                    out_scale(n, 2)
                if has_scan:
                    reduce_terms(1).then_inc(o_ready, 1)
                if following:
                    out_scale(n, 3)
                    dve.wait_ge(o_scaled, n * 4 + 4)
                    dve.nop().then_inc(tok_ready, 1)
                    first_residual(n)
                if has_scan:
                    output_norm(t)
                    y_of(t)
                    y_tok(t)
                if following:
                    second_residual(n, has_scan)
                if has_scan:
                    act_of(t, 0)
                    act_of(t, 1)
                if following:
                    beta_of(n)
                    convolve(n, 0)
                if has_scan:
                    act_of(t, 2)
                if following:
                    convolve(n, 1)
                if has_scan:
                    act_of(t, 3)
                    act_of(t, 4)
                if following:
                    convolve(n, 2)
                if has_scan:
                    act_of(t, 5)
                if following:
                    keep_taps()
                    units(n)
                if front:
                    norm_in(t + 2)
                if following:
                    products(n)
                if has_scan:
                    third_residual(t)
                if following:
                    inverse_head(n)
                if front:
                    rests_first(t + 2)
                if following:
                    inverse_rows(n)
                if front:
                    rests_second(t + 2)
                if has_scan:
                    result(t)
                dve.sem_clear(vstep)

            norm_in(0)
            rests_first(0)
            rests_second(0)
            dve.sem_clear(vstep)
            body(-1, has_scan=False)
            with dve.Fori(0, NB - 2) as t:
                body(t)
            body(NB - 2, front=False)
            body(NB - 1, following=False, front=False)

        @block.tensor
        def _(pe):
            pe.wait_ge(lora_in, 64)
            for k in range(KT):
                for c in range(2):
                    pe.matmul(bank[2 * k + c][:], lora_a_up[:, k * 128:(k + 1) * 128],
                              lora_b_up[:, c * 512:(c + 1) * 512], start=True, stop=True)
            for k in range(FT):
                last = pe.matmul(bank[4 + k // 2][:, (k % 2) * D:(k % 2 + 1) * D],
                                 lora_a_dn[:, k * 128:(k + 1) * 128], lora_b_dn, start=True, stop=True)
            last.then_inc(lora_prod, 1)
            pe.wait_ge(lora_added, FT // 2)
            pe.wait_ge(weights_scaled, 1)
            pe.wait_ge(consts_cast, 1)
            pe.wait_ge(stack_init, 2)

            f = feat[:].rearrange("p k b t -> p k (b t)")
            fc = feat_c[:].rearrange("p k b t -> p k (b t)")

            def turn(src, dst_bank):
                for k in range(KT):
                    for b in range(B):
                        at = (k * B + b) * W
                        last = pe.transpose(dst_bank[:, at:at + W], src[:, b, k * 128:(k + 1) * 128], ident[:])
                return last

            def turn_a(n, k):
                pe.wait_ge(tok_ready, n * 4 + k)
                turn(tok, bank[0]).then_inc(turned, 1)
                pe.wait_ge(feat_ready, n * 4 + k)

            def turn_c(n, k):
                pe.wait_ge(tok_c_ready, n * 2 + k)
                turn(tok_c, bank[7]).then_inc(turned_c, 1)

            def to_tokens(dst, src, w, tiles):
                for b in range(B):
                    for k, m in tiles:
                        last = pe.matmul(dst[:, b * D:(b + 1) * D], src[0:m, k, b * W:(b + 1) * W],
                                         w[0:m, k, :], start=(k == 0), stop=(k == tiles[-1][0]))
                return last

            def to_tokens_c(w, tiles, final):
                for b in range(B):
                    for k, m in tiles:
                        last = pe.matmul(bank[4 + b][:, 0:D], hid_c[0:m, k % HALF, b * W:(b + 1) * W],
                                         w[0:m, k, :], start=(k == 0), stop=(k == final))
                return last

            def queries_keys(n, after_p):
                if after_p:
                    pe.wait_ge(rn_ready, n * 2)
                for s in range(2):
                    for hh in range(HH):
                        for k in range(KT):
                            last = pe.matmul(bank[1 + s][:, hh * BT:(hh + 1) * BT],
                                             wqkv_a[:, k, s * D + hh * 128:s * D + (hh + 1) * 128],
                                             f[:, k], start=(k == 0), stop=(k == KT - 1))
                    last.then_inc(qkv_done, 1)

            def values_in(n, after_p):
                if after_p:
                    pe.wait_ge(pairs_copied, n)
                for b in range(B):
                    for k in range(KT):
                        last = pe.matmul(bank[3][:, b * D:(b + 1) * D], feat[:, k, b, :],
                                         wqkv_a[:, k, 2 * D:3 * D], start=(k == 0), stop=(k == KT - 1))
                last.then_inc(qkv_done, 1)

            def scores_max(n, g):
                pe.wait_ge(stacks_in[g % 2], (n * (NG // 2) + g // 2 + 1) * 16 * STACK_DMAS)
                for v in range(UPG):
                    u = g * UPG + v
                    if u >= 2:
                        pe.wait_ge(max_done, n * N_UNITS + u - 1)
                    pb = bank[1 + u % 2][:, 0:2 * SPAN]
                    edges = pb.rearrange("p (h k) -> p h k", h=2)
                    for e in range(2):
                        pe.matmul(edges[:, :, e * W:e * W + SUB], identb[:],
                                  edge_mask[:, e * SUB:(e + 1) * SUB].rearrange("p (o s) -> p o s", o=1)
                                  .broadcast_to([128, 2, SUB]), start=(e == 0), stop=False, skip_group_check=True)
                    for hp in range(2):
                        for s in range(W // SUB):
                            last = pe.matmul(pb[s * SUB:(s + 1) * SUB, hp * SPAN:(hp + 1) * SPAN],
                                             q_stack[:, g % 2, 2 * v + hp, s * SUB:(s + 1) * SUB],
                                             k_stack[:, g % 2, 2 * v + hp, s * SUB:s * SUB + SPAN],
                                             start=False, stop=True, skip_group_check=True)
                    last.then_inc(scores1, 1)

            def turn_max(n, pair):
                pe.wait_ge(mpieces_ready, n * (NG // 2) + pair + 1)
                if pair:
                    pe.wait_ge(o_scaled, n * NG + 2 * pair)
                pe.transpose(bank_b[0:6 * HPH, 0:W],
                             mpieces[:, 2 * pair:2 * pair + 2].rearrange("p g j h -> p (g j h)"),
                             identb[:]).then_inc(m_turned, 1)

            def scores(n, u):
                g, v = divmod(u, UPG)
                if v == 0:
                    pe.wait_ge(m_in[g % 2], (n * (NG // 2) + g // 2 + 1) * 48)
                if u >= 2:
                    pe.wait_ge(exp_done, n * N_UNITS + u - 1)
                pb = bank[3 + u % 2]
                pe.matmul(pb[:], identb[:], tri_mask[:].rearrange("p (o t) -> p o t", o=1)
                          .broadcast_to([128, 2, 2 * W]), start=True, stop=False, skip_group_check=True)
                for hp in range(2):
                    for kb in range(2):
                        at = (hp * 2 + kb) * W
                        last = pe.matmul(pb[:, at:at + W], k_stack[:, g % 2, 2 * v + hp, kb * W:(kb + 1) * W],
                                         q_stack[:, g % 2, 2 * v + hp, :], start=False, stop=True,
                                         skip_group_check=True)
                last.then_inc(scores2, 1)

            def values(n, u):
                g, v = divmod(u, UPG)
                pe.wait_ge(exp_done, n * N_UNITS + u + 1)
                if v == 0 and g:
                    pe.wait_ge(o_copied, n * NG + g)
                for hp in range(2):
                    b, h = divmod(2 * u + hp, H)
                    row, col = 32 * (h % 4), (h % HPH) // 4 * W
                    for kb in range(2):
                        last = pe.matmul(bank[5][row:row + VE, col:col + W], v_ext[:, b, kb, h, :],
                                         probs[:, u % 2, (hp * 2 + kb) * W:(hp * 2 + kb + 1) * W],
                                         start=(kb == 0), stop=(kb == 1))
                if v == UPG - 1:
                    last.then_inc(pv_done, 1)

            def turn_out(n, g):
                pe.wait_ge(o_copied, n * NG + g + 1)
                if g % 2 == 0:
                    pe.wait_ge(m_copied, n * (NG // 2) + g // 2 + 1)
                else:
                    pe.wait_ge(o_scaled, n * NG + g)
                for j in range(4):
                    last = pe.transpose(bank[0][:, j * W:(j + 1) * W], o_rows[:, j * W:(j + 1) * W], ident[:])
                last.then_inc(o_turned, 1)

            def attention(n, after_c):
                pe.wait_ge(rest1, n * 2 + 2)
                for pair in range(NG // 2):
                    for g in (2 * pair, 2 * pair + 1):
                        scores_max(n, g)
                    turn_max(n, pair)
                    if pair == 0:
                        pe.wait_ge(v_done, n + 1)
                        if after_c:
                            pe.wait_ge(out_stored, n * 16)
                    u0, u1 = 2 * pair * UPG, (2 * pair + 2) * UPG
                    for u in range(u0, u1 + 1):
                        if u < u1:
                            scores(n, u)
                        if u > u0:
                            values(n, u - 1)
                        if u == u0 + UPG + 2:
                            turn_out(n, 2 * pair)
                    turn_out(n, 2 * pair + 1)
                turn_a(n, 2)
                to_tokens(bank[1], f, wo_a, [(k, 128) for k in range(KT)]).then_inc(wo_done, 1)

            def ffn_up(n):
                turn_a(n, 3)
                pe.wait_ge(x1_ready, n + 1)
                for i in range(FT):
                    if i >= 2:
                        pe.wait_ge(hid_ready, n * FT + i - 1)
                    for k in range(KT):
                        last = pe.matmul(bank[1 + i % 2][:, 0:BT], w_up[:, k, i * 128:(i + 1) * 128],
                                         f[:, k], start=(k == 0), stop=(k == KT - 1))
                    last.then_inc(hid_done, 1)

            def ffn_down(n):
                pe.wait_ge(hid_ready, n * FT + FT)
                to_tokens(bank[3], hid, w_dn, [(k, 128) for k in range(FT)]).then_inc(ffn_done, 1)

            def beta_in(n):
                for b in range(B):
                    for k in range(KT):
                        last = pe.matmul(bank[4][:, 0:W], wbeta[:, k, b, :], feat[:, k, b, :],
                                         start=(b == 0 and k == 0), stop=(b == B - 1 and k == KT - 1))
                last.then_inc(projb_done, 1)

            def delta_in(n):
                for s in range(3):
                    for hh in range(HH):
                        for k in range(KT):
                            last = pe.matmul(bank[1 + s][:, hh * BT:(hh + 1) * BT],
                                             wqkv_b[:, k, s * D + hh * 128:s * D + (hh + 1) * 128],
                                             f[:, k], start=(k == 0), stop=(k == KT - 1))
                    last.then_inc(projb_done, 1)

            def square_sums(n):
                for s in range(2):
                    pe.wait_ge(raw_ready, n * 3 + s + 1)
                    pe.wait_ge(sq_ready, n * 2 + s + 1)
                    pe.matmul(bank[1 + s][:], head_sum[:], sqk[:, s], start=True, stop=True).then_inc(ss_done, 1)

            def pairs(n):
                pe.wait_ge(prod_ready, n + 1)
                pe.wait_ge(raw_ready, n * 3 + 3)
                for hh in range(HH):
                    for b in range(B):
                        g = b * HH + hh
                        last = pe.matmul(bank[3][:], to_lanes[:, g], prodk[:, hh, b].rearrange("p a c -> p (a c)"),
                                         start=(hh == 0 and b == 0), stop=(hh == HH - 1 and b == B - 1))
                last.then_inc(pairs_done, 1)

            def output_sums(n):
                pe.wait_ge(osq_ready, n + 1)
                for hh in range(HH):
                    last = pe.matmul(bank[6][:, 0:BT], ones[:], o_n[:, hh].rearrange("p b t -> p (b t)"),
                                     start=(hh == 0), stop=(hh == HH - 1))
                last.then_inc(oss_done, 1)

            def output_product(n):
                pe.wait_ge(on_ready, n + 1)
                pe.wait_ge(ors_ready, n + 1)
                to_tokens(bank[6], o_n.rearrange("p k b t -> p k (b t)"), wout_b,
                          [(k, 128) for k in range(KT)]).then_inc(wout_done, 1)

            def gate_up(n, i):
                m = inner[i][1]
                if i == 0:
                    pe.wait_ge(feat_c_ready, n * 2 + 1)
                    pe.wait_ge(y_ready, n + 1)
                if i >= 2:
                    pe.wait_ge(act_ready, n * IT + i - 1)
                for g in range(2):
                    for k in range(KT):
                        last = pe.matmul(bank[6 + i % 2][0:m, g * BT:(g + 1) * BT],
                                         wgu[:, k, g * INTER + 128 * i:g * INTER + 128 * i + m],
                                         fc[:, k], start=(k == 0), stop=(k == KT - 1))
                last.then_inc(gu_done, 1)

            def mlp_down(n, half, following):
                if half == 0:
                    if following:
                        pe.wait_ge(beta_exp, n + 2)
                    pe.wait_ge(act_ready, n * IT + HALF)
                    to_tokens_c(wdown_b, inner[:HALF], IT - 1).then_inc(mlp_half, 1)
                else:
                    pe.wait_ge(act_ready, n * IT + IT)
                    to_tokens_c(wdown_b, inner[HALF:], IT - 1).then_inc(mlp_done, 1)

            def ffn_c_up(n, lo, hi):
                for i in range(lo, hi):
                    if i == 0:
                        pe.wait_ge(feat_c_ready, n * 2 + 2)
                    if i >= 2:
                        pe.wait_ge(hid_c_ready, n * FT + i - 1)
                    for k in range(KT):
                        last = pe.matmul(bank[6 + i % 2][:, 0:BT], w_up[:, k, i * 128:(i + 1) * 128],
                                         fc[:, k], start=(k == 0), stop=(k == KT - 1))
                    last.then_inc(hid_c_done, 1)

            def ffn_c_down(n, half):
                pe.wait_ge(hid_c_ready, n * FT + (half + 1) * HALF)
                to_tokens_c(w_dn, [(k, 128) for k in range(half * HALF, (half + 1) * HALF)], FT - 1
                            ).then_inc((ffn_c_half, ffn_c_done)[half], 1)

            def body(t, scan=True, following=True, front=True):
                n = t + 1
                if following:
                    attention(n, scan)
                    ffn_up(n)
                if scan:
                    output_sums(t)
                    output_product(t)
                if following:
                    ffn_down(n)
                if scan:
                    turn_c(t, 1)
                    gate_up(t, 0)
                    gate_up(t, 1)
                if following:
                    turn_a(n, 4)
                    beta_in(n)
                    delta_in(n)
                if scan:
                    for i in range(2, HALF + 1):
                        gate_up(t, i)
                    mlp_down(t, 0, following)
                    gate_up(t, HALF + 1)
                if following:
                    square_sums(n)
                if scan:
                    mlp_down(t, 1, following)
                if front:
                    turn_a(t + 2, 1)
                    queries_keys(t + 2, True)
                if following:
                    pairs(n)
                if scan:
                    turn_c(t, 2)
                if front:
                    values_in(t + 2, True)
                if scan:
                    ffn_c_up(t, 0, HALF + 2)
                    ffn_c_down(t, 0)
                    ffn_c_up(t, HALF + 2, FT)
                    ffn_c_down(t, 1)

            turn_a(0, 1)
            queries_keys(0, False)
            values_in(0, False)
            body(-1, scan=False)
            with pe.Fori(0, NB - 2) as t:
                body(t)
            body(NB - 2, front=False)
            body(NB - 1, following=False, front=False)


def kernel(**inputs):
    import numpy as np
    import ml_dtypes
    import concourse.bacc as bacc
    from concourse.bass_utils import run_bass_kernel_spmd

    g = {k: np.asarray(v) for k, v in inputs.items()}
    t = lambda x: np.ascontiguousarray(x)
    A, Bp, Fp = "L0_attn_a_", "L0_attn_b_", "L0_ffn_"
    rows = lambda v: v.reshape(-1, 128).T
    ar = {
        "x": g[A + "x"],
        "wqkv_a": np.concatenate([g[A + "Wq"].T, g[A + "Wk"].T, g[A + "Wv"].T], axis=1),
        "wo_a": g[A + "Wo"].T,
        "wqkv_b": np.concatenate([g[Bp + "Wq"].T, g[Bp + "Wk"].T, g[Bp + "Wv"].T], axis=1),
        "wout_b": g[Bp + "Wout"].T,
        "wgu": np.concatenate([g[Bp + "Wgate"].T, g[Bp + "Wup"].T], axis=1),
        "wdown_b": g[Bp + "Wdown"].T,
        "norm_w": np.stack([rows(g[Bp + n]) for n in ("attn_norm_w", "out_norm_w", "mlp_norm_w")], axis=1),
        "conv_w": np.stack([g[Bp + n].reshape(HH, 128, TAPS).transpose(1, 0, 2)
                            for n in ("conv_q", "conv_k", "conv_v")], axis=1),
        "q_up": g[Fp + "w_up_q"].T, "s_up": g[Fp + "w_up_scale"].T, "b_up": rows(g[Fp + "b_up"]),
        "lora_a_up": g[Fp + "w_up_lora_a"].T, "lora_b_up": g[Fp + "w_up_lora_b"],
        "q_dn": g[Fp + "w_down_q"].T, "s_dn": g[Fp + "w_down_scale"].T, "b_dn": g[Fp + "b_down"][None],
        "lora_a_dn": g[Fp + "w_down_lora_a"].T, "lora_b_dn": g[Fp + "w_down_lora_b"],
    }
    wb = np.zeros((D, B, B, H, VH), np.float32)
    for b in range(B):
        wb[:, b, b] = g[Bp + "Wbeta"].T[:, :, None]
    ar["wbeta"] = wb.reshape(D, B, B * H * VH)
    p = np.arange(128)
    ar["ident"] = np.eye(128, dtype=np.float32)
    ar["ones"] = np.ones((128, 128), np.float32)
    ar["head_sum"] = (p[:, None] // DK == p[None] // DK).astype(np.float32)
    lanes = np.zeros((128, B * HH, B * HH, HPH, VH), np.float32)
    for s in range(B * HH):
        lanes[:, s, s] = (p[:, None] // DK == np.arange(HPH)[None])[:, :, None]
    ar["to_lanes"] = lanes.reshape(128, B * HH, 128)
    q32, c32 = (p % SUB)[:, None], np.arange(SUB)[None]
    ar["edge_mask"] = np.concatenate([np.where(c32 < q32, -BIG, 0), np.where(c32 > q32, -BIG, 0)], 1).astype(np.float32)
    ar["tri_mask"] = np.concatenate([np.where(p[:, None] < p[None], -BIG, 0),
                                     np.where(p[:, None] > p[None], -BIG, 0)], 1).astype(np.float32)
    cols = np.zeros((128, 2), np.float32)
    cols[PADROW, 0] = 1
    cols[MROW:MROW + 3, 1] = 1
    ar["stack_cols"] = cols
    ar["eps"] = np.tile(np.array([[LN_EPS, RMS_EPS, -L2_MIN2, L2_MIN2, 1, -1]], np.float32), (128, 1))
    pad = np.zeros((1, W + T), ml_dtypes.bfloat16)
    pad[:, :W] = -BIG
    ar["pad_row"] = pad
    ar["zero_rows"] = np.zeros((3, HPH, W), ml_dtypes.bfloat16)

    nc = bacc.Bacc("TRN2", target_bir_lowering=False, num_devices=1)
    arrays, aps = {}, {}
    for name, v in ar.items():
        v = np.ascontiguousarray(v)
        arrays[f"in_{name}"] = v
        aps[name] = nc.dram_tensor(f"in_{name}", v.shape, mybir.dt.from_np(v.dtype), kind="ExternalInput").ap()
    aps["out"] = nc.dram_tensor("out_x", (B, T, D), F32, kind="ExternalOutput").ap()
    layer_program(nc, aps)
    r = run_bass_kernel_spmd(nc, [arrays], core_ids=[0])
    return r.results[0]["out_x"]
```

```python
import concourse.bass as bass
from concourse import mybir
from contextlib import ExitStack

F32 = mybir.dt.float32
BF16 = mybir.dt.bfloat16
I32 = mybir.dt.int32
ACT = mybir.ActivationFunctionType
ALU = mybir.AluOpType
AX = mybir.AxisListType

B, T, D = 2, 1024, 256
H, DK = 32, 8
W = 128
NB = T // W
BT = B * W
KT = D // 128
HH = D // 128
HPH = H // HH
FF = 1024
FT = FF // 128
RANK = 16
QBLK = 64
INTER = 704
IT = (INTER + 127) // 128
TAPS = 4
C = 4
NC_ = W // C
VH = 2
VR = DK // VH
PAIRS_K = [(i, j) for i in range(1, C) for j in range(i)]
PAIRS_Q = [(i, j) for i in range(C) for j in range(i + 1)]
NPK, NPQ = len(PAIRS_K), len(PAIRS_Q)
PIECE_PAIRS = [(0, 0), (0, 1), (1, 0), (1, 1), (0, 2), (2, 0)]
SROWS = DK * len(PIECE_PAIRS)
MROW = SROWS
PADROW = SROWS + 3
BIG = 1e30
LOG_EXP_SET = "natural_log_exp_and_others"
LN_EPS, RMS_EPS, L2_MIN2 = 1e-5, 1e-6, 1e-24
HALF = FT // 2
SUB = 32
SPAN = W + SUB
VE = 16
PER = 4
MAX_TURN_AT = 5
UPG = HPH // 2
NG = B * HH


def layer_program(nc, a):
    with ExitStack() as ctx:
        def sb(name, shape, dt=F32):
            return ctx.enter_context(nc.sbuf_tensor(name, shape, dt))

        def sem(name):
            return ctx.enter_context(nc.semaphore(name))

        q_pieces = nc.dram_tensor("q_pieces", (NB, 3, HH, 128, B, W), BF16, kind="Internal").ap()
        k_pieces = nc.dram_tensor("k_pieces", (3, HH, 128, B, W + T), BF16, kind="Internal").ap()
        lane_q = nc.dram_tensor("lane_q", (B, HH, 128, W), F32, kind="Internal").ap()
        lane_k = nc.dram_tensor("lane_k", (B, HH, 128, W), F32, kind="Internal").ap()
        lane_v = nc.dram_tensor("lane_v", (B, HH, 128, W), F32, kind="Internal").ap()
        lane_o = nc.dram_tensor("lane_o", (B, HH, 128, W), F32, kind="Internal").ap()

        ident = sb("ident", [128, 128])
        ones = sb("ones", [128, 128])
        head_sum = sb("head_sum", [128, 128])
        to_lanes = sb("to_lanes", [128, B * HH, 128])
        edge_mask_f = sb("edge_mask_f", [128, 2 * SUB])
        tri_mask_f = sb("tri_mask_f", [128, 2 * W])
        identb = sb("identb", [128, 128], BF16)
        edge_mask = sb("edge_mask", [128, 2 * SUB], BF16)
        tri_mask = sb("tri_mask", [128, 2 * W], BF16)
        stack_cols = sb("stack_cols", [128, 2])
        eps = sb("eps", [128, 6])
        wqkv_a = sb("wqkv_a", [128, KT, 3 * D])
        wo_a = sb("wo_a", [128, KT, D])
        wqkv_b = sb("wqkv_b", [128, KT, 3 * D])
        wbeta = sb("wbeta", [128, KT, B, 128])
        wout_b = sb("wout_b", [128, KT, D])
        wgu = sb("wgu", [128, KT, 2 * INTER])
        wdown_b = sb("wdown_b", [128, IT, D])
        norm_w = sb("norm_w", [128, 3, KT])
        conv_w = sb("conv_w", [128, 3, HH, TAPS])
        w_up = sb("w_up", [128, KT, FF])
        w_dn = sb("w_dn", [128, FT, D])
        b_up = sb("b_up", [128, FT])
        b_dn = sb("b_dn", [128, D])

        x_in = sb("x_in", [128, B, D])
        tok = sb("tok", [128, B, D])
        feat = sb("feat", [128, KT, B, W])
        tok_c = sb("tok_c", [128, B, D])
        feat_c = sb("feat_c", [128, KT, B, W])
        stats = sb("stats", [128, B, 6])
        mv = sb("mv", [128, B, 2])
        lnv = sb("lnv", [128, B])
        rstd = sb("rstd", [128, B])
        sq = sb("sq", [128, D])
        lnt = sb("lnt", [128, B])
        lnt_c = sb("lnt_c", [128, B])
        stats_c = sb("stats_c", [128, B, 6])
        mv_c = sb("mv_c", [128, B, 2])
        lnv_c = sb("lnv_c", [128, B])
        rstd_c = sb("rstd_c", [128, B])
        rs_o = sb("rs_o", [128, BT])
        x1 = x_in
        x2 = sb("x2", [128, B, D])
        z = sb("z", [128, B, D])
        x2_c = sb("x2_c", [128, B, D])
        z_c = sb("z_c", [128, B, D])
        hid = sb("hid", [128, FT, BT])
        hid_c = sb("hid_c", [128, HALF, BT])
        sqk = sb("sqk", [128, 2, HH * BT])
        conv = sb("conv", [128, 3, HH * BT])
        pieces = conv[:].bitcast(BF16).rearrange("p s (a t) -> p (s a) t", a=2).rearrange("p (s j) t -> p s j t", s=2)
        rest = sqk
        x_next = x2
        tok_next = sqk[:, 0].rearrange("p (b d) -> p b d", b=B)
        q_stack = sb("q_stack", [128, 2, HPH, W], BF16)
        k_stack = sb("k_stack", [128, 2, HPH, 2 * W], BF16)
        v_ext = sb("v_ext", [128, B, 2, H, VE])
        mx = sb("mx", [128, NG, HPH])
        nmx = sb("nmx", [128, NG, HPH])
        mpieces = sb("mpieces", [128, NG, 5, HPH], BF16)
        m_rows = sb("m_rows", [3 * HPH, 2, W], BF16)
        probs = sb("probs", [128, 3, 2 * 2 * W])
        o_rows = tok_c[:].rearrange("p b d -> p (b d)")
        rden = sb("rden", [128, HPH])
        raw = sb("raw", [128, 3, HH, B, TAPS - 1 + W])
        prodk = hid[:].rearrange("p a b -> p (a b)").rearrange("p (h b q c) -> p h b q c", h=HH, b=B, q=NPK + NPQ)
        beta_l = sb("beta_l", [128, W])
        k_l = sb("k_l", [128, DK, W])
        q_l = sb("q_l", [128, DK, W])
        v_l = sb("v_l", [128, VR, W])
        tm = sb("tm", [128, NC_, C, C])
        mm_ = sb("mm_", [128, C, C, NC_])
        tmp_t = sb("tmp_t", [128, NC_, C])
        k_til = sb("k_til", [128, NC_, C, DK])
        tmp_k = prodk.rearrange("p h b q c -> p (h b q c)")[:, 0:NC_ * C * DK].rearrange("p (c i k) -> p c i k", i=C, k=DK)
        lane_buf = sb("lane_buf", [128, NC_ * VR * C * (DK + 1)])
        first = lane_buf[:].rearrange("p (c v i k) -> p c v i k", v=VR, i=C, k=DK + 1)
        tmp_v = sb("tmp_v", [128, NC_, VR, C])
        u_l = sb("u_l", [128, NC_, VR, C])
        pair_l = u_l[:].rearrange("p c v i -> p (c v i)").rearrange("p (a c) -> p a c", c=NC_)
        state = sb("state", [128, NC_ + 1, VR, DK, C + 1])
        out_terms = lane_buf[:, 0:VR * W // 2 * (DK + C)].rearrange("p (v c i e) -> p v c i e", v=VR, i=C, e=DK + C)
        o_l = k_l[:].rearrange("p k t -> p (k t)")[:, 0:VR * W].rearrange("p (v c i) -> p v c i", v=VR, i=C)
        o_t = q_l[:, 0:DK // 2].rearrange("p k t -> p (k t)").rearrange("p (h b t) -> p h b t", h=HH, b=B)
        o_n = q_l[:, DK // 2:DK].rearrange("p k t -> p (k t)").rearrange("p (h b t) -> p h b t", h=HH, b=B)
        gate = probs[:, 0].rearrange("p (i t) -> p i t", i=2)

        bank = [ctx.enter_context(nc.psum_tensor(f"bank{i}", [128, 512], F32)) for i in range(8)]
        score_bank = (bank[3], bank[4], bank[6])
        bank_b = bank[0][:, :].bitcast(BF16)

        early_in = sem("early_in")
        consts_in = sem("consts_in")
        weights_in = sem("weights_in")
        quant_in = sem("quant_in")
        dequantised = sem("dequantised")
        lora_in = sem("lora_in")
        lora_prod = sem("lora_prod")
        lora_added = sem("lora_added")
        consts_cast = sem("consts_cast")
        weights_scaled = sem("weights_scaled")
        zeroed = sem("zeroed")
        pad_out = sem("pad_out")
        x_loaded = sem("x_loaded")
        x_used = sem("x_used")
        vstep = sem("vstep")
        astep = sem("astep")
        gstep = sem("gstep")
        x_again = sem("x_again")
        vars_next = sem("vars_next")
        rstd_next = sem("rstd_next")
        tok_next_ready = sem("tok_next_ready")
        turned_next = sem("turned_next")
        feat_next = sem("feat_next")
        vars_ready = sem("vars_ready")
        rstd_ready = sem("rstd_ready")
        tok_ready = sem("tok_ready")
        turned = sem("turned")
        feat_ready = sem("feat_ready")
        qkv_done = sem("qkv_done")
        piece1 = sem("piece1")
        rest1 = sem("rest1")
        piece2 = sem("piece2")
        piece3 = sem("piece3")
        v_done = sem("v_done")
        pieces_out = sem("pieces_out")
        stacks_in = [sem("stacks_in0"), sem("stacks_in1")]
        pad_in = sem("pad_in")
        stack_init = sem("stack_init")
        sq_rstd = sem("sq_rstd")
        scores1 = sem("scores1")
        max_done = sem("max_done")
        mpieces_ready = sem("mpieces_ready")
        m_turned = sem("m_turned")
        m_copied = sem("m_copied")
        m_in = [sem("m_in0"), sem("m_in1")]
        scores2 = sem("scores2")
        exp_done = sem("exp_done")
        pv_done = sem("pv_done")
        o_copied = sem("o_copied")
        o_turned = sem("o_turned")
        o_scaled = sem("o_scaled")
        wo_done = sem("wo_done")
        x1_ready = sem("x1_ready")
        x1b_ready = sem("x1b_ready")
        hid_done = sem("hid_done")
        hid_ready = sem("hid_ready")
        ffn_done = sem("ffn_done")
        z_ready = sem("z_ready")
        projb_done = sem("projb_done")
        raw_ready = sem("raw_ready")
        beta_ready = sem("beta_ready")
        beta_exp = sem("beta_exp")
        conv_ready = sem("conv_ready")
        silu_ready = sem("silu_ready")
        sq_ready = sem("sq_ready")
        ss_done = sem("ss_done")
        rn_ready = sem("rn_ready")
        unit_ready = sem("unit_ready")
        prod_ready = sem("prod_ready")
        pairs_done = sem("pairs_done")
        pairs_copied = sem("pairs_copied")
        lanes_out = sem("lanes_out")
        lanes_in = sem("lanes_in")
        tm_ready = sem("tm_ready")
        til_ready = sem("til_ready")
        held = sem("held")
        scanned = sem("scanned")
        terms_ready = sem("terms_ready")
        o_ready = sem("o_ready")
        o_out = sem("o_out")
        o_in = sem("o_in")
        osq_ready = sem("osq_ready")
        oss_done = sem("oss_done")
        ors_ready = sem("ors_ready")
        on_ready = sem("on_ready")
        wout_done = sem("wout_done")
        y_ready = sem("y_ready")
        xy_ready = sem("xy_ready")
        var_c_ready = sem("var_c_ready")
        rstd_c_ready = sem("rstd_c_ready")
        tok_c_ready = sem("tok_c_ready")
        turned_c = sem("turned_c")
        feat_c_ready = sem("feat_c_ready")
        gu_done = sem("gu_done")
        gate_ready = sem("gate_ready")
        act_ready = sem("act_ready")
        mlp_half = sem("mlp_half")
        mlp_done = sem("mlp_done")
        x3b_ready = sem("x3b_ready")
        hid_c_done = sem("hid_c_done")
        hid_c_ready = sem("hid_c_ready")
        ffn_c_half = sem("ffn_c_half")
        ffn_c_done = sem("ffn_c_done")
        out_ready = sem("out_ready")
        out_stored = sem("out_stored")

        inner = [(i, min(128, INTER - 128 * i)) for i in range(IT)]
        N_UNITS = B * H // 2
        STACK_DMAS = 2 * len(PIECE_PAIRS) + 1
        x_v = a["x"].rearrange("b (n p) d -> n p b d", p=W)
        out_v = a["out"].rearrange("b (n p) d -> n p b d", p=W)

        plain = [
            (wo_a[:], a["wo_a"].rearrange("(k p) n -> p k n", p=128)),
            (b_up[:], a["b_up"]),
            (b_dn[:], a["b_dn"].broadcast_to([128, D])),
            (conv_w[:], a["conv_w"]),
            (wqkv_b[:], a["wqkv_b"].rearrange("(k p) n -> p k n", p=128)),
            (wbeta[:], a["wbeta"].rearrange("(k p) b n -> p k b n", p=128)),
            (norm_w[:], a["norm_w"]),
            (wout_b[:], a["wout_b"].rearrange("(k p) n -> p k n", p=128)),
            (wgu[:], a["wgu"].rearrange("(k p) n -> p k n", p=128)),
        ]
        early = [(ident[:], a["ident"]), (eps[:], a["eps"])]
        consts = [(ones[:], a["ones"]), (head_sum[:], a["head_sum"]),
                  (to_lanes[:], a["to_lanes"]), (edge_mask_f[:], a["edge_mask"]),
                  (tri_mask_f[:], a["tri_mask"]), (stack_cols[:], a["stack_cols"])]
        staged = state[:].rearrange("p c v k j -> p (c v k j)").bitcast(I32)
        q_up = staged[:, 0:KT * FF]
        q_dn = staged[:, KT * FF:KT * FF + FT * D]
        s_up = lane_buf[:, 0:KT * FF]
        s_dn = lane_buf[:, KT * FF:KT * FF + FT * D]
        small = u_l[:].rearrange("p c v i -> p (c v i)")
        lora_a_up = small[0:RANK, 0:D]
        lora_b_dn = small[0:RANK, D:2 * D]
        lora_b_up = hid[0:RANK, 0:4, :].rearrange("p a b -> p (a b)")
        lora_a_dn = hid[0:RANK, 4:8, :].rearrange("p a b -> p (a b)")

        block = ctx.enter_context(nc.Block())

        def terms_of(engine, cs, steps=range(C)):
            qc = q_l[:].rearrange("p k (c i) -> p i c k", i=C)
            n_c = cs.stop - cs.start
            for i in steps:
                for v in range(VR):
                    engine.tensor_tensor(out_terms[:, v, :, i, 0:DK], state[:, cs, v, :, C], qc[:, i, cs, :], ALU.mult)
                last = engine.tensor_tensor(
                    out_terms[:, :, :, i, DK:DK + C],
                    mm_[:, i, :, cs].rearrange("p j (o c) -> p o c j", o=1).broadcast_to([128, VR, n_c, C]),
                    u_l[:, cs].rearrange("p c v j -> p v c j"), ALU.mult)
            return last

        @block.sync
        def _(sp):
            def load_x(n, after_c):
                if after_c:
                    sp.wait_ge(held, n - 1)
                sp.dma_start(x_next[:], x_v[bass.ds(n, 1)].rearrange("n p b d -> (n p) b d")).then_inc(x_loaded, 16)

            def load_residual(n):
                sp.wait_ge(x_used, n + 1)
                sp.dma_start(x_in[:], x_v[bass.ds(n, 1)].rearrange("n p b d -> (n p) b d")).then_inc(x_again, 16)

            def load_stacks(n, g):
                b, hh = divmod(g, HH)
                sp.dma_start(q_stack[MROW:MROW + 3, g % 2], a["zero_rows"]).then_inc(stacks_in[g % 2], 16)
                for r, (i, j) in enumerate(PIECE_PAIRS):
                    rows = slice(r * DK, (r + 1) * DK)
                    sp.dma_start(q_stack[rows, g % 2], q_pieces[bass.ds(n, 1), i, hh, :, b, :].rearrange(
                        "n (h d) t -> d (n h) t", d=DK)).then_inc(stacks_in[g % 2], 16)
                    sp.dma_start(k_stack[rows, g % 2], k_pieces[j, hh, :, b, bass.ds(n * W, 2 * W)].rearrange(
                        "(h d) t -> d h t", d=DK)).then_inc(stacks_in[g % 2], 16)

            def load_pad(n):
                for ring in range(2):
                    sp.dma_start(k_stack[PADROW:PADROW + 1, ring],
                                 a["pad_row"][:, n * W:(n + 2) * W].rearrange("a (o t) -> a o t", o=1)
                                 .broadcast_to([1, HPH, 2 * W])).then_inc(pad_in, 16)

            def pieces_to_dram(n):
                sp.wait_ge(piece3, n * 2 + 2)
                for p in range(3):
                    sp.dma_start(q_pieces[bass.ds(n, 1), p].rearrange("n h p b t -> p (n h) b t"),
                                 pieces[:, 0, p, :].rearrange("p (h b t) -> p h b t", h=HH, b=B)
                                 ).then_inc(pieces_out, 16)
                    for hh in range(HH):
                        sp.dma_start(k_pieces[p, hh, :, :, bass.ds(n * W + W, W)],
                                     pieces[:, 1, p, hh * BT:(hh + 1) * BT].rearrange("p (b t) -> p b t", b=B)
                                     ).then_inc(pieces_out, 16)

            def load_max(n, g):
                sp.wait_ge(m_copied, n * NG + g + 1)
                for j in range(3):
                    sp.dma_start(q_stack[MROW + j:MROW + j + 1, g % 2], m_rows[j * HPH:(j + 1) * HPH, g % 2, :]
                                 ).then_inc(m_in[g % 2], 16)

            def outputs_out(n):
                sp.wait_ge(o_ready, n + 1)
                sp.dma_start(lane_o.rearrange("b hh (h v) t -> (b hh h) (v t)", v=VR),
                             o_l.rearrange("p v c i -> p (v c i)")).then_inc(o_out, 16)

            def outputs_in(n):
                sp.wait_ge(o_out, n * 16 + 16)
                for hh in range(HH):
                    sp.dma_start(o_t[:, hh], lane_o[:, hh].rearrange("b p t -> p b t")).then_inc(o_in, 16)

            def to_lanes_dma(n, after_c):
                sp.wait_ge(unit_ready, n * 2 + 2)
                sp.wait_ge(silu_ready, n * 3 + 3)
                for s, dst in enumerate((lane_q, lane_k, lane_v)):
                    for hh in range(HH):
                        sp.dma_start(dst[:, hh].rearrange("b p t -> p b t"),
                                     conv[:, s, hh * BT:(hh + 1) * BT].rearrange("p (b t) -> p b t", b=B)
                                     ).then_inc(lanes_out, 16)
                sp.wait_ge(lanes_out, n * 96 + 96)
                if after_c:
                    sp.wait_ge(wout_done, n)
                for src, dst in ((lane_q, q_l), (lane_k, k_l)):
                    sp.dma_start(dst[:].rearrange("p k t -> p (k t)"),
                                 src.rearrange("b hh (h o d) t -> (b hh h) o (d t)", o=1, d=DK)
                                 .broadcast_to([B * H, VH, DK * W])).then_inc(lanes_in, 16)
                sp.dma_start(v_l[:].rearrange("p k t -> p (k t)"),
                             lane_v.rearrange("b hh (h v) t -> (b hh h) (v t)", v=VR)).then_inc(lanes_in, 16)

            def body(t, scan=True, following=True, front=True):
                n = t + 1
                if front:
                    load_x(t + 2, scan)
                if following:
                    for g in range(2):
                        load_max(n, g)
                    for g in range(2, NG):
                        sp.wait_ge(scores2, n * N_UNITS + (g - 1) * UPG)
                        load_stacks(n, g)
                    load_max(n, 2)
                    load_max(n, 3)
                if scan:
                    outputs_out(t)
                    outputs_in(t)
                if front:
                    pieces_to_dram(t + 2)
                    sp.wait_ge(pieces_out, (t + 2) * 144 + 144)
                    for g in range(2):
                        load_stacks(t + 2, g)
                    if not scan:
                        load_pad(1)
                    load_residual(t + 2)
                if following:
                    to_lanes_dma(n, scan)
                if scan:
                    sp.wait_ge(out_ready, t + 1)
                    sp.dma_start(out_v[bass.ds(t, 1)].rearrange("n p b d -> (n p) b d"), z_c[:]
                                 ).then_inc(out_stored, 16)

            for dst, src in early:
                sp.dma_start(dst, src).then_inc(early_in, 16)
            load_x(0, False)
            for dst, src in consts:
                sp.dma_start(dst, src).then_inc(consts_in, 16)
            sp.wait_ge(zeroed, 1)
            for p in range(3):
                for hh in range(HH):
                    sp.dma_start(k_pieces[p, hh, :, :, 0:W],
                                 q_stack[:, 0, 0:B, :]).then_inc(pad_out, 16)
            for dst, src in plain:
                sp.dma_start(dst, src).then_inc(weights_in, 16)
            for i, m in inner:
                sp.dma_start(wdown_b[0:m, i, :], a["wdown_b"][128 * i:128 * i + m, :]).then_inc(weights_in, 16)
            load_residual(0)
            pieces_to_dram(0)
            sp.wait_ge(pieces_out, 144)
            sp.wait_ge(pad_out, 16 * 3 * HH)
            sp.wait_ge(stack_init, 2)
            for g in range(2):
                load_stacks(0, g)
            load_pad(0)
            body(-1, scan=False)
            with sp.Fori(0, NB - 2) as t:
                body(t)
            body(NB - 2, front=False)
            body(NB - 1, following=False, front=False)
            sp.wait_ge(out_stored, 16 * NB + 16)

        @block.gpsimd
        def _(pool):
            pool.memset(q_stack[:], 0.0).then_inc(zeroed, 1)
            pool.memset(v_ext[:], 0.0).then_inc(gstep, 1)
            pool.wait_ge(gstep, 1)
            pool.memset(v_ext[:, :, :, :, DK:DK + 1], 1.0).then_inc(zeroed, 1)
            pool.memset(raw[:], 0.0).then_inc(zeroed, 1)
            pool.memset(mpieces[:], 0.0).then_inc(zeroed, 1)
            pool.memset(tm[:], 0.0).then_inc(zeroed, 1)
            pool.memset(mm_[:], 0.0).then_inc(zeroed, 1)
            pool.memset(state[:, NC_], 0.0).then_inc(zeroed, 1)
            pool.sem_clear(gstep)

            steps = 0

            def done(ins):
                nonlocal steps
                steps += 1
                ins.then_inc(gstep, 1)
                pool.wait_ge(gstep, steps)

            def first_terms(n):
                pool.wait_ge(scanned, n + 1)
                terms_of(pool, slice(0, NC_ // 2)).then_inc(terms_ready, 1)

            def ffn_bias(n):
                pool.wait_ge(x1_ready, n + 1)
                pool.wait_ge(tok_ready, n * 3 + 2)
                for b in range(B):
                    last = pool.tensor_tensor(x1[:, b], x1[:, b], b_dn[:], ALU.add)
                last.then_inc(x1b_ready, 1)

            def residual(n):
                pool.wait_ge(y_ready, n + 1)
                pool.tensor_tensor(x2_c[:], x2_c[:], z_c[:], ALU.add).then_inc(xy_ready, 1)

            def ffn_bias_c(n):
                pool.wait_ge(tok_c_ready, n * 2 + 2)
                for b in range(B):
                    last = pool.tensor_tensor(z_c[:, b], z_c[:, b], b_dn[:], ALU.add)
                last.then_inc(x3b_ready, 1)

            def til(n):
                pool.wait_ge(tm_ready, n + 1)
                pool.wait_ge(lanes_in, n * 48 + 48)
                vc = v_l[:].rearrange("p v (c i) -> p c v i", i=C)
                for j in range(C):
                    for i in range(j, C):
                        dst = first[:, :, :, i, DK] if j == 0 else tmp_v[:, :, :, i]
                        last = pool.tensor_tensor(dst, tm[:, :, i, j:j + 1].broadcast_to([128, NC_, VR]),
                                                  vc[:, :, :, j], ALU.mult)
                    if j:
                        done(last)
                        last = pool.tensor_tensor(first[:, :, :, j:C, DK], first[:, :, :, j:C, DK],
                                                  tmp_v[:, :, :, j:C], ALU.add)
                    done(last)
                pool.nop().then_inc(til_ready, 1)

            def body(t, scan=True, following=True):
                nonlocal steps
                steps = 0
                if scan:
                    first_terms(t)
                if following:
                    ffn_bias(t + 1)
                if scan:
                    residual(t)
                    ffn_bias_c(t)
                if following:
                    til(t + 1)
                pool.sem_clear(gstep)

            body(-1, scan=False)
            with pool.Fori(0, NB - 2) as t:
                body(t)
            body(NB - 2)
            body(NB - 1, following=False)

        @block.scalar
        def _(act):
            nc.scalar.preload_act_table_set(LOG_EXP_SET)
            act.dma_start(wqkv_a[:], a["wqkv_a"].rearrange("(k p) n -> p k n", p=128)).then_inc(early_in, 16)
            act.dma_start(q_up.rearrange("p (k n) -> p k n", k=KT),
                          a["q_up"].rearrange("(k p) n -> p k n", p=128)).then_inc(quant_in, 16)
            act.dma_start(q_dn.rearrange("p (k n) -> p k n", k=FT),
                          a["q_dn"].rearrange("(k p) n -> p k n", p=128)).then_inc(quant_in, 16)
            for half in range(128 // QBLK):
                rows = slice(half * QBLK, (half + 1) * QBLK)
                for scales, name, tiles in ((s_up, "s_up", KT), (s_dn, "s_dn", FT)):
                    src = a[name].rearrange("(k h) n -> h k n", h=128 // QBLK)[half:half + 1]
                    act.dma_start(scales[rows].rearrange("p (k n) -> p k n", k=tiles),
                                  src.broadcast_to([QBLK, tiles, src.shape[2]])).then_inc(quant_in, 16)
            for dst, src in [(lora_a_up, a["lora_a_up"]), (lora_b_dn, a["lora_b_dn"]),
                             (lora_b_up, a["lora_b_up"]), (lora_a_dn, a["lora_a_dn"])]:
                act.dma_start(dst, src).then_inc(lora_in, 16)

            steps = 0

            def done(ins):
                nonlocal steps
                steps += 1
                ins.then_inc(astep, 1)
                act.wait_ge(astep, steps)

            def rsqrt(dst, src, tmp, e, scale):
                done(act.activation(tmp, src, ACT.Ln, bias=eps[:, e:e + 1], scale=scale))
                return act.activation(dst, tmp, ACT.Exp, scale=-0.5)

            def norm_next(n):
                act.wait_ge(vars_next, n + 1)
                rsqrt(rstd[:], mv[:, :, 1], lnv[:], 0, 1.0).then_inc(rstd_next, 1)

            def turn_next(n):
                act.wait_ge(turned_next, n + 1)
                act.copy(feat_c[:].rearrange("p k b t -> p (k b t)"), bank[7][:]).then_inc(feat_next, 1)

            def norm_a(n, k):
                act.wait_ge(vars_ready, n * 2 + k)
                rsqrt(rstd[:], mv[:, :, 1], lnv[:], 0, 1.0).then_inc(rstd_ready, 1)

            def turn_a(n, k):
                act.wait_ge(turned, n * 3 + k)
                act.copy(feat[:].rearrange("p k b t -> p (k b t)"), bank[0][:]).then_inc(feat_ready, 1)

            def turn_c(n, k):
                act.wait_ge(turned_c, n * 2 + k)
                act.copy(feat_c[:].rearrange("p k b t -> p (k b t)"), bank[7][:]).then_inc(feat_c_ready, 1)

            def hold(n):
                act.wait_ge(z_ready, n + 1)
                act.wait_ge(out_stored, n * 16 + 16)
                act.copy(z_c[:], z[:])
                act.copy(x2_c[:], x2[:]).then_inc(held, 1)

            def piece_first(n, s, after_p):
                act.wait_ge(qkv_done, n * 3 + s + 1)
                if after_p and s == 0:
                    act.wait_ge(lanes_out, (n - 1) * 96)
                    act.wait_ge(prod_ready, (n - 1) * HH)
                act.copy(pieces[:, s, 0], bank[6 + s][:]).then_inc(piece1, 1)

            def piece_second(n):
                for s in range(2):
                    act.wait_ge(rest1, n * 2 + s + 1)
                    act.copy(pieces[:, s, 1], rest[:, s]).then_inc(piece2, 1)

            def values_out(n):
                act.wait_ge(qkv_done, n * 3 + 3)
                for b in range(B):
                    last = act.copy(v_ext[:, b, 1, :, 0:DK],
                                    bank[2][:, b * D:(b + 1) * D].rearrange("p (h d) -> p h d", d=DK))
                last.then_inc(v_done, 1)

            def max_rows(n, g):
                act.wait_ge(m_turned, n * NG + g + 1)
                act.copy(m_rows[:, g % 2], bank_b[0:3 * HPH, 0:W]).then_inc(m_copied, 1)

            def exp_of(n, g, v):
                u = g * UPG + v
                act.wait_ge(scores2, n * N_UNITS + u + 1)
                act.activation(probs[:, u % 3], score_bank[u % 3][:], ACT.Exp,
                               scale=float(DK) ** -0.5).then_inc(exp_done, 1)

            def out_rows(n, g):
                act.wait_ge(pv_done, n * NG + g + 1)
                if g:
                    act.wait_ge(o_turned, n * NG + g)
                act.copy(o_rows, bank[5][:]).then_inc(o_copied, 1)

            def attention(n, after_c, front):
                for pair in range(NG // 2):
                    g = 2 * pair
                    max_rows(n, g)
                    for v in range(UPG):
                        exp_of(n, g, v)
                        if v == 0:
                            max_rows(n, g + 1)
                        if v == 5 and pair and front:
                            norm_next(n + 1)
                    out_rows(n, g)
                    for v in range(UPG):
                        exp_of(n, g + 1, v)
                        if v == 6 and pair and front:
                            turn_next(n + 1)
                    out_rows(n, g + 1)
                done(act.copy(v_ext[:, :, 0, :, 0:DK], v_ext[:, :, 1, :, 0:DK]))
                if front:
                    piece_first(n + 1, 0, after_c)
                turn_a(n, 1)
                if front:
                    piece_first(n + 1, 1, after_c)
                    values_out(n + 1)

            def ffn_start(n):
                norm_a(n, 1)
                turn_a(n, 2)

            def ffn(n, lo, hi):
                for i in range(lo, hi):
                    act.wait_ge(hid_done, n * FT + i + 1)
                    act.activation(hid[:, i, :], bank[1 + i % 2][:, 0:BT], ACT.Relu,
                                   bias=b_up[:, i:i + 1]).then_inc(hid_ready, 1)

            def norms_z(n):
                norm_a(n, 2)
                act.wait_ge(z_ready, n + 1)
                for b in range(B):
                    done(act.activation(sq[:], z[:, b], ACT.Square, accum_out=lnv[:, b:b + 1]))
                rsqrt(rstd[:], lnv[:], lnt[:], 1, 1.0 / D).then_inc(sq_rstd, 1)

            def beta_exp_of(n):
                act.wait_ge(projb_done, n * 4 + 1)
                act.activation(beta_l[:], bank[4][:, 0:W], ACT.Exp, scale=-1.0).then_inc(beta_exp, 1)

            def raw_of(n, s):
                act.wait_ge(projb_done, n * 4 + s + 2)
                for hh in range(HH):
                    last = act.copy(raw[:, s, hh, :, TAPS - 1:],
                                    bank[1 + s][:, hh * BT:(hh + 1) * BT].rearrange("p (b t) -> p b t", b=B))
                last.then_inc(raw_ready, 1)

            def silu_twice(n, s):
                act.wait_ge(conv_ready, n * 3 + s + 1)
                done(act.activation(conv[:, s], conv[:, s], ACT.Silu))
                act.activation(conv[:, s], conv[:, s], ACT.Silu).then_inc(silu_ready, 1)
                if s < 2:
                    act.wait_ge(silu_ready, n * 3 + s + 1)
                    act.activation(sqk[:, s], conv[:, s], ACT.Square).then_inc(sq_ready, 1)

            def l2_norms(n):
                for s in range(2):
                    act.wait_ge(ss_done, n * 2 + s + 1)
                    done(act.activation(sqk[:, s], bank[1 + s][:], ACT.Relu, bias=eps[:, 2:3]))
                    done(act.activation(sqk[:, s], sqk[:, s], ACT.Ln, bias=eps[:, 3:4]))
                    act.activation(sqk[:, s], sqk[:, s], ACT.Exp, scale=-0.5).then_inc(rn_ready, 1)

            def pairs_out(n):
                act.wait_ge(pairs_done, n + 1)
                act.copy(pair_l.rearrange("p a c -> p (a c)"), bank[3][:]).then_inc(pairs_copied, 1)

            def output_squares(n):
                act.wait_ge(o_in, n * 32 + 32)
                act.activation(o_n, o_t, ACT.Square).then_inc(osq_ready, 1)

            def output_rstd(n):
                act.wait_ge(oss_done, n + 1)
                rsqrt(rs_o[:], bank[6][:, 0:BT], rs_o[:], 1, 1.0 / D).then_inc(ors_ready, 1)

            def y_norm(n):
                act.wait_ge(y_ready, n + 1)
                for b in range(B):
                    done(act.activation(sq[:], z_c[:, b], ACT.Square, accum_out=lnv_c[:, b:b + 1]))
                rsqrt(rstd_c[:], lnv_c[:], lnt_c[:], 1, 1.0 / D).then_inc(rstd_c_ready, 1)

            def gate_of(n, i):
                m = inner[i][1]
                act.wait_ge(gu_done, n * IT + i + 1)
                if i >= 2:
                    act.wait_ge(act_ready, n * IT + i - 1)
                act.activation(gate[0:m, i % 2], bank[6 + i % 2][0:m, 0:BT], ACT.Silu).then_inc(gate_ready, 1)

            def norm_c(n):
                act.wait_ge(var_c_ready, n + 1)
                rsqrt(rstd_c[:], mv_c[:, :, 1], lnv_c[:], 0, 1.0).then_inc(rstd_c_ready, 1)

            def ffn_c(n, lo, hi):
                for i in range(lo, hi):
                    act.wait_ge(hid_c_done, n * FT + i + 1)
                    if i == HALF:
                        act.wait_ge(ffn_c_half, n + 1)
                    act.activation(hid_c[:, i % HALF, :], bank[6 + i % 2][:, 0:BT], ACT.Relu,
                                   bias=b_up[:, i:i + 1]).then_inc(hid_c_ready, 1)

            def body(t, scan=True, following=True, front=True):
                nonlocal steps
                steps = 0
                n = t + 1
                if scan:
                    hold(t)
                if following:
                    attention(n, scan, front)
                    ffn_start(n)
                    ffn(n, 0, 2)
                if front:
                    piece_second(t + 2)
                if following:
                    ffn(n, 2, FT)
                if scan:
                    output_squares(t)
                    output_rstd(t)
                if following:
                    norms_z(n)
                    turn_a(n, 3)
                    beta_exp_of(n)
                if scan:
                    y_norm(t)
                if following:
                    for s in range(3):
                        raw_of(n, s)
                if scan:
                    turn_c(t, 1)
                if following:
                    silu_twice(n, 0)
                if scan:
                    gate_of(t, 0)
                if following:
                    silu_twice(n, 1)
                if scan:
                    gate_of(t, 1)
                if following:
                    silu_twice(n, 2)
                if scan:
                    for i in range(2, IT):
                        gate_of(t, i)
                nc.scalar.preload_act_table_set(LOG_EXP_SET)
                if following:
                    l2_norms(n)
                if scan:
                    norm_c(t)
                if following:
                    pairs_out(n)
                if scan:
                    turn_c(t, 2)
                    ffn_c(t, 0, FT)
                act.sem_clear(astep)

            act.wait_ge(early_in, 16 * (len(early) + 1))
            norm_next(0)
            turn_next(0)
            piece_first(0, 0, False)
            piece_first(0, 1, False)
            act.wait_ge(zeroed, 7)
            values_out(0)
            piece_second(0)
            act.wait_ge(weights_in, 16 * (len(plain) + IT))
            act.sem_clear(astep)
            body(-1, scan=False)
            with act.Fori(0, NB - 2) as t:
                body(t)
            body(NB - 2, front=False)
            body(NB - 1, following=False, front=False)

        AHEAD = 3
        MAX_AT = [4 * AHEAD + k // PER for k in range(2 * UPG)] + [61 + k // PER for k in range(2 * UPG)]
        PIECES_AT = [(g, MAX_AT[(g + 1) * UPG - 1] + 1) for g in range(NG)]
        OUT_AT, NEXT_AT = (48, 60), (86, 94)
        CUTS = (25, 29, NC_)

        @block.vector
        def _(dve):
            steps = 0

            def mark(ins):
                nonlocal steps
                steps += 1
                ins.then_inc(vstep, 1)
                return steps

            def done(ins):
                dve.wait_ge(vstep, mark(ins))

            def flat(x):
                return x[:].rearrange("p b d -> p (b d)")

            def variance(src, st, m_v, ready):
                for b in range(B):
                    last = dve.bn_stats(st[:, b], src[:, b])
                done(last)
                for b in range(B):
                    last = dve.bn_aggr(m_v[:, b], st[:, b])
                last.then_inc(ready, 1)

            def subtract_scale(src, dst, m_v, rs, rs_sem, rs_count):
                dve.wait_ge(rs_sem, rs_count)
                for b in range(B):
                    last = dve.tensor_scalar(dst[:, b], src[:, b], m_v[:, b, 0:1], rs[:, b:b + 1],
                                             ALU.subtract, ALU.mult)
                return last

            def normalise(src, dst, st, m_v, rs, ready, rs_sem, rs_count):
                variance(src, st, m_v, ready)
                return subtract_scale(src, dst, m_v, rs, rs_sem, rs_count)

            def norm_next_vars(n):
                dve.wait_ge(x_loaded, n * 16 + 16)
                variance(x_next, stats, mv, vars_next)

            def norm_next_apply(n):
                subtract_scale(x_next, tok_next, mv, rstd, rstd_next, n + 1).then_inc(tok_next_ready, 1)

            def rests_first(n):
                for s in range(2):
                    dve.wait_ge(piece1, n * 2 + s + 1)
                    dve.tensor_tensor(rest[:, s], bank[6 + s][:], pieces[:, s, 0], ALU.subtract).then_inc(rest1, 1)

            def rests_second(n):
                for s in range(2):
                    dve.wait_ge(piece2, n * 2 + s + 1)
                    dve.tensor_tensor(pieces[:, s, 2], rest[:, s], pieces[:, s, 1], ALU.subtract).then_inc(piece3, 1)

            def max_unit(n, u):
                g, v = divmod(u, UPG)
                dve.wait_ge(scores1, n * N_UNITS + u + 1)
                dve.tensor_reduce(mx[:, g, 2 * v:2 * v + 2],
                                  bank[1 + u % 2][:, 0:2 * SPAN].rearrange("p (h k) -> p h k", h=2),
                                  AX.X, ALU.max).then_inc(max_done, 1)

            def max_piece(n, g, step, before):
                nm = nmx[:, g]
                if step == 0:
                    dve.wait_ge(max_done, n * N_UNITS + (g + 1) * UPG)
                    return mark(dve.tensor_scalar(nm, mx[:, g], -1.0, None, ALU.mult))
                dve.wait_ge(vstep, before)
                if step == 1:
                    return mark(dve.tensor_copy(mpieces[:, g, 0], nm))
                if step == 2:
                    return mark(dve.tensor_tensor(nm, nm, mpieces[:, g, 0], ALU.subtract))
                if step == 3:
                    return mark(dve.tensor_copy(mpieces[:, g, 1], nm))
                dve.tensor_tensor(mpieces[:, g, 2], nm, mpieces[:, g, 1], ALU.subtract).then_inc(mpieces_ready, 1)
                return None

            def out_scale(n, g):
                b, hh = divmod(g, HH)
                dve.wait_ge(o_turned, n * NG + g + 1)
                ov = bank[0][:].rearrange("p (h e) -> p h e", e=32)
                done(dve.reciprocal(rden[:], ov[:, :, DK]))
                dve.tensor_tensor(
                    tok[:, b, hh * 128:(hh + 1) * 128].rearrange("p (h d) -> p h d", d=DK), ov[:, :, 0:DK],
                    rden[:].rearrange("p (h o) -> p h o", o=1).broadcast_to([128, HPH, DK]),
                    ALU.mult).then_inc(o_scaled, 1)

            def first_residual(n):
                dve.wait_ge(wo_done, n + 1)
                dve.wait_ge(x_again, n * 16 + 16)
                done(dve.tensor_tensor(flat(x1), bank[1][:], flat(x_in), ALU.add))
                dve.nop().then_inc(x1_ready, 1)
                normalise(x1, tok, stats, mv, rstd, vars_ready, rstd_ready, n * 2 + 1).then_inc(tok_ready, 1)

            def second_residual(n, after_c):
                dve.wait_ge(ffn_done, n + 1)
                dve.wait_ge(x1b_ready, n + 1)
                if after_c:
                    dve.wait_ge(held, n)
                done(dve.tensor_tensor(flat(x2), bank[3][:], flat(x1), ALU.add))
                dve.nop().then_inc(x_used, 1)
                variance(x2, stats, mv, vars_ready)

            def z_of(n):
                subtract_scale(x2, z, mv, rstd, rstd_ready, n * 2 + 2).then_inc(z_ready, 1)

            def z_tok(n):
                dve.wait_ge(sq_rstd, n + 1)
                for b in range(B):
                    last = dve.tensor_scalar(tok[:, b], z[:, b], rstd[:, b:b + 1], None, ALU.mult)
                last.then_inc(tok_ready, 1)

            def convolve(n, s, front):
                dve.wait_ge(raw_ready, n * 3 + s + 1)
                if front and s == 0:
                    dve.wait_ge(pieces_out, n * 144 + 288)
                for tap in range(TAPS):
                    for hh in range(HH):
                        src = raw[:, s, hh, :, tap:tap + W]
                        dst = conv[:, s, hh * BT:(hh + 1) * BT].rearrange("p (b t) -> p b t", b=B)
                        w = conv_w[:, s, hh, tap:tap + 1]
                        if tap == 0:
                            last = dve.tensor_scalar(dst, src, w, None, ALU.mult)
                        else:
                            last = dve.scalar_tensor_tensor(out=dst, in0=src, scalar=w, in1=dst,
                                                            op0=ALU.mult, op1=ALU.add)
                    if tap < TAPS - 1:
                        done(last)
                last.then_inc(conv_ready, 1)

            def keep_taps():
                dve.tensor_copy(raw[:, :, :, :, 0:TAPS - 1].rearrange("p s h b t -> p (s h b) t"),
                                raw[:, :, :, :, W:W + TAPS - 1].rearrange("p s h b t -> p (s h b) t"))

            def beta_of(n):
                dve.wait_ge(beta_exp, n + 1)
                done(dve.tensor_scalar(beta_l[:], beta_l[:], 1.0, None, ALU.add))
                dve.reciprocal(beta_l[:], beta_l[:]).then_inc(beta_ready, 1)

            def units(n):
                for s in range(2):
                    dve.wait_ge(rn_ready, n * 2 + s + 1)
                    dve.tensor_tensor(conv[:, s], conv[:, s], sqk[:, s], ALU.mult).then_inc(unit_ready, 1)

            def products(n, hh):
                if hh == 0:
                    dve.wait_ge(unit_ready, n * 2 + 2)
                kk = conv[:, 1, hh * BT:(hh + 1) * BT].rearrange("p (b c i) -> p b i c", b=B, i=C)
                qq = conv[:, 0, hh * BT:(hh + 1) * BT].rearrange("p (b c i) -> p b i c", b=B, i=C)
                at = 0
                for left, lo in ((kk, 1), (qq, 0)):
                    for i in range(lo, C):
                        m = i if lo else i + 1
                        for b in range(B):
                            last = dve.tensor_tensor(prodk[:, hh, b, at:at + m, :], kk[:, b, 0:m],
                                                     left[:, b, i:i + 1].broadcast_to([128, m, NC_]), ALU.mult)
                        at += m
                last.then_inc(prod_ready, 1)

            def inverse_head(n):
                dve.wait_ge(pairs_copied, n + 1)
                dve.wait_ge(beta_ready, n + 1)
                bc = beta_l[:].rearrange("p (c i) -> p c i", i=C)
                for i in range(C):
                    dve.tensor_scalar(tm[:, :, i, i], bc[:, :, i], -1.0, None, ALU.mult)
                for at, (i, j) in enumerate(PAIRS_K):
                    dve.scalar_tensor_tensor(out=pair_l[:, at, :], in0=pair_l[:, at, :], scalar=-1.0,
                                             in1=bc[:, :, i], op0=ALU.mult, op1=ALU.mult)
                for at, (i, j) in enumerate(PAIRS_Q):
                    dve.tensor_copy(mm_[:, i, j, :], pair_l[:, NPK + at, :])
                done(dve.tensor_copy(state[:, 0, :, :, C], state[:, NC_, :, :, C]))

            def inverse_rows(n):
                for i in range(1, C):
                    for j in reversed(range(i)):
                        at = PAIRS_K.index((i, j))
                        g = pair_l[:, at, :].rearrange("p (c o) -> p c o", o=1).broadcast_to([128, NC_, j + 1])
                        row = tm[:, :, i, 0:j + 1]
                        if j == i - 1:
                            done(dve.tensor_tensor(row, g, tm[:, :, j, 0:j + 1], ALU.mult))
                        else:
                            done(dve.tensor_tensor(tmp_t[:, :, 0:j + 1], g, tm[:, :, j, 0:j + 1], ALU.mult))
                            done(dve.tensor_tensor(row, row, tmp_t[:, :, 0:j + 1], ALU.add))
                dve.nop().then_inc(tm_ready, 1)

            def til_keys(n):
                dve.wait_ge(lanes_in, n * 48 + 48)
                kc = k_l[:].rearrange("p k (c i) -> p c i k", i=C)
                for j in range(C):
                    for i in range(j, C):
                        last = dve.tensor_tensor(
                            (k_til if j == 0 else tmp_k)[:, :, i, :],
                            tm[:, :, i, j:j + 1].broadcast_to([128, NC_, DK]), kc[:, :, j, :], ALU.mult)
                    done(last)
                    if j:
                        done(dve.tensor_tensor(k_til[:, :, j:C, :], k_til[:, :, j:C, :],
                                               tmp_k[:, :, j:C, :], ALU.add))

            def between(n, at, before, front):
                units = [u for u in range(N_UNITS) if MAX_AT[u] == at]
                for k in range(PER):
                    for g, start in PIECES_AT:
                        step = PER * (at - start) + k
                        if 0 <= step < 5:
                            before = max_piece(n, g, step, before)
                    if k < len(units):
                        max_unit(n, units[k])
                if at == OUT_AT[0]:
                    out_scale(n, 0)
                if at == OUT_AT[1]:
                    out_scale(n, 1)
                if front and at == NEXT_AT[0]:
                    norm_next_vars(n + 1)
                if front and at == NEXT_AT[1]:
                    norm_next_apply(n + 1)
                return before

            def scan(n, lo, hi, following, front):
                kc = k_l[:].rearrange("p k (c i) -> p c k i", i=C)
                if lo == 0:
                    dve.wait_ge(til_ready, n + 1)
                other = None
                for c in range(lo, hi):
                    at = mark(dve.tensor_tensor(
                        first[:, c, :, :, 0:DK],
                        state[:, c, :, :, C].rearrange("p v (o k) -> p v o k", o=1).broadcast_to([128, VR, C, DK]),
                        k_til[:, c:c + 1].broadcast_to([128, VR, C, DK]), ALU.mult))
                    if following:
                        other = between(n + 1, 4 * c, other, front)
                    dve.wait_ge(vstep, at)
                    at = mark(dve.tensor_reduce(u_l[:, c], first[:, c], AX.X, ALU.add))
                    if following:
                        other = between(n + 1, 4 * c + 1, other, front)
                    dve.wait_ge(vstep, at)
                    at = mark(dve.tensor_tensor(
                        state[:, c, :, :, 0:C],
                        u_l[:, c].rearrange("p v (o i) -> p v o i", o=1).broadcast_to([128, VR, DK, C]),
                        kc[:, c:c + 1].broadcast_to([128, VR, DK, C]), ALU.mult))
                    if following:
                        other = between(n + 1, 4 * c + 2, other, front)
                    dve.wait_ge(vstep, at)
                    at = mark(dve.tensor_reduce(state[:, c + 1, :, :, C], state[:, c], AX.X, ALU.add))
                    if following:
                        other = between(n + 1, 4 * c + 3, other, front)
                    dve.wait_ge(vstep, at)
                    if (c + 1) * (DK + 1) >= NC_ // 2 * (DK + C) > c * (DK + 1):
                        dve.nop().then_inc(scanned, 1)
                return other

            def reduce_terms(half):
                cs = slice(half * NC_ // 2, (half + 1) * NC_ // 2)
                return dve.tensor_reduce(o_l[:, :, cs], out_terms, AX.X, ALU.add)

            def half_outputs(n):
                dve.wait_ge(terms_ready, n + 1)
                done(reduce_terms(0))
                done(terms_of(dve, slice(NC_ // 2, NC_)))
                reduce_terms(1).then_inc(o_ready, 1)

            def output_norm(n):
                dve.wait_ge(ors_ready, n + 1)
                dve.wait_ge(oss_done, n + 1)
                for hh in range(HH):
                    last = dve.scalar_tensor_tensor(out=o_n[:, hh].rearrange("p b t -> p (b t)"),
                                                    in0=o_t[:, hh].rearrange("p b t -> p (b t)"), scalar=-1.0,
                                                    in1=rs_o[:], op0=ALU.mult, op1=ALU.mult)
                last.then_inc(on_ready, 1)

            def y_of(n):
                dve.wait_ge(wout_done, n + 1)
                dve.wait_ge(held, n + 1)
                dve.tensor_tensor(flat(z_c), bank[6][:], flat(z_c), ALU.add).then_inc(y_ready, 1)

            def y_tok(n):
                dve.wait_ge(rstd_c_ready, n * 2 + 1)
                dve.wait_ge(y_ready, n + 1)
                for b in range(B):
                    last = dve.tensor_scalar(tok_c[:, b], z_c[:, b], rstd_c[:, b:b + 1], None, ALU.mult)
                last.then_inc(tok_c_ready, 1)

            def act_of(n, i):
                m = inner[i][1]
                dve.wait_ge(gate_ready, n * IT + i + 1)
                if i == HALF:
                    dve.wait_ge(mlp_half, n + 1)
                dve.tensor_tensor(hid_c[0:m, i % HALF], bank[6 + i % 2][0:m, BT:2 * BT], gate[0:m, i % 2],
                                  ALU.mult).then_inc(act_ready, 1)

            def third_residual(n):
                dve.wait_ge(mlp_done, n + 1)
                dve.wait_ge(xy_ready, n + 1)
                for b in range(B):
                    last = dve.tensor_tensor(z_c[:, b], bank[4 + b][:, 0:D], x2_c[:, b], ALU.add)
                done(last)
                variance(z_c, stats_c, mv_c, var_c_ready)

            def third_apply(n):
                subtract_scale(z_c, tok_c, mv_c, rstd_c, rstd_c_ready, n * 2 + 2).then_inc(tok_c_ready, 1)

            def result(n):
                dve.wait_ge(ffn_c_done, n + 1)
                dve.wait_ge(x3b_ready, n + 1)
                for b in range(B):
                    last = dve.tensor_tensor(z_c[:, b], bank[4 + b][:, 0:D], z_c[:, b], ALU.add)
                last.then_inc(out_ready, 1)

            def body(t, has_scan=True, following=True, front=True):
                nonlocal steps
                steps = 0
                n = t + 1
                if has_scan:
                    scan(t, AHEAD, CUTS[0], following, front)
                else:
                    other = None
                    for at in range(4 * CUTS[0]):
                        other = between(n, at, other, front)
                if following:
                    out_scale(n, 2)
                if has_scan:
                    scan(t, CUTS[0], CUTS[1], False, False)
                if following:
                    out_scale(n, 3)
                    dve.wait_ge(o_scaled, n * 4 + 4)
                    dve.nop().then_inc(tok_ready, 1)
                if has_scan:
                    scan(t, CUTS[1], CUTS[2], False, False)
                if following:
                    first_residual(n)
                if front:
                    rests_first(t + 2)
                if has_scan:
                    half_outputs(t)
                if front:
                    rests_second(t + 2)
                if following:
                    second_residual(n, has_scan)
                if has_scan:
                    output_norm(t)
                if following:
                    z_of(n)
                if has_scan:
                    y_of(t)
                if following:
                    z_tok(n)
                    beta_of(n)
                if has_scan:
                    y_tok(t)
                if following:
                    convolve(n, 0, front)
                    convolve(n, 1, front)
                if has_scan:
                    act_of(t, 0)
                if following:
                    convolve(n, 2, front)
                    keep_taps()
                if has_scan:
                    act_of(t, 1)
                    act_of(t, 2)
                if has_scan:
                    act_of(t, 3)
                if has_scan:
                    for i in range(HALF, IT):
                        act_of(t, i)
                if following:
                    units(n)
                if following:
                    products(n, 0)
                if has_scan:
                    third_residual(t)
                if following:
                    products(n, 1)
                if has_scan:
                    third_apply(t)
                if following:
                    inverse_head(n)
                    inverse_rows(n)
                    til_keys(n)
                    scan(n, 0, AHEAD, False, False)
                if has_scan:
                    result(t)
                dve.sem_clear(vstep)

            dve.nop().then_inc(x_used, 1)
            dve.nop().then_inc(out_stored, 16)
            dve.wait_ge(early_in, 16 * (len(early) + 1))
            norm_next_vars(0)
            norm_next_apply(0)
            rests_first(0)
            rests_second(0)
            dve.wait_ge(zeroed, 7)
            dve.wait_ge(consts_in, 16 * len(consts))
            dve.wait_ge(pad_out, 16 * 3 * HH)
            dve.tensor_scalar(q_stack[:], q_stack[:], stack_cols[:, 0:1], None, ALU.add).then_inc(stack_init, 1)
            done(dve.memset(k_stack[:], 0.0))
            dve.tensor_scalar(k_stack[:], k_stack[:], stack_cols[:, 1:2], None, ALU.add).then_inc(stack_init, 1)
            dve.wait_ge(consts_in, 16 * len(consts))
            dve.tensor_copy(identb[:], ident[:])
            dve.tensor_copy(edge_mask[:], edge_mask_f[:])
            dve.tensor_copy(tri_mask[:], tri_mask_f[:]).then_inc(consts_cast, 1)
            dve.wait_ge(quant_in, 16 * (2 + 2 * (128 // QBLK)))
            dve.scalar_tensor_tensor(out=w_up[:].rearrange("p k n -> p (k n)"), in0=q_up, scalar=-7.5,
                                     in1=s_up, op0=ALU.add, op1=ALU.mult)
            dve.scalar_tensor_tensor(out=w_dn[:].rearrange("p k n -> p (k n)"), in0=q_dn, scalar=-7.5,
                                     in1=s_dn, op0=ALU.add, op1=ALU.mult).then_inc(dequantised, 1)
            dve.wait_ge(dequantised, 1)
            dve.wait_ge(lora_prod, 1)
            for k in range(KT):
                for c in range(2):
                    w = w_up[:, k, c * 512:(c + 1) * 512]
                    dve.tensor_tensor(w, w, bank[2 * k + c][:], ALU.add)
            for k in range(FT // 2):
                w = w_dn[:, 2 * k:2 * k + 2, :].rearrange("p a n -> p (a n)")
                dve.tensor_tensor(w, w, bank[4 + k][:], ALU.add).then_inc(lora_added, 1)
            dve.wait_ge(weights_in, 16 * (len(plain) + IT))
            for k in range(KT):
                for w, i in ((wqkv_b[:, k], 0), (wbeta[:, k], 0), (wout_b[:, k], 1), (wgu[:, k], 2)):
                    last = dve.tensor_scalar(w, w, norm_w[:, i, k:k + 1], None, ALU.mult)
            last.then_inc(weights_scaled, 1)
            dve.sem_clear(vstep)
            body(-1, has_scan=False)
            with dve.Fori(0, NB - 2) as t:
                body(t)
            body(NB - 2, front=False)
            body(NB - 1, following=False, front=False)

        @block.tensor
        def _(pe):
            f = feat[:].rearrange("p k b t -> p k (b t)")
            fc = feat_c[:].rearrange("p k b t -> p k (b t)")

            def turn(src, dst_bank):
                for k in range(KT):
                    for b in range(B):
                        at = (k * B + b) * W
                        last = pe.transpose(dst_bank[:, at:at + W], src[:, b, k * 128:(k + 1) * 128], ident[:])
                return last

            def turn_a(n, k):
                pe.wait_ge(tok_ready, n * 3 + k)
                turn(tok, bank[0]).then_inc(turned, 1)
                pe.wait_ge(feat_ready, n * 3 + k)

            def turn_next(n):
                pe.wait_ge(tok_next_ready, n + 1)
                turn(tok_next, bank[7]).then_inc(turned_next, 1)

            def turn_c(n, k):
                pe.wait_ge(tok_c_ready, n * 2 + k)
                turn(tok_c, bank[7]).then_inc(turned_c, 1)

            def to_tokens(dst, src, w, tiles):
                for b in range(B):
                    for k, m in tiles:
                        last = pe.matmul(dst[:, b * D:(b + 1) * D], src[0:m, k, b * W:(b + 1) * W],
                                         w[0:m, k, :], start=(k == 0), stop=(k == tiles[-1][0]))
                return last

            def to_tokens_c(w, tiles, final):
                for b in range(B):
                    for k, m in tiles:
                        last = pe.matmul(bank[4 + b][:, 0:D], hid_c[0:m, k % HALF, b * W:(b + 1) * W],
                                         w[0:m, k, :], start=(k == 0), stop=(k == final))
                return last

            def queries_keys(n, s):
                if s == 0:
                    pe.wait_ge(feat_next, n + 1)
                for hh in range(HH):
                    for k in range(KT):
                        last = pe.matmul(bank[6 + s][:, hh * BT:(hh + 1) * BT],
                                         wqkv_a[:, k, s * D + hh * 128:s * D + (hh + 1) * 128],
                                         fc[:, k], start=(k == 0), stop=(k == KT - 1))
                last.then_inc(qkv_done, 1)

            def values_in(n, b):
                for k in range(KT):
                    last = pe.matmul(bank[2][:, b * D:(b + 1) * D], feat_c[:, k, b, :],
                                     wqkv_a[:, k, 2 * D:3 * D], start=(k == 0), stop=(k == KT - 1))
                if b == B - 1:
                    last.then_inc(qkv_done, 1)

            def scores_max(n, g, lo, hi):
                if lo == 0:
                    pe.wait_ge(stacks_in[g % 2], (n * (NG // 2) + g // 2 + 1) * 16 * STACK_DMAS)
                for v in range(lo, hi):
                    u = g * UPG + v
                    if u >= 2:
                        pe.wait_ge(max_done, n * N_UNITS + u - 1)
                    pb = bank[1 + u % 2][:, 0:2 * SPAN]
                    edges = pb.rearrange("p (h k) -> p h k", h=2)
                    for e in range(2):
                        pe.matmul(edges[:, :, e * W:e * W + SUB], identb[:],
                                  edge_mask[:, e * SUB:(e + 1) * SUB].rearrange("p (o s) -> p o s", o=1)
                                  .broadcast_to([128, 2, SUB]), start=(e == 0), stop=False, skip_group_check=True)
                    for hp in range(2):
                        for s in range(W // SUB):
                            last = pe.matmul(pb[s * SUB:(s + 1) * SUB, hp * SPAN:(hp + 1) * SPAN],
                                             q_stack[:, g % 2, 2 * v + hp, s * SUB:(s + 1) * SUB],
                                             k_stack[:, g % 2, 2 * v + hp, s * SUB:s * SUB + SPAN],
                                             start=False, stop=True, skip_group_check=True)
                    last.then_inc(scores1, 1)

            def turn_max(n, g):
                pe.wait_ge(mpieces_ready, n * NG + g + 1)
                if g % 2:
                    pe.wait_ge(m_copied, n * NG + g)
                elif g:
                    pe.wait_ge(o_scaled, n * NG + g)
                pe.transpose(bank_b[0:5 * HPH, 0:W], mpieces[:, g].rearrange("p j h -> p (j h)"),
                             identb[:]).then_inc(m_turned, 1)

            def scores(n, u):
                g, v = divmod(u, UPG)
                if v == 0:
                    pe.wait_ge(m_in[g % 2], (n * (NG // 2) + g // 2 + 1) * 48)
                if u >= 3:
                    pe.wait_ge(exp_done, n * N_UNITS + u - 2)
                pb = score_bank[u % 3]
                pe.matmul(pb[:], identb[:], tri_mask[:].rearrange("p (o t) -> p o t", o=1)
                          .broadcast_to([128, 2, 2 * W]), start=True, stop=False, skip_group_check=True)
                for hp in range(2):
                    for kb in range(2):
                        at = (hp * 2 + kb) * W
                        last = pe.matmul(pb[:, at:at + W], k_stack[:, g % 2, 2 * v + hp, kb * W:(kb + 1) * W],
                                         q_stack[:, g % 2, 2 * v + hp, :], start=False, stop=True,
                                         skip_group_check=True)
                last.then_inc(scores2, 1)

            def values(n, u):
                g, v = divmod(u, UPG)
                pe.wait_ge(exp_done, n * N_UNITS + u + 1)
                if v == 0 and g:
                    pe.wait_ge(o_copied, n * NG + g)
                for hp in range(2):
                    b, h = divmod(2 * u + hp, H)
                    row, col = 32 * (h % 4), (h % HPH) // 4 * W
                    for kb in range(2):
                        last = pe.matmul(bank[5][row:row + VE, col:col + W], v_ext[:, b, kb, h, :],
                                         probs[:, u % 3, (hp * 2 + kb) * W:(hp * 2 + kb + 1) * W],
                                         start=(kb == 0), stop=(kb == 1))
                if v == UPG - 1:
                    last.then_inc(pv_done, 1)

            def turn_out(n, g):
                pe.wait_ge(o_copied, n * NG + g + 1)
                if g % 2 == 0:
                    pe.wait_ge(m_copied, n * NG + g + 2)
                else:
                    pe.wait_ge(o_scaled, n * NG + g)
                for j in range(4):
                    last = pe.transpose(bank[0][:, j * W:(j + 1) * W], o_rows[:, j * W:(j + 1) * W], ident[:])
                last.then_inc(o_turned, 1)

            def attention(n, after_c, front):
                for pair in range(NG // 2):
                    g = 2 * pair
                    if pair == 0:
                        pe.wait_ge(pad_in, 64 if after_c else 32)
                    scores_max(n, g, 0, UPG)
                    scores_max(n, g + 1, 0, MAX_TURN_AT)
                    turn_max(n, g)
                    scores_max(n, g + 1, MAX_TURN_AT, UPG)
                    if pair == 0:
                        pe.wait_ge(v_done, n + 1)
                        if after_c:
                            pe.wait_ge(out_stored, n * 16)
                    u0, u1 = 2 * pair * UPG, (2 * pair + 2) * UPG
                    scores(n, u0)
                    turn_max(n, g + 1)
                    scores(n, u0 + 1)
                    for u in range(u0 + 1, u1 + 1):
                        if u + 1 < u1:
                            scores(n, u + 1)
                        values(n, u - 1)
                        if u == u0 + UPG + 2:
                            turn_out(n, g)
                        if u == u0 + UPG + 6 and pair and front:
                            turn_next(n + 1)
                    if pair and front:
                        queries_keys(n + 1, 0)
                    turn_out(n, g + 1)
                    if pair and front:
                        queries_keys(n + 1, 1)
                pe.wait_ge(tok_ready, n * 3 + 1)
                turn(tok, bank[0]).then_inc(turned, 1)
                if front:
                    values_in(n + 1, 0)
                pe.wait_ge(feat_ready, n * 3 + 1)
                to_tokens(bank[1], f, wo_a, [(k, 128) for k in range(KT)]).then_inc(wo_done, 1)
                if front:
                    values_in(n + 1, 1)

            def ffn_up(n, lo, hi, front):
                if lo == 0:
                    turn_a(n, 2)
                    pe.wait_ge(x1_ready, n + 1)
                    if front:
                        pe.wait_ge(v_done, n + 2)
                for i in range(lo, hi):
                    if i >= 2:
                        pe.wait_ge(hid_ready, n * FT + i - 1)
                    for k in range(KT):
                        last = pe.matmul(bank[1 + i % 2][:, 0:BT], w_up[:, k, i * 128:(i + 1) * 128],
                                         f[:, k], start=(k == 0), stop=(k == KT - 1))
                    last.then_inc(hid_done, 1)

            def ffn_down(n):
                pe.wait_ge(hid_ready, n * FT + FT)
                to_tokens(bank[3], hid, w_dn, [(k, 128) for k in range(FT)]).then_inc(ffn_done, 1)

            def beta_in(n):
                for b in range(B):
                    for k in range(KT):
                        last = pe.matmul(bank[4][:, 0:W], wbeta[:, k, b, :], feat[:, k, b, :],
                                         start=(b == 0 and k == 0), stop=(b == B - 1 and k == KT - 1))
                last.then_inc(projb_done, 1)

            def delta_in(n):
                for s in range(3):
                    for hh in range(HH):
                        for k in range(KT):
                            last = pe.matmul(bank[1 + s][:, hh * BT:(hh + 1) * BT],
                                             wqkv_b[:, k, s * D + hh * 128:s * D + (hh + 1) * 128],
                                             f[:, k], start=(k == 0), stop=(k == KT - 1))
                    last.then_inc(projb_done, 1)

            def square_sums(n):
                for s in range(2):
                    pe.wait_ge(raw_ready, n * 3 + s + 1)
                    pe.wait_ge(sq_ready, n * 2 + s + 1)
                    pe.matmul(bank[1 + s][:], head_sum[:], sqk[:, s], start=True, stop=True).then_inc(ss_done, 1)

            def pairs(n):
                pe.wait_ge(raw_ready, n * 3 + 3)
                for hh in range(HH):
                    pe.wait_ge(prod_ready, n * HH + hh + 1)
                    for b in range(B):
                        g = b * HH + hh
                        last = pe.matmul(bank[3][:], to_lanes[:, g], prodk[:, hh, b].rearrange("p a c -> p (a c)"),
                                         start=(hh == 0 and b == 0), stop=(hh == HH - 1 and b == B - 1))
                last.then_inc(pairs_done, 1)

            def output_sums(n, front):
                pe.wait_ge(osq_ready, n + 1)
                if front:
                    pe.wait_ge(rest1, n * 2 + 6)
                for hh in range(HH):
                    last = pe.matmul(bank[6][:, 0:BT], ones[:], o_n[:, hh].rearrange("p b t -> p (b t)"),
                                     start=(hh == 0), stop=(hh == HH - 1))
                last.then_inc(oss_done, 1)

            def output_product(n):
                pe.wait_ge(on_ready, n + 1)
                pe.wait_ge(ors_ready, n + 1)
                to_tokens(bank[6], o_n.rearrange("p k b t -> p k (b t)"), wout_b,
                          [(k, 128) for k in range(KT)]).then_inc(wout_done, 1)

            def gate_up(n, i):
                m = inner[i][1]
                if i == 0:
                    pe.wait_ge(feat_c_ready, n * 2 + 1)
                    pe.wait_ge(y_ready, n + 1)
                if i >= 2:
                    pe.wait_ge(act_ready, n * IT + i - 1)
                for g in range(2):
                    for k in range(KT):
                        last = pe.matmul(bank[6 + i % 2][0:m, g * BT:(g + 1) * BT],
                                         wgu[:, k, g * INTER + 128 * i:g * INTER + 128 * i + m],
                                         fc[:, k], start=(k == 0), stop=(k == KT - 1))
                last.then_inc(gu_done, 1)

            def mlp_down(n, half, following):
                if half == 0:
                    if following:
                        pe.wait_ge(beta_exp, n + 2)
                    pe.wait_ge(act_ready, n * IT + HALF)
                    to_tokens_c(wdown_b, inner[:HALF], IT - 1).then_inc(mlp_half, 1)
                else:
                    pe.wait_ge(act_ready, n * IT + IT)
                    to_tokens_c(wdown_b, inner[HALF:], IT - 1).then_inc(mlp_done, 1)

            def ffn_c_up(n, lo, hi):
                for i in range(lo, hi):
                    if i == 0:
                        pe.wait_ge(feat_c_ready, n * 2 + 2)
                    if i >= 2:
                        pe.wait_ge(hid_c_ready, n * FT + i - 1)
                    for k in range(KT):
                        last = pe.matmul(bank[6 + i % 2][:, 0:BT], w_up[:, k, i * 128:(i + 1) * 128],
                                         fc[:, k], start=(k == 0), stop=(k == KT - 1))
                    last.then_inc(hid_c_done, 1)

            def ffn_c_down(n, half):
                pe.wait_ge(hid_c_ready, n * FT + (half + 1) * HALF)
                to_tokens_c(w_dn, [(k, 128) for k in range(half * HALF, (half + 1) * HALF)], FT - 1
                            ).then_inc((ffn_c_half, ffn_c_done)[half], 1)

            def body(t, scan=True, following=True, front=True):
                n = t + 1
                if following:
                    attention(n, scan, front)
                    ffn_up(n, 0, HALF, front)
                    ffn_up(n, HALF, FT, front)
                    ffn_down(n)
                if scan:
                    output_sums(t, front)
                    output_product(t)
                if following:
                    turn_a(n, 3)
                    beta_in(n)
                    delta_in(n)
                if scan:
                    turn_c(t, 1)
                    for i in range(IT):
                        gate_up(t, i)
                if following:
                    square_sums(n)
                if scan:
                    mlp_down(t, 0, following)
                    mlp_down(t, 1, following)
                if following:
                    pairs(n)
                if scan:
                    turn_c(t, 2)
                    ffn_c_up(t, 0, HALF + 2)
                    ffn_c_down(t, 0)
                    ffn_c_up(t, HALF + 2, FT)
                    ffn_c_down(t, 1)

            pe.wait_ge(early_in, 16 * (len(early) + 1))
            turn_next(0)
            queries_keys(0, 0)
            queries_keys(0, 1)
            values_in(0, 0)
            values_in(0, 1)
            pe.wait_ge(rest1, 2)
            pe.wait_ge(v_done, 1)
            pe.wait_ge(lora_in, 64)
            for k in range(KT):
                for c in range(2):
                    pe.matmul(bank[2 * k + c][:], lora_a_up[:, k * 128:(k + 1) * 128],
                              lora_b_up[:, c * 512:(c + 1) * 512], start=True, stop=True)
            for k in range(FT):
                last = pe.matmul(bank[4 + k // 2][:, (k % 2) * D:(k % 2 + 1) * D],
                                 lora_a_dn[:, k * 128:(k + 1) * 128], lora_b_dn, start=True, stop=True)
            last.then_inc(lora_prod, 1)
            pe.wait_ge(lora_added, FT // 2)
            pe.wait_ge(weights_scaled, 1)
            pe.wait_ge(consts_cast, 1)
            pe.wait_ge(stack_init, 2)

            body(-1, scan=False)
            with pe.Fori(0, NB - 2) as t:
                body(t)
            body(NB - 2, front=False)
            body(NB - 1, following=False, front=False)


def kernel(**inputs):
    import numpy as np
    import ml_dtypes
    import concourse.bacc as bacc
    from concourse.bass_utils import run_bass_kernel_spmd

    g = {k: np.asarray(v) for k, v in inputs.items()}
    t = lambda x: np.ascontiguousarray(x)
    A, Bp, Fp = "L0_attn_a_", "L0_attn_b_", "L0_ffn_"
    rows = lambda v: v.reshape(-1, 128).T
    ar = {
        "x": g[A + "x"],
        "wqkv_a": np.concatenate([g[A + "Wq"].T, g[A + "Wk"].T, g[A + "Wv"].T], axis=1),
        "wo_a": g[A + "Wo"].T,
        "wqkv_b": np.concatenate([g[Bp + "Wq"].T, g[Bp + "Wk"].T, g[Bp + "Wv"].T], axis=1),
        "wout_b": g[Bp + "Wout"].T,
        "wgu": np.concatenate([g[Bp + "Wgate"].T, g[Bp + "Wup"].T], axis=1),
        "wdown_b": g[Bp + "Wdown"].T,
        "norm_w": np.stack([rows(g[Bp + n]) for n in ("attn_norm_w", "out_norm_w", "mlp_norm_w")], axis=1),
        "conv_w": np.stack([g[Bp + n].reshape(HH, 128, TAPS).transpose(1, 0, 2)
                            for n in ("conv_q", "conv_k", "conv_v")], axis=1),
        "q_up": g[Fp + "w_up_q"].T, "s_up": g[Fp + "w_up_scale"].T, "b_up": rows(g[Fp + "b_up"]),
        "lora_a_up": g[Fp + "w_up_lora_a"].T, "lora_b_up": g[Fp + "w_up_lora_b"],
        "q_dn": g[Fp + "w_down_q"].T, "s_dn": g[Fp + "w_down_scale"].T, "b_dn": g[Fp + "b_down"][None],
        "lora_a_dn": g[Fp + "w_down_lora_a"].T, "lora_b_dn": g[Fp + "w_down_lora_b"],
    }
    wb = np.zeros((D, B, B, H, VH), np.float32)
    for b in range(B):
        wb[:, b, b] = g[Bp + "Wbeta"].T[:, :, None]
    ar["wbeta"] = wb.reshape(D, B, B * H * VH)
    p = np.arange(128)
    ar["ident"] = np.eye(128, dtype=np.float32)
    ar["ones"] = np.ones((128, 128), np.float32)
    ar["head_sum"] = (p[:, None] // DK == p[None] // DK).astype(np.float32)
    lanes = np.zeros((128, B * HH, B * HH, HPH, VH), np.float32)
    for s in range(B * HH):
        lanes[:, s, s] = (p[:, None] // DK == np.arange(HPH)[None])[:, :, None]
    ar["to_lanes"] = lanes.reshape(128, B * HH, 128)
    q32, c32 = (p % SUB)[:, None], np.arange(SUB)[None]
    ar["edge_mask"] = np.concatenate([np.where(c32 < q32, -BIG, 0), np.where(c32 > q32, -BIG, 0)], 1).astype(np.float32)
    ar["tri_mask"] = np.concatenate([np.where(p[:, None] < p[None], -BIG, 0),
                                     np.where(p[:, None] > p[None], -BIG, 0)], 1).astype(np.float32)
    cols = np.zeros((128, 2), np.float32)
    cols[PADROW, 0] = 1
    cols[MROW:MROW + 3, 1] = 1
    ar["stack_cols"] = cols
    ar["eps"] = np.tile(np.array([[LN_EPS, RMS_EPS, -L2_MIN2, L2_MIN2, 1, -1]], np.float32), (128, 1))
    pad = np.zeros((1, W + T), ml_dtypes.bfloat16)
    pad[:, :W] = -BIG
    ar["pad_row"] = pad
    ar["zero_rows"] = np.zeros((3, HPH, W), ml_dtypes.bfloat16)

    nc = bacc.Bacc("TRN2", target_bir_lowering=False, num_devices=1)
    arrays, aps = {}, {}
    for name, v in ar.items():
        v = np.ascontiguousarray(v)
        arrays[f"in_{name}"] = v
        aps[name] = nc.dram_tensor(f"in_{name}", v.shape, mybir.dt.from_np(v.dtype), kind="ExternalInput").ap()
    aps["out"] = nc.dram_tensor("out_x", (B, T, D), F32, kind="ExternalOutput").ap()
    layer_program(nc, aps)
    r = run_bass_kernel_spmd(nc, [arrays], core_ids=[0])
    return r.results[0]["out_x"]
```
